# Optimizing a Trainium2 kernel written in Bass

```python
import numpy as np
import jax
import jax.numpy as jnp

def _softmax(x, axis=-1):
    return jax.nn.softmax(x, axis=axis)

def _gelu(x):
    return jax.nn.gelu(x, approximate=True)

def _silu(x):
    return jax.nn.silu(x)

def _sigmoid(x):
    return jax.nn.sigmoid(x)

def _layernorm(x, axis=-1, eps=1e-05):
    m = jnp.mean(x, axis=axis, keepdims=True)
    v = jnp.var(x, axis=axis, keepdims=True)
    return (x - m) / jnp.sqrt(v + eps)

def _scatter_add(tgt, idx, src, axis=0):
    return tgt.at[idx].add(src)

def _segment_sum(src, seg, n):
    return jax.ops.segment_sum(src, seg, n)
kernel_name = 'mk_vit_tower_d2_tok_img768_r4_24424e'

def setup_inputs(seed: int=0):
    np.random.seed(seed)
    _w = jnp.asarray

    def _rec_inputs():
        import jax
        import jax.numpy as jnp
        _rk = jax.random.key(seed)
        x = -0.000348323 + 0.999952 * jax.random.normal(jax.random.fold_in(_rk, 1), (64, 3, 64, 64), jnp.float32)
        return x
    x = _rec_inputs()

    def _L0_tok_setup():
        import jax, jax.numpy as jnp
        import numpy as np
        PATCH = 16
        DIM = 192
        LN_EPS = 1e-05

        def _spt_forward(x, ln_gamma, ln_beta, w, b):
            B, C, H, W = x.shape
            p = PATCH
            x_right = jnp.pad(x, ((0, 0), (0, 0), (0, 0), (1, 0)))[:, :, :, :-1]
            x_left = jnp.pad(x, ((0, 0), (0, 0), (0, 0), (0, 1)))[:, :, :, 1:]
            x_down = jnp.pad(x, ((0, 0), (0, 0), (1, 0), (0, 0)))[:, :, :-1, :]
            x_up = jnp.pad(x, ((0, 0), (0, 0), (0, 1), (0, 0)))[:, :, 1:, :]
            xc = jnp.concatenate((x, x_right, x_left, x_down, x_up), axis=1)
            C5 = 5 * C
            h, wgrid = (H // p, W // p)
            tokens = xc.reshape(B, C5, h, p, wgrid, p)
            tokens = tokens.transpose(0, 2, 4, 3, 5, 1)
            tokens = tokens.reshape(B, h * wgrid, p * p * C5)
            mean = jnp.mean(tokens, axis=-1, keepdims=True)
            var = jnp.var(tokens, axis=-1, keepdims=True)
            normed = (tokens - mean) * jax.lax.rsqrt(var + LN_EPS) * ln_gamma + ln_beta
            return jnp.einsum('bnd,de->bne', normed, w) + b
        key = jax.random.key(seed)
        k1, k2 = jax.random.split(key)
        B, C, H, W = (32, 3, 96, 96)
        patch_dim = PATCH * PATCH * 5 * C
        x = jax.random.normal(k1, (B, C, H, W), dtype=jnp.float32)
        ln_gamma = jnp.ones((patch_dim,), dtype=jnp.float32)
        ln_beta = jnp.zeros((patch_dim,), dtype=jnp.float32)
        w = jax.random.normal(k2, (patch_dim, DIM), dtype=jnp.float32) * patch_dim ** (-0.5)
        b = jnp.zeros((DIM,), dtype=jnp.float32)
        return {'x': x, 'ln_gamma': ln_gamma, 'ln_beta': ln_beta, 'w': w, 'b': b}
    _L0_tok_all = _L0_tok_setup()
    _L0_tok_in = {k: v for k, v in _L0_tok_all.items() if k in ('ln_gamma', 'ln_beta', 'w', 'b')}
    del _L0_tok_all

    def _L0_attn_setup():
        import jax, jax.numpy as jnp
        import numpy as np
        B, N, C = (32, 577, 192)
        H = 12
        D = C // H
        key = jax.random.key(seed)
        ks = jax.random.split(key, 4)
        x = jax.random.normal(ks[0], (B, N, C), dtype=jnp.float32)
        w_qkv = jax.random.normal(ks[1], (C, 3 * C), dtype=jnp.float32) * C ** (-0.5)
        b_qkv = jnp.zeros((3 * C,), dtype=jnp.float32)
        scale = jnp.ones((H,), dtype=jnp.float32) * D ** (-0.5)
        w_proj = jax.random.normal(ks[2], (C, C), dtype=jnp.float32) * C ** (-0.5)
        b_proj = jnp.zeros((C,), dtype=jnp.float32)
        return {'x': x, 'w_qkv': w_qkv, 'b_qkv': b_qkv, 'scale': scale, 'w_proj': w_proj, 'b_proj': b_proj}
    _L0_attn_all = _L0_attn_setup()
    _L0_attn_in = {k: v for k, v in _L0_attn_all.items() if k in ('w_qkv', 'b_qkv', 'scale', 'w_proj', 'b_proj')}
    del _L0_attn_all

    def _L0_ffn_setup():
        import jax, jax.numpy as jnp
        import numpy as np
        H = 12
        ALPHA = (1, 2, 3)
        DEPTH = 5
        BLOCK_DEPTH = 3
        TOTAL_DEPTH_M1 = 14 - 1
        SMALL_ACTIVE = BLOCK_DEPTH <= DEPTH <= TOTAL_DEPTH_M1 - BLOCK_DEPTH

        def _ln(x, g, b, eps=1e-05):
            m = jnp.mean(x, axis=-1, keepdims=True)
            v = jnp.mean((x - m) ** 2, axis=-1, keepdims=True)
            return (x - m) * jax.lax.rsqrt(v + eps) * g + b

        def _attn_branch(xp, w_qkv, w_proj, b_proj, keep_heads, keep_ch):
            B2, N, C = xp.shape
            hd = C // H
            scale = hd ** (-0.5)
            qkv = (xp @ w_qkv).reshape(B2, N, 3, H, hd).transpose(2, 0, 3, 1, 4)
            hmask = (jnp.arange(H) < keep_heads).astype(xp.dtype)[None, :, None, None]
            q, k, v = (qkv[0] * hmask, qkv[1] * hmask, qkv[2] * hmask)
            a = jax.nn.softmax(jnp.einsum('bhnd,bhmd->bhnm', q, k) * scale, axis=-1)
            o = jnp.einsum('bhnm,bhmd->bhnd', a, v).transpose(0, 2, 1, 3).reshape(B2, N, C)
            o = o @ w_proj + b_proj
            cmask = (jnp.arange(C) < keep_ch).astype(xp.dtype)
            return o * cmask

        def _mlp_branch(xp, w1, b1, w2, b2, keep_ch):
            C = xp.shape[-1]
            cmask = (jnp.arange(C) < keep_ch).astype(xp.dtype)
            h = jax.nn.gelu(xp * cmask @ w1 + b1, approximate=False)
            return (h @ w2 + b2) * cmask
        key = jax.random.key(seed)
        ks = jax.random.split(key, 8)
        B, N, C = (64, 257, 192)
        HID = 4 * C

        def w(k, shape):
            return jax.random.normal(k, shape, jnp.float32) * 0.02
        return {'x': jax.random.normal(ks[0], (B, N, C), jnp.float32), 'gumbel_weights': jax.random.uniform(ks[1], (3,), jnp.float32), 'n1l_g': jnp.ones((C,), jnp.float32), 'n1l_b': jnp.zeros((C,), jnp.float32), 'n1s_g': jnp.ones((C,), jnp.float32), 'n1s_b': jnp.zeros((C,), jnp.float32), 'w_qkv': w(ks[2], (C, 3 * C)), 'w_proj': w(ks[3], (C, C)), 'b_proj': jnp.zeros((C,), jnp.float32), 'n2l_g': jnp.ones((C,), jnp.float32), 'n2l_b': jnp.zeros((C,), jnp.float32), 'n2s_g': jnp.ones((C,), jnp.float32), 'n2s_b': jnp.zeros((C,), jnp.float32), 'w_fc1': w(ks[4], (C, HID)), 'b_fc1': jnp.zeros((HID,), jnp.float32), 'w_fc2': w(ks[5], (HID, C)), 'b_fc2': jnp.zeros((C,), jnp.float32)}
    _L0_ffn_all = _L0_ffn_setup()
    _L0_ffn_in = {k: v for k, v in _L0_ffn_all.items() if k in ('gumbel_weights', 'n1l_g', 'n1l_b', 'n1s_g', 'n1s_b', 'w_qkv', 'w_proj', 'b_proj', 'n2l_g', 'n2l_b', 'n2s_g', 'n2s_b', 'w_fc1', 'b_fc1', 'w_fc2', 'b_fc2')}
    del _L0_ffn_all

    def _L1_attn_setup():
        import jax, jax.numpy as jnp
        import numpy as np
        import math
        N_HEAD = 12
        N_EMBD = 192
        HEAD_DIM = N_EMBD // N_HEAD // 2
        DEPTH = 12
        LAMBDA_INIT = 0.8 - 0.6 * math.exp(-0.3 * DEPTH)

        def _sdpa_over_heads(q, k, v):
            scale = 1.0 / math.sqrt(q.shape[-1])
            s = jnp.einsum('bnqd,bnkd->bnqk', q, k) * scale
            a = jax.nn.softmax(s, axis=-1)
            return jnp.einsum('bnqk,bnkd->bnqd', a, v)
        key = jax.random.key(seed)
        ks = jax.random.split(key, 7)
        B, N, D = (4, 2048, N_EMBD)
        s = 0.02
        return {'x': jax.random.normal(ks[0], (B, N, D), dtype=jnp.float32), 'W_attn': jax.random.normal(ks[1], (3 * D, D), dtype=jnp.float32) * s, 'W_out': jax.random.normal(ks[2], (D, D), dtype=jnp.float32) * s, 'lambda_q1': jax.random.normal(ks[3], (HEAD_DIM,), dtype=jnp.float32) * 0.1, 'lambda_k1': jax.random.normal(ks[4], (HEAD_DIM,), dtype=jnp.float32) * 0.1, 'lambda_q2': jax.random.normal(ks[5], (HEAD_DIM,), dtype=jnp.float32) * 0.1, 'lambda_k2': jax.random.normal(ks[6], (HEAD_DIM,), dtype=jnp.float32) * 0.1}
    _L1_attn_all = _L1_attn_setup()
    _L1_attn_in = {k: v for k, v in _L1_attn_all.items() if k in ('W_attn', 'W_out', 'lambda_q1', 'lambda_k1', 'lambda_q2', 'lambda_k2')}
    del _L1_attn_all

    def _L1_ffn_setup():
        import jax, jax.numpy as jnp
        import numpy as np
        D = 192
        M = 768
        G = 4
        E = 8
        KG = 2
        KE = 4
        EPS = 1e-06

        def _topk_gates(logits, k):
            top, idx = jax.lax.top_k(logits, k)
            gates = jax.nn.softmax(top, axis=-1)
            gates = jnp.where(gates >= EPS, gates, jnp.zeros_like(gates))
            return (gates, idx)
        key = jax.random.key(seed)
        ks = jax.random.split(key, 9)
        x = jax.random.normal(ks[0], (1, 256, D), dtype=jnp.float32)
        Wg = jax.random.normal(ks[1], (D, G), dtype=jnp.float32) * 0.02
        bg = jax.random.normal(ks[2], (G,), dtype=jnp.float32) * 0.01
        We = jax.random.normal(ks[3], (G, D, E), dtype=jnp.float32) * 0.02
        be = jax.random.normal(ks[4], (G, E), dtype=jnp.float32) * 0.01
        W1 = jax.random.normal(ks[5], (G, E, D, M), dtype=jnp.float32) * 0.02
        b1 = jax.random.normal(ks[6], (G, E, M), dtype=jnp.float32) * 0.01
        W2 = jax.random.normal(ks[7], (G, E, M, D), dtype=jnp.float32) * 0.02
        b2 = jax.random.normal(ks[8], (G, E, D), dtype=jnp.float32) * 0.01
        return {'x': x, 'Wg': Wg, 'bg': bg, 'We': We, 'be': be, 'W1': W1, 'b1': b1, 'W2': W2, 'b2': b2}
    _L1_ffn_all = _L1_ffn_setup()
    _L1_ffn_in = {k: v for k, v in _L1_ffn_all.items() if k in ('Wg', 'bg', 'We', 'be', 'W1', 'b1', 'W2', 'b2')}
    del _L1_ffn_all
    return {'x': x, 'L0_tok_ln_gamma': _L0_tok_in['ln_gamma'], 'L0_tok_ln_beta': _L0_tok_in['ln_beta'], 'L0_tok_w': _L0_tok_in['w'], 'L0_tok_b': _L0_tok_in['b'], 'L0_attn_w_qkv': _L0_attn_in['w_qkv'], 'L0_attn_b_qkv': _L0_attn_in['b_qkv'], 'L0_attn_scale': _L0_attn_in['scale'], 'L0_attn_w_proj': _L0_attn_in['w_proj'], 'L0_attn_b_proj': _L0_attn_in['b_proj'], 'L0_ffn_gumbel_weights': _L0_ffn_in['gumbel_weights'], 'L0_ffn_n1l_g': _L0_ffn_in['n1l_g'], 'L0_ffn_n1l_b': _L0_ffn_in['n1l_b'], 'L0_ffn_n1s_g': _L0_ffn_in['n1s_g'], 'L0_ffn_n1s_b': _L0_ffn_in['n1s_b'], 'L0_ffn_w_qkv': _L0_ffn_in['w_qkv'], 'L0_ffn_w_proj': _L0_ffn_in['w_proj'], 'L0_ffn_b_proj': _L0_ffn_in['b_proj'], 'L0_ffn_n2l_g': _L0_ffn_in['n2l_g'], 'L0_ffn_n2l_b': _L0_ffn_in['n2l_b'], 'L0_ffn_n2s_g': _L0_ffn_in['n2s_g'], 'L0_ffn_n2s_b': _L0_ffn_in['n2s_b'], 'L0_ffn_w_fc1': _L0_ffn_in['w_fc1'], 'L0_ffn_b_fc1': _L0_ffn_in['b_fc1'], 'L0_ffn_w_fc2': _L0_ffn_in['w_fc2'], 'L0_ffn_b_fc2': _L0_ffn_in['b_fc2'], 'L1_attn_W_attn': _L1_attn_in['W_attn'], 'L1_attn_W_out': _L1_attn_in['W_out'], 'L1_attn_lambda_q1': _L1_attn_in['lambda_q1'], 'L1_attn_lambda_k1': _L1_attn_in['lambda_k1'], 'L1_attn_lambda_q2': _L1_attn_in['lambda_q2'], 'L1_attn_lambda_k2': _L1_attn_in['lambda_k2'], 'L1_ffn_Wg': _L1_ffn_in['Wg'], 'L1_ffn_bg': _L1_ffn_in['bg'], 'L1_ffn_We': _L1_ffn_in['We'], 'L1_ffn_be': _L1_ffn_in['be'], 'L1_ffn_W1': _L1_ffn_in['W1'], 'L1_ffn_b1': _L1_ffn_in['b1'], 'L1_ffn_W2': _L1_ffn_in['W2'], 'L1_ffn_b2': _L1_ffn_in['b2']}

def reference(x, L0_tok_ln_gamma, L0_tok_ln_beta, L0_tok_w, L0_tok_b, L0_attn_w_qkv, L0_attn_b_qkv, L0_attn_scale, L0_attn_w_proj, L0_attn_b_proj, L0_ffn_gumbel_weights, L0_ffn_n1l_g, L0_ffn_n1l_b, L0_ffn_n1s_g, L0_ffn_n1s_b, L0_ffn_w_qkv, L0_ffn_w_proj, L0_ffn_b_proj, L0_ffn_n2l_g, L0_ffn_n2l_b, L0_ffn_n2s_g, L0_ffn_n2s_b, L0_ffn_w_fc1, L0_ffn_b_fc1, L0_ffn_w_fc2, L0_ffn_b_fc2, L1_attn_W_attn, L1_attn_W_out, L1_attn_lambda_q1, L1_attn_lambda_k1, L1_attn_lambda_q2, L1_attn_lambda_k2, L1_ffn_Wg, L1_ffn_bg, L1_ffn_We, L1_ffn_be, L1_ffn_W1, L1_ffn_b1, L1_ffn_W2, L1_ffn_b2):
    import jax
    import jax.numpy as jnp

    def _L0_tok_ref(x, ln_gamma, ln_beta, w, b):
        import jax, jax.numpy as jnp
        import numpy as np
        PATCH = 16
        DIM = 192
        LN_EPS = 1e-05

        def _spt_forward(x, ln_gamma, ln_beta, w, b):
            B, C, H, W = x.shape
            p = PATCH
            x_right = jnp.pad(x, ((0, 0), (0, 0), (0, 0), (1, 0)))[:, :, :, :-1]
            x_left = jnp.pad(x, ((0, 0), (0, 0), (0, 0), (0, 1)))[:, :, :, 1:]
            x_down = jnp.pad(x, ((0, 0), (0, 0), (1, 0), (0, 0)))[:, :, :-1, :]
            x_up = jnp.pad(x, ((0, 0), (0, 0), (0, 1), (0, 0)))[:, :, 1:, :]
            xc = jnp.concatenate((x, x_right, x_left, x_down, x_up), axis=1)
            C5 = 5 * C
            h, wgrid = (H // p, W // p)
            tokens = xc.reshape(B, C5, h, p, wgrid, p)
            tokens = tokens.transpose(0, 2, 4, 3, 5, 1)
            tokens = tokens.reshape(B, h * wgrid, p * p * C5)
            mean = jnp.mean(tokens, axis=-1, keepdims=True)
            var = jnp.var(tokens, axis=-1, keepdims=True)
            normed = (tokens - mean) * jax.lax.rsqrt(var + LN_EPS) * ln_gamma + ln_beta
            return jnp.einsum('bnd,de->bne', normed, w) + b
        return _spt_forward(x, ln_gamma, ln_beta, w, b)

    def _L0_attn_ref(x, w_qkv, b_qkv, scale, w_proj, b_proj):
        import jax, jax.numpy as jnp
        import numpy as np
        B, N, C = (32, 577, 192)
        H = 12
        D = C // H
        b, n, c = x.shape
        h = scale.shape[0]
        d = c // h
        qkv = (x @ w_qkv + b_qkv).reshape(b, n, 3, h, d)
        q = qkv[:, :, 0]
        k = qkv[:, :, 1]
        v = qkv[:, :, 2]
        attn = jnp.einsum('bihd,bjhd->bhij', q, k) * scale[None, :, None, None]
        if n > 1:
            mask = jnp.zeros((n, n), dtype=bool).at[1:, 1:].set(jnp.eye(n - 1, dtype=bool))
            attn = jnp.where(mask[None, None], -jnp.inf, attn)
        attn = jax.nn.softmax(attn, axis=-1)
        out = jnp.einsum('bhij,bjhd->bihd', attn, v).reshape(b, n, c)
        return out @ w_proj + b_proj

    def _L0_ffn_ref(x, gumbel_weights, n1l_g, n1l_b, n1s_g, n1s_b, w_qkv, w_proj, b_proj, n2l_g, n2l_b, n2s_g, n2s_b, w_fc1, b_fc1, w_fc2, b_fc2):
        import jax, jax.numpy as jnp
        import numpy as np
        H = 12
        ALPHA = (1, 2, 3)
        DEPTH = 5
        BLOCK_DEPTH = 3
        TOTAL_DEPTH_M1 = 14 - 1
        SMALL_ACTIVE = BLOCK_DEPTH <= DEPTH <= TOTAL_DEPTH_M1 - BLOCK_DEPTH

        def _ln(x, g, b, eps=1e-05):
            m = jnp.mean(x, axis=-1, keepdims=True)
            v = jnp.mean((x - m) ** 2, axis=-1, keepdims=True)
            return (x - m) * jax.lax.rsqrt(v + eps) * g + b

        def _attn_branch(xp, w_qkv, w_proj, b_proj, keep_heads, keep_ch):
            B2, N, C = xp.shape
            hd = C // H
            scale = hd ** (-0.5)
            qkv = (xp @ w_qkv).reshape(B2, N, 3, H, hd).transpose(2, 0, 3, 1, 4)
            hmask = (jnp.arange(H) < keep_heads).astype(xp.dtype)[None, :, None, None]
            q, k, v = (qkv[0] * hmask, qkv[1] * hmask, qkv[2] * hmask)
            a = jax.nn.softmax(jnp.einsum('bhnd,bhmd->bhnm', q, k) * scale, axis=-1)
            o = jnp.einsum('bhnm,bhmd->bhnd', a, v).transpose(0, 2, 1, 3).reshape(B2, N, C)
            o = o @ w_proj + b_proj
            cmask = (jnp.arange(C) < keep_ch).astype(xp.dtype)
            return o * cmask

        def _mlp_branch(xp, w1, b1, w2, b2, keep_ch):
            C = xp.shape[-1]
            cmask = (jnp.arange(C) < keep_ch).astype(xp.dtype)
            h = jax.nn.gelu(xp * cmask @ w1 + b1, approximate=False)
            return (h @ w2 + b2) * cmask
        B, N, C = x.shape
        B2 = B // 2
        nl = _ln(x[:B2], n1l_g, n1l_b)
        ns = _ln(x[B2:], n1s_g, n1s_b)
        a_large = _attn_branch(nl, w_qkv, w_proj, b_proj, H, C)
        if SMALL_ACTIVE:
            a_small = sum((gumbel_weights[i] * _attn_branch(ns, w_qkv, w_proj, b_proj, H // ALPHA[i], C // ALPHA[i]) for i in range(3)))
            attn_out = jnp.concatenate([a_large, a_small], axis=0)
        else:
            attn_out = jnp.concatenate([a_large, a_large], axis=0)
        x = x + attn_out
        nl2 = _ln(x[:B2], n2l_g, n2l_b)
        ns2 = _ln(x[B2:], n2s_g, n2s_b)
        m_large = _mlp_branch(nl2, w_fc1, b_fc1, w_fc2, b_fc2, C)
        if SMALL_ACTIVE:
            m_small = sum((gumbel_weights[i] * _mlp_branch(ns2, w_fc1, b_fc1, w_fc2, b_fc2, C // ALPHA[i]) for i in range(3)))
            mlp_out = jnp.concatenate([m_large, m_small], axis=0)
        else:
            mlp_out = jnp.concatenate([m_large, m_large], axis=0)
        return x + mlp_out

    def _L1_attn_ref(x, W_attn, W_out, lambda_q1, lambda_k1, lambda_q2, lambda_k2):
        import jax, jax.numpy as jnp
        import numpy as np
        import math
        N_HEAD = 12
        N_EMBD = 192
        HEAD_DIM = N_EMBD // N_HEAD // 2
        DEPTH = 12
        LAMBDA_INIT = 0.8 - 0.6 * math.exp(-0.3 * DEPTH)

        def _sdpa_over_heads(q, k, v):
            scale = 1.0 / math.sqrt(q.shape[-1])
            s = jnp.einsum('bnqd,bnkd->bnqk', q, k) * scale
            a = jax.nn.softmax(s, axis=-1)
            return jnp.einsum('bnqk,bnkd->bnqd', a, v)
        B, N, D = x.shape
        H, hd = (N_HEAD, HEAD_DIM)
        qkv = x @ W_attn.T
        q, k, v = jnp.split(qkv, 3, axis=-1)
        q = q.reshape(B, N, H, 2, hd)
        k = k.reshape(B, N, H, 2, hd)
        v = v.reshape(B, N, H, 2 * hd)
        q1, q2 = (q[:, :, :, 0], q[:, :, :, 1])
        k1, k2 = (k[:, :, :, 0], k[:, :, :, 1])
        o1 = _sdpa_over_heads(q1, k1, v)
        o2 = _sdpa_over_heads(q2, k2, v)
        lam1 = jnp.exp(jnp.sum(lambda_q1 * lambda_k1))
        lam2 = jnp.exp(jnp.sum(lambda_q2 * lambda_k2))
        lam_full = lam1 - lam2 + LAMBDA_INIT
        y = (o1 - lam_full * o2) * (1.0 - LAMBDA_INIT)
        y = y.reshape(B, N, H * 2 * hd)
        return y @ W_out.T

    def _L1_ffn_ref(x, Wg, bg, We, be, W1, b1, W2, b2):
        import jax, jax.numpy as jnp
        import numpy as np
        D = 192
        M = 768
        G = 4
        E = 8
        KG = 2
        KE = 4
        EPS = 1e-06

        def _topk_gates(logits, k):
            top, idx = jax.lax.top_k(logits, k)
            gates = jax.nn.softmax(top, axis=-1)
            gates = jnp.where(gates >= EPS, gates, jnp.zeros_like(gates))
            return (gates, idx)
        orig_shape = x.shape
        xf = x.reshape(-1, D)
        glog = xf @ Wg + bg
        ggates, gidx = _topk_gates(glog, KG)
        gw = jnp.einsum('nk,nkg->ng', ggates, jax.nn.one_hot(gidx, G, dtype=xf.dtype))
        elog = jnp.einsum('nd,gde->nge', xf, We) + be
        egates, eidx = _topk_gates(elog, KE)
        ew = jnp.einsum('ngk,ngke->nge', egates, jax.nn.one_hot(eidx, E, dtype=xf.dtype))
        combine = gw[:, :, None] * ew
        y = jnp.zeros_like(xf)
        for g in range(G):
            h = jax.nn.gelu(jnp.einsum('nd,edm->enm', xf, W1[g]) + b1[g][:, None, :], approximate=False)
            o = jnp.einsum('enm,emd->end', h, W2[g]) + b2[g][:, None, :]
            y = y + jnp.einsum('end,ne->nd', o, combine[:, g, :])
        return y.reshape(orig_shape)
    h = _L0_tok_ref(x, L0_tok_ln_gamma, L0_tok_ln_beta, L0_tok_w, L0_tok_b)
    h = h + _L0_attn_ref(_layernorm(h, axis=-1), L0_attn_w_qkv, L0_attn_b_qkv, L0_attn_scale, L0_attn_w_proj, L0_attn_b_proj)
    h = h + _L0_ffn_ref(_layernorm(h, axis=-1), L0_ffn_gumbel_weights, L0_ffn_n1l_g, L0_ffn_n1l_b, L0_ffn_n1s_g, L0_ffn_n1s_b, L0_ffn_w_qkv, L0_ffn_w_proj, L0_ffn_b_proj, L0_ffn_n2l_g, L0_ffn_n2l_b, L0_ffn_n2s_g, L0_ffn_n2s_b, L0_ffn_w_fc1, L0_ffn_b_fc1, L0_ffn_w_fc2, L0_ffn_b_fc2)
    h = h + _L1_attn_ref(_layernorm(h, axis=-1), L1_attn_W_attn, L1_attn_W_out, L1_attn_lambda_q1, L1_attn_lambda_k1, L1_attn_lambda_q2, L1_attn_lambda_k2)
    h = h + _L1_ffn_ref(_layernorm(h, axis=-1), L1_ffn_Wg, L1_ffn_bg, L1_ffn_We, L1_ffn_be, L1_ffn_W1, L1_ffn_b1, L1_ffn_W2, L1_ffn_b2)
    return h

_drawn_inputs = setup_inputs


def setup_inputs(seed=0):
    import zlib

    import numpy as np

    out = dict(_drawn_inputs(seed))
    spreads = {'L0_tok_ln_gamma': (1.0, 0.2),
     'L0_tok_ln_beta': (0.0, 0.1),
     'L0_tok_b': (0.0, 0.1),
     'L0_attn_b_qkv': (0.0, 0.1),
     'L0_attn_scale': (0.25, 0.2),
     'L0_attn_b_proj': (0.0, 0.1),
     'L0_ffn_n1l_g': (1.0, 0.6),
     'L0_ffn_n1l_b': (0.0, 0.8),
     'L0_ffn_n1s_g': (1.0, 0.6),
     'L0_ffn_n1s_b': (0.0, 0.8),
     'L0_ffn_b_proj': (0.0, 0.1),
     'L0_ffn_n2l_g': (1.0, 0.6),
     'L0_ffn_n2l_b': (0.0, 0.8),
     'L0_ffn_n2s_g': (1.0, 0.6),
     'L0_ffn_n2s_b': (0.0, 0.8),
     'L0_ffn_b_fc1': (0.0, 0.798),
     'L0_ffn_b_fc2': (0.0, 0.1)}
    factors = {'L0_ffn_gumbel_weights': 6.487,
     'L0_ffn_w_qkv': 5.368,
     'L0_ffn_w_proj': 5.421,
     'L1_attn_W_attn': 8.0,
     'L1_attn_W_out': 8.0,
     'L1_attn_lambda_q1': 8.0,
     'L1_attn_lambda_k1': 8.0,
     'L1_attn_lambda_q2': 8.0,
     'L1_attn_lambda_k2': 8.0,
     'L1_ffn_Wg': 5.618,
     'L1_ffn_bg': 23.265,
     'L1_ffn_We': 5.71,
     'L1_ffn_be': 47.525,
     'L1_ffn_W1': 4.17,
     'L1_ffn_b1': 49.923,
     'L1_ffn_W2': 4.079,
     'L1_ffn_b2': 64.0}
    for name, (base, spread) in spreads.items():
        noise = np.random.default_rng([zlib.crc32(name.encode()), seed]).standard_normal(out[name].shape)
        drawn = base * np.exp(spread * noise) if base else spread * noise
        out[name] = jnp.asarray(drawn.astype(out[name].dtype))
    for name, factor in factors.items():
        out[name] = (out[name] * factor).astype(out[name].dtype)
    return out
```

```python
from contextlib import ExitStack

import numpy as np

import concourse.bass as bass
from concourse import mybir
from concourse.alu_op_type import AluOpType as ALU

ACT = mybir.ActivationFunctionType
F32 = mybir.dt.float32
AX_X = mybir.AxisListType.X

P = 128
B, NCH, IMG, PATCH = 64, 3, 64, 16
SIDE = IMG // PATCH
NTOK = SIDE * SIDE
TOK = B * NTOK
T = TOK // P
TB = P // NTOK
D = 192
HC = D // 2
H, HH, HD = 12, 6, 16
HALF = TOK // 2
IB = B // 2
HID = 768
MC = HID // P
NSH = 5
NF = NCH * ((PATCH + 2) ** 2 - 4)
FC, FP = 8, NF // 8
NPATCH = PATCH * PATCH * NSH * NCH
KEEP = (D, D // 2, D // 3)
G, E, KG, KE = 4, 8, 2, 4
NE = G * E
EPS_LN, EPS_GATE = 1e-5, 1e-6
LAMBDA_INIT = 0.8 - 0.6 * float(np.exp(-0.3 * 12))
NEG = -1.0e30


def pixel_layout():
    order = [(c, i, j) for c in range(NCH) for i in range(-1, PATCH + 1) for j in range(-1, PATCH + 1)
             if not (i in (-1, PATCH) and j in (-1, PATCH))]
    moves = [(0, 0), (0, -1), (0, 1), (-1, 0), (1, 0)]
    rows = np.full((NSH, NF), -1, np.int64)
    for f, (c, i, j) in enumerate(order):
        for v, (di, dj) in enumerate(moves):
            pi, pj = i - di, j - dj
            if 0 <= pi < PATCH and 0 <= pj < PATCH:
                rows[v, f] = (pi * PATCH + pj) * NSH * NCH + v * NCH + c
    return order, rows


def repeat(ap, axis, n):
    ap = ap.unsqueeze(axis)
    shape = list(ap.shape)
    shape[axis] = n
    return ap.broadcast_to(shape)


def vit_tower(nc, a, out):
    ctx = ExitStack()
    with ctx:
        def sb(name, shape):
            return ctx.enter_context(nc.sbuf_tensor(name, shape, F32))

        sems = {}

        def sem(name):
            if name not in sems:
                sems[name] = ctx.enter_context(nc.semaphore(name))
            return sems[name]

        ident = sb("ident", [P, P])
        ones = sb("ones", [P, P])
        blockmask = sb("blockmask", [P, TB])
        headmask = sb("headmask", [HC, HH])
        selfmask = sb("selfmask", [HC, NTOK])
        tri = sb("tri", [P, E * E])
        cnt = sb("cnt", [FP, FC])
        gamma5 = sb("gamma5", [FP, NSH, FC])
        beta5 = sb("beta5", [FP, NSH, FC])
        minus_half = sb("minus_half", [P, T])
        rows_sb = sb("rows_sb", [1, 2048])
        cols_sb = sb("cols_sb", [HC, 24])
        b1_sb = sb("b1_sb", [P, MC])
        gum = sb("gum", [P, 5])
        lamv = sb("lamv", [P, 4, 8])
        lam = sb("lam", [P, 8])
        headfac = sb("headfac", [P, 2, H])
        weights = {L: sb(f"wqkv{L}", [HC, 2, 3 * D]) for L in "ABD"}
        wout = {L: sb(f"wout{L}", [HC, 2, D]) for L in "ABDS"}
        w1 = sb("w1", [HC, 2, HID])
        w2 = sb("w2", [P, MC, D])
        w2s = [sb(f"w2s{i}", [P, MC, KEEP[i]]) for i in range(3)]
        wr = sb("wr", [HC, 2, G + NE])
        b2all = sb("b2all", [NE, D])

        h = sb("h", [P, T, D])
        z = sb("z", [P, T, D])
        xn = sb("xn", [P, T, D])
        V = sb("V", [P, T, D])
        xT = sb("xT", [HC, 2, TOK])
        osb = sb("osb", [P, 2, D])
        oT = sb("oT", [HC, 2, 2, P])
        stats = sb("stats", [P, T, 6])
        mv = sb("mv", [P, T, 2])
        rstd = sb("rstd", [P, T])
        tokst = sb("tokst", [P, T, 4])
        tmpt = sb("tmpt", [P, 2, D])
        colsum = sb("colsum", [P, D])
        cbias = sb("cbias", [P, D])
        smx = sb("smx", [HC, 2, IB])
        ssum = sb("ssum", [HC, 2, IB])
        srec = sb("srec", [HC, 2, IB])

        arena = sb("arena", [P, 24320])
        at = [0]

        def view(parts, n):
            v = arena[0:parts, at[0]:at[0] + n]
            at[0] += n
            return v

        xf = view(FP, FC * TOK).rearrange("p (c t) -> p c t", c=FC)
        xsq = view(FP, FC * TOK).rearrange("p (c t) -> p c t", c=FC)
        w5 = view(FP, NSH * FC * D).rearrange("p (c v n) -> p c v n", c=FC, v=NSH)
        weff = V[0:FP, :, :]
        at[0] = 0
        qbd = [view(HC, IB * HC).rearrange("p (b h i) -> p b h i", b=IB, h=HH) for _ in range(4)]
        prob = view(HC, 2 * B * NTOK).rearrange("p (f n x) -> p f n x", f=2, n=2)
        ptbd = [view(P, H * P).rearrange("p (h b i) -> p h b i", h=H, b=TB) for _ in range(2)]
        qk = view(HC, 4 * TOK).rearrange("p (o n x) -> p o n x", o=4, n=2)
        at[0] = 0
        qkD = view(P, T * 2 * D).rearrange("p (t n) -> p t n", t=T)
        prodS = [view(P, H * H * HD) for _ in range(2)]
        prodV = [view(P, H * H * HD) for _ in range(2)]
        scD = [view(P, 2 * H * H) for _ in range(3)]
        mxD = [view(P, 2 * H) for _ in range(3)]
        peff = [view(P, H * H) for _ in range(2)]
        oD = [view(P, D) for _ in range(2)]
        at[0] = 0
        hT = [view(P, MC * HALF).rearrange("p (m t) -> p m t", m=MC) for _ in range(4)]
        at[0] = 0
        mo_w1 = [view(HC, 2 * HID).rearrange("p (k m) -> p k m", k=2) for _ in range(2)]
        mo_w2 = [view(P, MC * D).rearrange("p (m d) -> p m d", m=MC) for _ in range(2)]
        mo_b1 = [view(P, MC) for _ in range(2)]
        mo_hT = view(P, MC * HALF).rearrange("p (m t) -> p m t", m=MC)
        lgG = view(P, T * G).rearrange("p (r e) -> p r e", e=G)
        lgE = view(P, T * NE).rearrange("p (r e) -> p r e", e=E)
        comb = view(P, T * NE).rearrange("p (t e) -> p t e", t=T)
        cmpa = view(P, 4 * T * NE * 2)
        cmpb = view(P, 4 * T * NE * 2)
        gwork = view(P, 6 * T * NE)
        cT = view(NE, T * P).rearrange("p (t x) -> p t x", t=T)
        y = view(P, T * D).rearrange("p (t d) -> p t d", t=T)

        gparts = {}
        gat = 0
        for which, r_, n_ in (("G", T, G), ("E", T * G, E)):
            for part, size in (("sel", r_ * n_), ("d", r_ * n_), ("mx", r_)):
                v = gwork[:, gat:gat + size]
                gparts[which, part] = v.rearrange("p (r e) -> p r e", e=n_) if part != "mx" else v
                gat += size

        def gview(which, part):
            return gparts[which, part]

        bank = [ctx.enter_context(nc.psum_tensor(f"bank{i}", [P, 512], F32)) for i in range(8)]
        full = [sem(f"bank{i}_full") for i in range(8)]
        free = [sem(f"bank{i}_free") for i in range(8)]

        uses, used = {}, [0] * 8

        def use(b, *key):
            uses[key] = (b, used[b])
            used[b] += 1

        def claim(*key):
            b, k = uses[key]
            if k:
                nc.tensor.wait_ge(free[b], k)
            return bank[b]

        def filled(eng, *key):
            b, k = uses[key]
            eng.wait_ge(full[b], k + 1)
            return bank[b]

        def was_read(eng, *key):
            b, k = uses[key]
            eng.wait_ge(free[b], k + 1)

        def full_of(*key):
            return full[uses[key][0]]

        def free_of(*key):
            return free[uses[key][0]]

        def plan_transposes(L):
            for n in range(2):
                for k in range(2):
                    use(2 + k, L, "xT", n, k)

        def plan_attention(L):
            for n in range(2):
                for o in range(4):
                    use(4 + o % 2, L, "qk", n, o)
            for t in range(T):
                use(t % 2, L, "V", t)
            for n in range(2):
                for f in range(2):
                    use(6 + f, L, "score", n, f)
            for t in range(T + 3):
                if t < T:
                    use(2 + t % 2, L, "PT", t)
                if 0 <= t - 1 < T:
                    use((t - 1) % 2, L, "AV", t - 1)
                if 0 <= t - 2 < T:
                    use(4 + t % 2, L, "oT", t - 2)
                if 0 <= t - 3 < T:
                    use(6 + (t - 3) % 2, L, "proj", t - 3)

        for t in range(T // 2):
            use(t, "tok", t)
        use(5, "cbias")
        use(4, "colsum")
        for t in range(T // 2, T):
            use(t % 4, "tok", t)
        for L in "AB":
            plan_transposes(L)
            plan_attention(L)
        plan_transposes("M")
        for m in range(MC):
            use(2 + m, "fc1", 3, m)
        for i in (2, 1, 0):
            for m in range(MC):
                use(2 + m, "fc1", i, m)
        for t in range(T):
            use(t % 2, "fc2", t)
        plan_transposes("D")
        for t in range(T):
            use(4 + t % 2, "D", "qk", t)
            use(t % 2, "D", "V", t)
        for t in range(T + 1):
            if t < T:
                use(2 + t % 2, "D", "oT", t)
            if t >= 1:
                use(6 + t % 2, "D", "proj", t - 1)
        plan_transposes("R")
        for t in range(T):
            use(4 + t % 2, "logit", t)
        for t in range(T):
            use(6, "cT", t)
            use(7, "y0", t)
        moe_base = list(used)

        lots = {}

        def load(eng, lot, dst, src):
            lots[lot] = lots.get(lot, 0) + 16
            eng.dma_start(dst, src).then_inc(sem(f"in_{lot}"), 16)

        LOT = {"const": 16 * 8, "A": 16 * 2, "B": 16 * 2, "D": 16 * 2, "mlp": 16 * 2, "small": 16 * 7,
               "route": 16 * 2}

        def loaded(eng, lot):
            eng.wait_ge(sem(f"in_{lot}"), LOT[lot])

        halves = "(k p) n -> p k n"
        block = ctx.enter_context(nc.Block())

        @block.sync
        def _(sp):
            load(sp, "const", gamma5[:], a["gamma5"])
            for c in range(FC):
                sp.dma_start(w5[:, c], a["w5"][c]).then_inc(sem(f"in_pixels{c}"), 16)
                sp.dma_start(xf[:, c], a["xf"][c]).then_inc(sem(f"in_pixels{c}"), 16)
                if c == 0:
                    load(sp, "const", beta5[:], a["beta5"])
                    load(sp, "const", cnt[:], a["cnt"])
                    load(sp, "const", ident[:], a["ident"])
                    load(sp, "const", blockmask[:], a["blockmask"])
                    load(sp, "const", headmask[:], a["headmask"])
                    load(sp, "const", selfmask[:], a["selfmask"])
                    load(sp, "const", tri[:], a["tri"])
                    load(sp, "small", rows_sb[:], a["rows"])
                    load(sp, "small", cols_sb[:], a["cols"])
            load(sp, "A", weights["A"][:], a["wqkvA"].rearrange(halves, p=HC))
            load(sp, "A", wout["A"][:], a["woutA"].rearrange(halves, p=HC))
            load(sp, "small", gum[:, 0:3], a["gum"].broadcast_to([P, 3]))
            load(sp, "small", lamv[:], a["lamv"].broadcast_to([P, 4, 8]))
            load(sp, "small", b1_sb[:], a["b1"])
            load(sp, "small", b2all[:], a["moe_b2"])
            load(sp, "small", wr[:], a["wr"].rearrange(halves, p=HC))
            for L in "BD":
                load(sp, L, weights[L][:], a[f"wqkv{L}"].rearrange(halves, p=HC))
                load(sp, L, wout[L][:], a[f"wout{L}"].rearrange(halves, p=HC))
            load(sp, "mlp", w1[:], a["w1"].rearrange(halves, p=HC))
            load(sp, "mlp", w2[:], a["w2"].rearrange("(m p) n -> p m n", p=P))
            was_read(sp, "D", "proj", T - 1)
            with sp.Fori(0, NE // 2) as pair:
                e = pair * 2
                for u in range(2):
                    sp.wait_ge(full[1], e * 4 + (moe_base[1] + 4 * (u - 1)))
                    sp.dma_start(mo_w1[u], a["moe_w1"][bass.ds(e + u, 1)].rearrange("o (k p) n -> p (o k) n", p=HC)).then_inc(sem(f"in_expert{u}"), 16)
                    sp.dma_start(mo_w2[u], a["moe_w2"][bass.ds(e + u, 1)].rearrange("o (m p) n -> p (o m) n", p=P)).then_inc(sem(f"in_expert{u}"), 16)
                    sp.dma_start(mo_b1[u], a["moe_b1"][bass.ds(e + u, 1)].rearrange("o p m -> p (o m)")).then_inc(sem(f"in_expert{u}"), 16)
            for t in range(T):
                sp.wait_ge(free[t % 2], moe_base[t % 2] + 4 * (NE - 1) + t // 2 + 1)
                sp.dma_start(out[t * P:(t + 1) * P, :], y[:, t, :]).then_inc(sem("out_stored"), 16)
            sp.wait_ge(sem("out_stored"), 16 * T)

        ROW = {"tokb": 0, "bqkvA": D, "boutA": 4 * D, "boutB": 5 * D, "b2": 6 * D, "route": 7 * D,
               "boutS": 7 * D + 64, "b2S": 8 * D + 64}
        COL = {"bqkA": 0, "n1l": 4, "n1s": 8, "n2l": 12, "n2s": 16, "scaleA": 20}

        def row(name, n=D):
            return rows_sb[0:1, ROW[name]:ROW[name] + n]

        @block.gpsimd
        def _(pool):
            step = [0]

            def link(ins):
                step[0] += 1
                ins.then_inc(sem("pool_step"), 1)
                pool.wait_ge(sem("pool_step"), step[0])

            nc.gpsimd.memset(ones[:], 1.0).then_inc(sem("ones_set"), 1)
            nc.gpsimd.memset(minus_half[:], -0.5).then_inc(sem("ones_set"), 1)
            pool.wait_ge(sem("ones_set"), 2)

            for n in range(2):
                s = slice(4 * n, 4 * n + 4)
                pool.wait_ge(sem("tokvar"), n + 1)
                nc.gpsimd.tensor_tensor(out=tokst[:, s, 3:4].rearrange("p t o -> p (t o)"), in0=tokst[:, s, 2:3].rearrange("p t o -> p (t o)"), in1=minus_half[:, s],
                                        op=ALU.pow).then_inc(sem("tokrstd"), 1)
            if True:
                loaded(pool, "small")
                loaded(pool, "B")
                loaded(pool, "mlp")
                link(nc.gpsimd.tensor_tensor(out=gum[:, 3:4], in0=gum[:, 0:1], in1=gum[:, 1:2], op=ALU.add))
                link(nc.gpsimd.tensor_tensor(out=gum[:, 4:5], in0=gum[:, 3:4], in1=gum[:, 2:3], op=ALU.add))

                def times(dst, src, g, p0, p1):
                    link(nc.gpsimd.tensor_scalar(out=dst, in0=src, scalar1=gum[p0:p1, g:g + 1], scalar2=None, op0=ALU.mult))

                for p0, p1, k, c0, c1, g in ((0, KEEP[2], 0, 0, KEEP[2], 4), (KEEP[2], HC, 0, 0, KEEP[2], 3),
                                             (0, HC, 0, KEEP[2], KEEP[1], 3), (0, HC, 0, KEEP[1], D, 0),
                                             (0, HC, 1, 0, D, 0)):
                    times(wout["S"][p0:p1, k, c0:c1], wout["B"][p0:p1, k, c0:c1], g, p0, p1)
                for dst, src in (("boutS", "boutB"), ("b2S", "b2")):
                    for c0, c1, g in ((0, KEEP[2], 4), (KEEP[2], KEEP[1], 3), (KEEP[1], D, 0)):
                        times(rows_sb[0:1, ROW[dst] + c0:ROW[dst] + c1], rows_sb[0:1, ROW[src] + c0:ROW[src] + c1], g, 0, 1)
                for i in range(3):
                    nc.gpsimd.tensor_scalar(out=w2s[i][:], in0=w2[:, :, 0:KEEP[i]], scalar1=gum[:, i:i + 1], scalar2=None, op0=ALU.mult).then_inc(sem("small_weights"), 1)

            ln = [0]

            def ln_rstd(first=0):
                for n in range(2):
                    s = slice(4 * n, 4 * n + 4)
                    ln[0] += 1
                    pool.wait_ge(sem("ln_stats"), ln[0])
                    link(nc.gpsimd.tensor_scalar(out=rstd[:, s], in0=mv[:, s, 1:2].rearrange("p t o -> p (t o)"), scalar1=EPS_LN, scalar2=None, op0=ALU.add))
                    nc.gpsimd.tensor_tensor(out=rstd[:, s], in0=rstd[:, s], in1=minus_half[:, s], op=ALU.pow).then_inc(sem("ln_rstd"), 1)

            for _ in range(5):
                ln_rstd()
            for t in range(T):
                pool.wait_ge(sem("D_probs"), t + 1)
                was_read(pool, "D", "V", t)
                if t >= 2:
                    pool.wait_ge(sem("D_rows"), t - 1)
                p = peff[t % 2].rearrange("p (a b) -> p a b", a=H)
                v = V[:, t, :].rearrange("p (b x) -> p x b", x=HD)
                nc.gpsimd.tensor_tensor(out=prodV[t % 2].rearrange("p (a x b) -> p a x b", a=H, x=HD), in0=repeat(p, 2, HD), in1=repeat(v, 1, H), op=ALU.mult).then_inc(sem("D_weighed"), 1)
            ln_rstd()

        @block.scalar
        def _(act):
            for c in range(FC):
                act.wait_ge(sem(f"in_pixels{c}"), 32)
                nc.scalar.activation(xsq[:, c], xf[:, c], ACT.Square).then_inc(sem("squares"), 1)

            def transposed(L, affine):
                for n in range(2):
                    for k in range(2):
                        ps = filled(act, L, "xT", n, k)
                        dst = xT[:, k, n * HALF:(n + 1) * HALF]
                        if affine:
                            c = affine[n] + k
                            ins = nc.scalar.activation(dst, ps[0:HC, :], ACT.Identity, scale=cols_sb[:, c:c + 1], bias=cols_sb[:, c + 2:c + 3])
                        else:
                            ins = nc.scalar.activation(dst, ps[0:HC, :], ACT.Copy)
                        ins.then_inc(free_of(L, "xT", n, k), 1)

            def attention(L):
                for n in range(2):
                    for o in range(4):
                        ps = filled(act, L, "qk", n, o)
                        if L == "A":
                            ins = nc.scalar.activation(qk[:, o, n, :], ps[0:HC, :], ACT.Identity, bias=cols_sb[:, COL["bqkA"] + o:COL["bqkA"] + o + 1])
                        else:
                            ins = nc.scalar.activation(qk[:, o, n, :], ps[0:HC, :], ACT.Copy)
                        ins.then_inc(free_of(L, "qk", n, o), 1)
                for t in range(T):
                    ps = filled(act, L, "V", t)
                    nc.scalar.activation(V[:, t, :], ps[:, 0:D], ACT.Copy).then_inc(free_of(L, "V", t), 1)
                u = 0
                for n in range(2):
                    for f in range(2):
                        u += 1
                        if L == "A":
                            act.wait_ge(sem("A_shifted"), u)
                        else:
                            was_read(act, L, "score", n, f)
                        p = prob[:, f, n, :]
                        nc.scalar.activation(p, p, ACT.Exp, scale={"A": 1.0, "B": HD ** -0.5}[L]).then_inc(sem(f"{L}_exp"), 1)
                for t in range(T + 2):
                    if 0 <= t - 1 < T:
                        ps = filled(act, L, "AV", t - 1)
                        if t - 1 >= 2:
                            act.wait_ge(full_of(L, "oT", t - 3), uses[L, "oT", t - 3][1] + 1)
                        nc.scalar.activation(osb[:, (t - 1) % 2, :], ps[:, 0:D], ACT.Copy).then_inc(free_of(L, "AV", t - 1), 1)
                    if 0 <= t - 2 < T:
                        ps = filled(act, L, "oT", t - 2)
                        if t - 2 >= 2:
                            act.wait_ge(full_of(L, "proj", t - 4), uses[L, "proj", t - 4][1] + 1)
                        nc.scalar.activation(oT[:, t % 2, :, :].rearrange("p k x -> p (k x)"), ps[0:HC, 0:2 * P], ACT.Copy).then_inc(free_of(L, "oT", t - 2), 1)

            loaded(act, "small")
            transposed("A", None)
            attention("A")
            transposed("B", (COL["n1l"], COL["n1s"]))
            attention("B")
            transposed("M", (COL["n2l"], COL["n2s"]))
            for i in (3, 2, 1, 0):
                for m in range(MC):
                    ps = filled(act, "fc1", i, m)
                    nc.scalar.activation(hT[i][:, m, :], ps[:, :], ACT.Gelu, bias=b1_sb[:, m:m + 1]).then_inc(free_of("fc1", i, m), 1)
            act.wait_ge(sem("lam_sums"), 1)
            nc.scalar.activation(lam[:, 2:4], lam[:, 0:2], ACT.Exp).then_inc(sem("lam_exp"), 1)
            transposed("D", None)
            for t in range(T):
                ps = filled(act, "D", "qk", t)
                nc.scalar.activation(qkD[:, t, :], ps[:, 0:2 * D], ACT.Copy).then_inc(free_of("D", "qk", t), 1)
                ps = filled(act, "D", "V", t)
                nc.scalar.activation(V[:, t, :], ps[:, 0:D], ACT.Copy).then_inc(free_of("D", "V", t), 1)
            for t in range(T + 3):
                if t < T:
                    act.wait_ge(sem("D_shifted"), t + 1)
                    nc.scalar.activation(scD[t % 3], scD[t % 3], ACT.Exp, scale=(HD // 2) ** -0.5).then_inc(sem("D_exp"), 1)
                if t >= 3:
                    q = t - 3
                    ps = filled(act, "D", "oT", q)
                    if q >= 2:
                        act.wait_ge(full_of("D", "proj", q - 2), uses["D", "proj", q - 2][1] + 1)
                    nc.scalar.activation(oT[:, q % 2, :, :].rearrange("p k x -> p (k x)"), ps[0:HC, 0:2 * P], ACT.Copy).then_inc(free_of("D", "oT", q), 1)
            transposed("R", None)
            act.wait_ge(sem("gate_shifted"), 1)
            nc.scalar.activation(gview("G", "d"), gview("G", "d"), ACT.Exp).then_inc(sem("gate_exp"), 1)
            act.wait_ge(sem("gate_shifted"), 2)
            nc.scalar.activation(gview("E", "d"), gview("E", "d"), ACT.Exp).then_inc(sem("gate_exp"), 1)
            with act.Fori(0, NE // 2) as pair:
                e = pair * 2
                for u in range(2):
                    act.wait_ge(sem(f"in_expert{u}"), e * 24 + 48)
                    for n in range(2):
                        for m in range(MC):
                            act.wait_ge(full[2 + m], e * 2 + (moe_base[2 + m] + 2 * u + n + 1))
                            if m == 0:
                                act.wait_ge(full[1], e * 4 + (moe_base[1] + 4 * u + 2 * n))
                            nc.scalar.activation(mo_hT[:, m, :], bank[2 + m][:, :], ACT.Gelu, bias=mo_b1[u][:, m:m + 1]).then_inc(free[2 + m], 1)

        @block.vector
        def _(dve):
            step = [0]

            def link(ins):
                step[0] += 1
                ins.then_inc(sem("dve_step"), 1)
                dve.wait_ge(sem("dve_step"), step[0])

            tt, ts, stt = nc.vector.tensor_tensor, nc.vector.tensor_scalar, nc.vector.scalar_tensor_tensor
            loaded(dve, "const")
            for c in range(FC):
                dve.wait_ge(sem(f"in_pixels{c}"), 32)
                link(ts(out=weff[:, c, :], in0=w5[:, c, 0, :], scalar1=gamma5[:, 0, c:c + 1], scalar2=None, op0=ALU.mult))
                for v in range(1, NSH):
                    ins = stt(out=weff[:, c, :], in0=w5[:, c, v, :], scalar=gamma5[:, v, c:c + 1], in1=weff[:, c, :], op0=ALU.mult, op1=ALU.add)
                    if v < NSH - 1:
                        link(ins)
                ins.then_inc(sem("weff"), 1)
            ps = filled(dve, "cbias")
            nc.vector.tensor_copy(cbias[:], ps[:, 0:D]).then_inc(free_of("cbias"), 1)
            ps = filled(dve, "colsum")
            nc.vector.tensor_copy(colsum[:], ps[:, 0:D]).then_inc(free_of("colsum"), 1)
            was_read(dve, "cbias")
            was_read(dve, "colsum")
            for n in range(2):
                s = slice(4 * n, 4 * n + 4)
                for t in range(4 * n, 4 * n + 4):
                    ps = filled(dve, "tok", t)
                    link(nc.vector.tensor_copy(tokst[:, t, 0:2], ps[:, D:D + 2]))
                    link(stt(out=tokst[:, t, 2:3], in0=tokst[:, t, 0:1], scalar=tokst[:, t, 0:1], in1=tokst[:, t, 1:2], op0=ALU.mult, op1=ALU.subtract))
                ts(out=tokst[:, s, 2:3].rearrange("p t o -> p (t o)"), in0=tokst[:, s, 2:3].rearrange("p t o -> p (t o)"), scalar1=-1.0, scalar2=EPS_LN,
                   op0=ALU.mult, op1=ALU.add).then_inc(sem("tokvar"), 1)
                dve.wait_ge(sem("tokrstd"), n + 1)
                link(ts(out=tokst[:, s, 3:4].rearrange("p t o -> p (t o)"), in0=tokst[:, s, 3:4].rearrange("p t o -> p (t o)"), scalar1=-1.0, scalar2=None, op0=ALU.mult))
                for t in range(4 * n, 4 * n + 4):
                    ps = bank[uses["tok", t][0]]
                    stt(out=tmpt[:, t % 2, :], in0=colsum[:], scalar=tokst[:, t, 0:1], in1=ps[:, 0:D], op0=ALU.mult, op1=ALU.subtract).then_inc(free_of("tok", t), 1)
                    was_read(dve, "tok", t)
                    link(stt(out=h[:, t, :], in0=tmpt[:, t % 2, :], scalar=tokst[:, t, 3:4], in1=cbias[:], op0=ALU.mult, op1=ALU.add))

            ln = [0]

            def layernorm(src, dst, name, ready=None):
                for n in range(2):
                    for t in range(4 * n, 4 * n + 4):
                        if ready:
                            ready(t)
                        link(nc.vector.bn_stats(out=stats[:, t, :], in_=src[:, t, :]))
                    for t in range(4 * n, 4 * n + 4):
                        ins = nc.vector.bn_aggr(out=mv[:, t, :], in_=stats[:, t, :])
                        if t < 4 * n + 3:
                            link(ins)
                        else:
                            ins.then_inc(sem("ln_stats"), 1)
                for n in range(2):
                    ln[0] += 1
                    dve.wait_ge(sem("ln_rstd"), ln[0])
                    for t in range(4 * n, 4 * n + 4):
                        ts(out=dst[:, t, :], in0=src[:, t, :], scalar1=mv[:, t, 0:1], scalar2=rstd[:, t:t + 1],
                           op0=ALU.subtract, op1=ALU.mult).then_inc(sem(f"normed_{name}"), 1)

            def attention(L, residual, dst):
                units = [(n, f) for n in range(2) for f in range(2)]

                def spread(n, f):
                    was_read(dve, L, "qk", n, f)
                    for hh in range(HH):
                        ins = ts(out=qbd[2 * n + f][:, :, hh, :], in0=qk[:, f, n, :].rearrange("p (b i) -> p b i", i=NTOK),
                                 scalar1=headmask[:, hh:hh + 1], scalar2=None, op0=ALU.mult)
                    ins.then_inc(sem(f"{L}_spread"), 1)

                def softmax_front(n, f, u):
                    ps = filled(dve, L, "score", n, f)
                    sc = ps[0:HC, :].rearrange("p (b j) -> p b j", j=NTOK)
                    p = prob[:, f, n, :].rearrange("p (b j) -> p b j", j=NTOK)
                    if L == "A":
                        stt(out=p, in0=sc, scalar=cols_sb[:, COL["scaleA"] + f:COL["scaleA"] + f + 1], in1=repeat(selfmask[:], 1, IB), op0=ALU.mult, op1=ALU.add).then_inc(free_of(L, "score", n, f), 1)
                        was_read(dve, L, "score", n, f)
                        sc = p
                    link(nc.vector.reduce_max(smx[:, u % 2, :], sc, AX_X))
                    tt(out=p, in0=sc, in1=repeat(smx[:, u % 2, :], 2, NTOK), op=ALU.subtract).then_inc(sem("A_shifted") if L == "A" else free_of(L, "score", n, f), 1)

                def softmax_back(n, f, u):
                    p = prob[:, f, n, :].rearrange("p (b j) -> p b j", j=NTOK)
                    dve.wait_ge(sem(f"{L}_exp"), u + 1)
                    link(nc.vector.reduce_sum(ssum[:, u % 2, :], p, AX_X))
                    link(nc.vector.reciprocal(srec[:, u % 2, :], ssum[:, u % 2, :]))
                    tt(out=p, in0=p, in1=repeat(srec[:, u % 2, :], 2, NTOK), op=ALU.mult).then_inc(sem(f"{L}_probs"), 1)

                for k in range(4 + 4):
                    if k < 4:
                        spread(*units[k])
                    if 0 <= k - 2 < 4:
                        softmax_front(*units[k - 2], k - 2)
                    if 0 <= k - 4 < 4:
                        softmax_back(*units[k - 4], k - 4)
                for t in range(T + 3):
                    if t < T:
                        ps = filled(dve, L, "PT", t)
                        if t >= 2:
                            dve.wait_ge(full_of(L, "AV", t - 2), uses[L, "AV", t - 2][1] + 1)
                        src = ps[:, 0:D].rearrange("p (h i) -> p h i", i=NTOK)
                        tt(out=ptbd[t % 2], in0=repeat(src, 2, TB),
                           in1=repeat(repeat(blockmask[:], 1, H), 3, NTOK), op=ALU.mult).then_inc(free_of(L, "PT", t), 1)
                    if t >= 3:
                        ps = filled(dve, L, "proj", t - 3)
                        tt(out=dst[:, t - 3, :], in0=ps[:, 0:D], in1=residual[:, t - 3, :], op=ALU.add).then_inc(free_of(L, "proj", t - 3), 1)

            layernorm(h, xn, "A")
            loaded(dve, "small")
            attention("A", h, h)
            layernorm(h, z, "z", lambda t: was_read(dve, "A", "proj", t))
            layernorm(z, xn, "B", lambda t: dve.wait_ge(sem("normed_z"), t + 1))
            attention("B", z, z)
            layernorm(z, xn, "M", lambda t: was_read(dve, "B", "proj", t))
            for t in range(T):
                ps = filled(dve, "fc2", t)
                tt(out=z[:, t, :], in0=ps[:, 0:D], in1=z[:, t, :], op=ALU.add).then_inc(free_of("fc2", t), 1)
                was_read(dve, "fc2", t)
                link(tt(out=h[:, t, :], in0=z[:, t, :], in1=h[:, t, :], op=ALU.add))
            loaded(dve, "small")
            for s in range(2):
                link(tt(out=lamv[:, 2 * s, :], in0=lamv[:, 2 * s, :], in1=lamv[:, 2 * s + 1, :], op=ALU.mult))
                ins = nc.vector.reduce_sum(lam[:, s:s + 1], lamv[:, 2 * s, :], AX_X)
                if s == 0:
                    link(ins)
                else:
                    ins.then_inc(sem("lam_sums"), 1)
            dve.wait_ge(sem("lam_exp"), 1)
            link(tt(out=lam[:, 4:5], in0=lam[:, 3:4], in1=lam[:, 2:3], op=ALU.subtract))
            link(ts(out=lam[:, 5:6], in0=lam[:, 4:5], scalar1=LAMBDA_INIT, scalar2=None, op0=ALU.subtract))
            link(ts(out=lam[:, 7:8], in0=lam[:, 5:6], scalar1=1.0 - LAMBDA_INIT, scalar2=None, op0=ALU.mult))
            link(nc.vector.memset(headfac[:], 1.0))
            link(ts(out=headfac[:, 1, :], in0=headfac[:, 1, :], scalar1=lam[:, 7:8], scalar2=None, op0=ALU.mult))
            link(ts(out=headfac[:, 0, :], in0=headfac[:, 0, :], scalar1=1.0 - LAMBDA_INIT, scalar2=None, op0=ALU.mult))
            layernorm(h, xn, "D")
            for t in range(T + 5):
                if t < T:
                    was_read(dve, "D", "qk", t)
                    q = qkD[:, t, 0:D].rearrange("p (h x) -> p h x", h=H)
                    k = qkD[:, t, D:2 * D].rearrange("p (h x) -> p h x", h=H)
                    pr = prodS[t % 2].rearrange("p (a b x) -> p a b x", a=H, b=H)
                    link(tt(out=pr, in0=repeat(q, 2, H), in1=repeat(k, 1, H), op=ALU.mult))
                    sc, mx = scD[t % 3], mxD[t % 3]
                    link(nc.vector.reduce_sum(sc.rearrange("p (s y) -> p y s", s=2), prodS[t % 2].rearrange("p (y s x) -> p y s x", s=2, x=HD // 2), AX_X))
                    sc3 = sc.rearrange("p (s x) -> p s x", x=H)
                    link(nc.vector.reduce_max(mx, sc3, AX_X))
                    tt(out=sc3, in0=sc3, in1=repeat(mx, 2, H), op=ALU.subtract).then_inc(sem("D_shifted"), 1)
                if 0 <= t - 1 < T:
                    q = t - 1
                    sc, mx = scD[q % 3], mxD[q % 3]
                    sc3 = sc.rearrange("p (s x) -> p s x", x=H)
                    dve.wait_ge(sem("D_exp"), q + 1)
                    link(nc.vector.reduce_sum(mx, sc3, AX_X))
                    link(nc.vector.reciprocal(mx, mx))
                    link(tt(out=mx, in0=mx, in1=headfac[:].rearrange("p s h -> p (s h)"), op=ALU.mult))
                    link(tt(out=sc3, in0=sc3, in1=repeat(mx, 2, H), op=ALU.mult))
                    if q >= 2:
                        dve.wait_ge(sem("D_weighed"), q - 1)
                    tt(out=peff[q % 2], in0=sc[:, 0:H * H], in1=sc[:, H * H:2 * H * H], op=ALU.add).then_inc(sem("D_probs"), 1)
                if 0 <= t - 3 < T:
                    q = t - 3
                    dve.wait_ge(sem("D_weighed"), q + 1)
                    if q >= 2:
                        dve.wait_ge(full_of("D", "oT", q - 2), uses["D", "oT", q - 2][1] + 1)
                    nc.vector.reduce_sum(oD[q % 2], prodV[q % 2].rearrange("p (y x) -> p y x", x=H), AX_X).then_inc(sem("D_rows"), 1)
                if t >= 5:
                    q = t - 5
                    ps = filled(dve, "D", "proj", q)
                    tt(out=h[:, q, :], in0=ps[:, 0:D], in1=h[:, q, :], op=ALU.add).then_inc(free_of("D", "proj", q), 1)
            layernorm(h, xn, "R", lambda t: was_read(dve, "D", "proj", t))

            for t in range(T):
                ps = filled(dve, "logit", t)
                link(nc.vector.tensor_copy(lgG[:, t, :], ps[:, 0:G]))
                nc.vector.tensor_copy(comb[:, t, :], ps[:, G:G + NE]).then_inc(free_of("logit", t), 1)
            was_read(dve, "logit", T - 2)
            was_read(dve, "logit", T - 1)
            link(nc.vector.tensor_copy(lgE.rearrange("p r e -> p (r e)"), comb.rearrange("p t e -> p (t e)")))

            def top_gates(which, lg, R, n, k, order):
                a4 = cmpa[:, 0:R * n * n].rearrange("p (r a b) -> p r a b", a=n, b=n)
                b4 = cmpb[:, 0:R * n * n].rearrange("p (r a b) -> p r a b", a=n, b=n)
                other, own = repeat(lg, 2, n), repeat(lg, 3, n)
                link(tt(out=a4, in0=other, in1=own, op=ALU.is_gt))
                link(tt(out=b4, in0=other, in1=own, op=ALU.is_equal))
                low = tri[:].rearrange("p (a b) -> p a b", b=E)[:, 0:n, 0:n]
                link(tt(out=b4, in0=b4, in1=repeat(low, 1, R), op=ALU.mult))
                link(tt(out=a4, in0=a4, in1=b4, op=ALU.add))
                sel, d, mx = gview(which, "sel"), gview(which, "d"), gview(which, "mx")
                link(nc.vector.reduce_sum(sel, a4, AX_X))
                link(ts(out=sel, in0=sel, scalar1=float(k), scalar2=None, op0=ALU.is_lt))
                link(nc.vector.reduce_max(mx, lg, AX_X))
                tt(out=d, in0=lg, in1=repeat(mx, 2, n), op=ALU.subtract).then_inc(sem("gate_shifted"), 1)
                dve.wait_ge(sem("gate_exp"), order)
                link(tt(out=d, in0=d, in1=sel, op=ALU.mult))
                link(nc.vector.reduce_sum(mx, d, AX_X))
                link(nc.vector.reciprocal(mx, mx))
                link(tt(out=d, in0=d, in1=repeat(mx, 2, n), op=ALU.mult))
                link(stt(out=d, in0=d, scalar=EPS_GATE, in1=d, op0=ALU.is_ge, op1=ALU.mult))

            top_gates("G", lgG, T, G, KG, 1)
            top_gates("E", lgE, T * G, E, KE, 2)
            gg = gview("G", "d").rearrange("p r e -> p (r e)")
            tt(out=comb.rearrange("p t (g e) -> p (t g) e", e=E), in0=gview("E", "d"), in1=repeat(gg, 2, E), op=ALU.mult).then_inc(sem("combined"), 1)
            for t in range(T):
                ps = filled(dve, "cT", t)
                nc.vector.tensor_copy(cT[:, t, :], ps[0:NE, 0:P]).then_inc(free_of("cT", t), 1)
                ps = filled(dve, "y0", t)
                tt(out=y[:, t, :], in0=ps[:, 0:D], in1=h[:, t, :], op=ALU.add).then_inc(free_of("y0", t), 1)
            was_read(dve, "y0", T - 1)
            with dve.Fori(0, NE // 2) as pair:
                e = pair * 2
                for u in range(2):
                    for t in range(T):
                        b = t % 2
                        dve.wait_ge(full[b], e * 4 + (moe_base[b] + 4 * u + t // 2 + 1))
                        dve.wait_ge(free[b], e * 4 + (moe_base[b] + 4 * u + t // 2))
                        stt(out=y[:, t, :], in0=bank[b][:, 0:D], scalar=comb[:, t, bass.ds(e + u, 1)], in1=y[:, t, :], op0=ALU.mult, op1=ALU.add).then_inc(free[b], 1)

        @block.tensor
        def _(pe):
            mm = nc.tensor.matmul
            pe.wait_ge(sem("ones_set"), 2)
            loaded(pe, "const")

            def tok_products(tiles):
                for c in range(FC):
                    for t in tiles:
                        if c == 0:
                            claim("tok", t)
                        if t == 0:
                            pe.wait_ge(sem("weff"), c + 1)
                        x = xf[:, c, t * P:(t + 1) * P]
                        ps = bank[uses["tok", t][0]]
                        mm(ps[:, 0:D], x, weff[:, c, :], start=(c == 0), stop=(c == FC - 1))

            def tok_sums(tiles):
                for col, src in ((D, xf), (D + 1, xsq)):
                    for c in range(FC):
                        pe.wait_ge(sem("squares"), c + 1)
                        for t in tiles:
                            ps = bank[uses["tok", t][0]]
                            ins = mm(ps[:, col:col + 1], src[:, c, t * P:(t + 1) * P], cnt[:, c:c + 1], start=(c == 0), stop=(c == FC - 1))
                            if col == D + 1 and c == FC - 1:
                                ins.then_inc(full_of("tok", t), 1)

            first = range(T // 2)
            tok_products(first)
            tok_sums(first)
            loaded(pe, "small")
            ps = claim("cbias")
            for c in range(FC):
                for v in range(NSH):
                    mm(ps[:, 0:D], beta5[:, v, c:c + 1].broadcast_to([FP, P]), w5[:, c, v, :], start=(c == 0 and v == 0), stop=False)
            mm(ps[:, 0:D], ones[0:1, :], row("tokb"), start=False, stop=True).then_inc(full_of("cbias"), 1)
            ps = claim("colsum")
            for c in range(FC):
                ins = mm(ps[:, 0:D], ones[0:FP, :], weff[:, c, :], start=(c == 0), stop=(c == FC - 1))
            ins.then_inc(full_of("colsum"), 1)
            tok_products(range(T // 2, T))
            tok_sums(range(T // 2, T))

            def transposes(L):
                for n in range(2):
                    for k in range(2):
                        ps = claim(L, "xT", n, k)
                        for j in range(4):
                            t = 4 * n + j
                            if k == 0:
                                pe.wait_ge(sem(f"normed_{L}"), t + 1)
                            ins = nc.tensor.transpose(ps[0:HC, j * P:(j + 1) * P], xn[:, t, k * HC:(k + 1) * HC], ident[:])
                        ins.then_inc(full_of(L, "xT", n, k), 1)

            def attention(L):
                W = weights[L]
                loaded(pe, L)
                for n in range(2):
                    for k in range(2):
                        was_read(pe, L, "xT", n, k)
                    for o in range(4):
                        ps = claim(L, "qk", n, o)
                        for k in range(2):
                            ins = mm(ps[0:HC, :], W[:, k, o * HC:(o + 1) * HC], xT[:, k, n * HALF:(n + 1) * HALF], start=(k == 0), stop=(k == 1))
                        ins.then_inc(full_of(L, "qk", n, o), 1)
                for t in range(T):
                    ps = claim(L, "V", t)
                    for k in range(2):
                        ins = mm(ps[:, 0:D], xT[:, k, t * P:(t + 1) * P], W[:, k, 2 * D:3 * D], start=(k == 0), stop=(k == 1 and L != "A"))
                    if L == "A":
                        ins = mm(ps[:, 0:D], ones[0:1, :], rows_sb[0:1, ROW["bqkvA"] + 2 * D:ROW["bqkvA"] + 3 * D], start=False, stop=True)
                    ins.then_inc(full_of(L, "V", t), 1)
                u = 0
                for n in range(2):
                    for f in range(2):
                        u += 1
                        pe.wait_ge(sem(f"{L}_spread"), u)
                        was_read(pe, L, "qk", n, 2 + f)
                        ps = claim(L, "score", n, f)
                        for b in range(IB):
                            ins = mm(ps[0:HC, b * NTOK:(b + 1) * NTOK], qbd[2 * n + f][:, b, :, :].rearrange("p h i -> p (h i)"),
                                     qk[:, 2 + f, n, b * NTOK:(b + 1) * NTOK], start=True, stop=True)
                        ins.then_inc(full_of(L, "score", n, f), 1)
                for t in range(T + 3):
                    if t < T:
                        n = t // 4
                        pe.wait_ge(sem(f"{L}_probs"), 2 * n + 2)
                        ps = claim(L, "PT", t)
                        for f in range(2):
                            ins = nc.tensor.transpose(ps[:, f * HC:(f + 1) * HC], prob[:, f, n, (t % 4) * P:(t % 4 + 1) * P], ident[0:HC, 0:HC])
                        ins.then_inc(full_of(L, "PT", t), 1)
                    if 0 <= t - 1 < T:
                        q = t - 1
                        was_read(pe, L, "PT", q)
                        was_read(pe, L, "V", q)
                        ps = claim(L, "AV", q)
                        for hh in range(H):
                            ins = mm(ps[:, hh * HD:(hh + 1) * HD], ptbd[q % 2][:, hh, :, :].rearrange("p b i -> p (b i)"), V[:, q, hh * HD:(hh + 1) * HD], start=True, stop=True)
                        ins.then_inc(full_of(L, "AV", q), 1)
                    if 0 <= t - 2 < T:
                        q = t - 2
                        was_read(pe, L, "AV", q)
                        ps = claim(L, "oT", q)
                        for k in range(2):
                            ins = nc.tensor.transpose(ps[0:HC, k * P:(k + 1) * P], osb[:, q % 2, k * HC:(k + 1) * HC], ident[:])
                        ins.then_inc(full_of(L, "oT", q), 1)
                    if 0 <= t - 3 < T:
                        q = t - 3
                        was_read(pe, L, "oT", q)
                        ps = claim(L, "proj", q)
                        wo = wout["S"] if L == "B" and q >= T // 2 else wout[L]
                        if L == "B" and q == T // 2:
                            pe.wait_ge(sem("small_weights"), 3)
                        for k in range(2):
                            ins = mm(ps[:, 0:D], oT[:, q % 2, k, :], wo[:, k, :], start=(k == 0), stop=False)
                        if True:
                            ins = mm(ps[:, 0:D], ones[0:1, :], row("boutA" if L == "A" else "boutB" if q < T // 2 else "boutS"), start=False, stop=True)
                        ins.then_inc(full_of(L, "proj", q), 1)

            transposes("A")
            attention("A")
            transposes("B")
            attention("B")
            transposes("M")
            loaded(pe, "mlp")
            for k in range(2):
                was_read(pe, "M", "xT", 0, k)
            for m in range(MC):
                ps = claim("fc1", 3, m)
                for k in range(2):
                    ins = mm(ps[:, :], w1[:, k, m * P:(m + 1) * P], xT[:, k, 0:HALF], start=(k == 0), stop=(k == 1))
                ins.then_inc(full_of("fc1", 3, m), 1)
            for k in range(2):
                was_read(pe, "M", "xT", 1, k)
            for i, p0, p1, k in ((2, 0, KEEP[2], 0), (1, KEEP[2], KEEP[1], 0), (0, 0, HC, 1)):
                for m in range(MC):
                    ps = claim("fc1", i, m)
                    mm(ps[:, :], w1[p0:p1, k, m * P:(m + 1) * P], xT[p0:p1, k, HALF:TOK], start=(i == 2), stop=True, skip_group_check=(i != 2)).then_inc(full_of("fc1", i, m), 1)
            for t in range(T):
                ps = claim("fc2", t)
                col = slice((t % 4) * P, (t % 4 + 1) * P)
                if t < T // 2:
                    for m in range(MC):
                        was_read(pe, "fc1", 3, m)
                        mm(ps[:, 0:D], hT[3][:, m, col], w2[:, m, :], start=(m == 0), stop=False)
                    mm(ps[:, 0:D], ones[0:1, :], row("b2"), start=False, stop=True).then_inc(full_of("fc2", t), 1)
                else:
                    mm(ps[:, 0:D], ones[0:1, :], row("b2S"), start=True, stop=False)
                    for i in (2, 1, 0):
                        for m in range(MC):
                            was_read(pe, "fc1", i, m)
                            ins = mm(ps[:, 0:KEEP[i]], hT[i][:, m, col], w2s[i][:, m, :], start=False, stop=(i == 0 and m == MC - 1))
                    ins.then_inc(full_of("fc2", t), 1)
            transposes("D")
            loaded(pe, "D")
            W = weights["D"]
            for t in range(T):
                for k in range(2):
                    was_read(pe, "D", "xT", t // 4, k)
                for name, c0, c1 in (("qk", 0, 2 * D), ("V", 2 * D, 3 * D)):
                    ps = claim("D", name, t)
                    for k in range(2):
                        ins = mm(ps[:, 0:c1 - c0], xT[:, k, t * P:(t + 1) * P], W[:, k, c0:c1], start=(k == 0), stop=(k == 1))
                    ins.then_inc(full_of("D", name, t), 1)
            for t in range(T + 1):
                if t < T:
                    pe.wait_ge(sem("D_rows"), t + 1)
                    ps = claim("D", "oT", t)
                    for k in range(2):
                        ins = nc.tensor.transpose(ps[0:HC, k * P:(k + 1) * P], oD[t % 2][:, k * HC:(k + 1) * HC], ident[:])
                    ins.then_inc(full_of("D", "oT", t), 1)
                if t >= 1:
                    was_read(pe, "D", "oT", t - 1)
                    ps = claim("D", "proj", t - 1)
                    for k in range(2):
                        ins = mm(ps[:, 0:D], oT[:, (t - 1) % 2, k, :], wout["D"][:, k, :], start=(k == 0), stop=(k == 1))
                    ins.then_inc(full_of("D", "proj", t - 1), 1)
            transposes("R")
            for n in range(2):
                for k in range(2):
                    was_read(pe, "R", "xT", n, k)
            for t in range(T):
                ps = claim("logit", t)
                for k in range(2):
                    mm(ps[:, 0:G + NE], xT[:, k, t * P:(t + 1) * P], wr[:, k, :], start=(k == 0), stop=False)
                mm(ps[:, 0:G + NE], ones[0:1, :], row("route", G + NE), start=False, stop=True).then_inc(full_of("logit", t), 1)
            pe.wait_ge(sem("combined"), 1)
            for t in range(T):
                ps = claim("cT", t)
                nc.tensor.transpose(ps[0:NE, 0:P], comb[:, t, :], ident[:]).then_inc(full_of("cT", t), 1)
                was_read(pe, "cT", t)
                ps = claim("y0", t)
                mm(ps[:, 0:D], cT[:, t, :], b2all[:], start=True, stop=True).then_inc(full_of("y0", t), 1)
            with pe.Fori(0, NE // 2) as pair:
                e = pair * 2
                for u in range(2):
                    pe.wait_ge(sem(f"in_expert{u}"), e * 24 + 48)
                    for n in range(2):
                        for m in range(MC):
                            pe.wait_ge(free[2 + m], e * 2 + (moe_base[2 + m] + 2 * u + n))
                            for k in range(2):
                                ins = mm(bank[2 + m][:, :], mo_w1[u][:, k, m * P:(m + 1) * P], xT[:, k, n * HALF:(n + 1) * HALF], start=(k == 0), stop=(k == 1))
                            ins.then_inc(full[2 + m], 1)
                        for j in range(4):
                            b = j % 2
                            pe.wait_ge(free[b], e * 4 + (moe_base[b] + 4 * u + 2 * n + j // 2))
                            for m in range(MC):
                                if j == 0:
                                    pe.wait_ge(free[2 + m], e * 2 + (moe_base[2 + m] + 2 * u + n + 1))
                                ins = mm(bank[b][:, 0:D], mo_hT[:, m, j * P:(j + 1) * P], mo_w2[u][:, m, :], start=(m == 0), stop=(m == MC - 1))
                            ins.then_inc(full[b], 1)
        for k, v in lots.items():
            assert v == LOT[k], (k, v)


def kernel(**inputs):
    import concourse.bacc as bacc
    from concourse.bass_utils import run_bass_kernel_spmd

    f32 = np.float32
    i = {k: np.asarray(v) for k, v in inputs.items()}

    order, rows = pixel_layout()
    padded = np.pad(i["x"], ((0, 0), (0, 0), (1, 1), (1, 1)))
    xf = np.empty((NF, B, SIDE, SIDE), f32)
    for f, (c, r, w) in enumerate(order):
        xf[f] = padded[:, c, r + 1:r + 1 + IMG:PATCH, w + 1:w + 1 + IMG:PATCH][:, :SIDE, :SIDE]
    xf = xf.reshape(FC, FP, TOK)

    def by_shift(a):
        a = np.concatenate([a, np.zeros((1,) + a.shape[1:], a.dtype)])
        return a[rows]

    w5 = by_shift(i["L0_tok_w"]).reshape(NSH, FC, FP, D).transpose(1, 2, 0, 3)
    arr = {
        "xf": xf, "w5": w5,
        "gamma5": by_shift(i["L0_tok_ln_gamma"]).reshape(NSH, FC, FP).transpose(2, 0, 1),
        "beta5": by_shift(i["L0_tok_ln_beta"]).reshape(NSH, FC, FP).transpose(2, 0, 1),
        "cnt": ((rows >= 0).sum(0) / NPATCH).astype(f32).reshape(FC, FP).T,
        "ident": np.eye(P, dtype=f32),
        "blockmask": (np.arange(P)[:, None] // NTOK == np.arange(TB)[None, :]).astype(f32),
        "wqkvA": i["L0_attn_w_qkv"], "woutA": i["L0_attn_w_proj"],
        "wqkvB": i["L0_ffn_w_qkv"], "woutB": i["L0_ffn_w_proj"],
        "wqkvD": i["L1_attn_W_attn"].T, "woutD": i["L1_attn_W_out"].T,
        "gum": i["L0_ffn_gumbel_weights"].reshape(1, 3),
        "lamv": np.stack([i["L1_attn_lambda_q1"], i["L1_attn_lambda_k1"], i["L1_attn_lambda_q2"], i["L1_attn_lambda_k2"]])[None],
        "b1": i["L0_ffn_b_fc1"].reshape(MC, P).T, "w1": i["L0_ffn_w_fc1"], "w2": i["L0_ffn_w_fc2"],
        "wr": np.concatenate([i["L1_ffn_Wg"], i["L1_ffn_We"].transpose(1, 0, 2).reshape(D, NE)], 1),
        "moe_w1": i["L1_ffn_W1"].reshape(NE, D, HID), "moe_b1": i["L1_ffn_b1"].reshape(NE, MC, P).transpose(0, 2, 1),
        "moe_w2": i["L1_ffn_W2"].reshape(NE, HID, D), "moe_b2": i["L1_ffn_b2"].reshape(NE, D),
    }
    c = np.arange(HC)
    arr["headmask"] = (c[:, None] // HD == np.arange(HH)[None, :]).astype(f32)
    j = np.arange(NTOK)
    arr["selfmask"] = np.where((c % NTOK)[:, None] == j[None, :], np.where(j > 0, NEG, 0.0)[None, :], 0.0).astype(f32)
    arr["tri"] = np.tile((np.arange(E)[None, :] < np.arange(E)[:, None]).astype(f32).reshape(1, E * E), (P, 1))
    rowv = np.zeros((1, 2048), f32)
    pieces = [i["L0_tok_b"], i["L0_attn_b_qkv"], i["L0_attn_b_proj"], i["L0_ffn_b_proj"], i["L0_ffn_b_fc2"],
              i["L1_ffn_bg"], i["L1_ffn_be"].reshape(NE)]
    n = 0
    for p in pieces:
        rowv[0, n:n + p.size] = p
        n += p.size
    arr["rows"] = rowv
    colv = np.zeros((HC, 24), f32)
    colv[:, 0:4] = i["L0_attn_b_qkv"][:4 * HC].reshape(4, HC).T
    for at, name in ((4, "n1l"), (8, "n1s"), (12, "n2l"), (16, "n2s")):
        colv[:, at:at + 2] = i[f"L0_ffn_{name}_g"].reshape(2, HC).T
        colv[:, at + 2:at + 4] = i[f"L0_ffn_{name}_b"].reshape(2, HC).T
    colv[:, 20:22] = np.repeat(i["L0_attn_scale"], NTOK).reshape(2, HC).T
    arr["cols"] = colv

    nc = bacc.Bacc("TRN2", target_bir_lowering=False, num_devices=1)
    arrays = {f"in_{k}_dram": np.ascontiguousarray(v) for k, v in arr.items()}
    aps = {k: nc.dram_tensor(f"in_{k}_dram", arrays[f"in_{k}_dram"].shape, F32, kind="ExternalInput").ap() for k in arr}
    out = nc.dram_tensor("out_0_dram", (TOK, D), F32, kind="ExternalOutput").ap()
    vit_tower(nc, aps, out)
    r = run_bass_kernel_spmd(nc, [arrays], core_ids=[0])
    return r.results[0]["out_0_dram"].reshape(B, NTOK, D)
```

```python
from contextlib import ExitStack

import numpy as np

import concourse.bass as bass
from concourse import mybir
from concourse.alu_op_type import AluOpType as ALU

ACT = mybir.ActivationFunctionType
F32 = mybir.dt.float32
U32 = mybir.dt.uint32
I32 = mybir.dt.int32
AX_X = mybir.AxisListType.X

P = 128
B, NCH, IMG, PATCH = 64, 3, 64, 16
SIDE = IMG // PATCH
NTOK = SIDE * SIDE
TOK = B * NTOK
T = TOK // P
TB = P // NTOK
D = 192
HC = D // 2
H, HH, HD = 12, 6, 16
HALF = TOK // 2
IB = B // 2
HID = 768
MC = HID // P
NSH = 5
NF = NCH * ((PATCH + 2) ** 2 - 4)
FC, FP = 8, NF // 8
NPATCH = PATCH * PATCH * NSH * NCH
KEEP = (D, D // 2, D // 3)
G, E, KG, KE = 4, 8, 2, 4
NE = G * E
EPS_LN, EPS_GATE = 1e-5, 1e-6
LAMBDA_INIT = 0.8 - 0.6 * float(np.exp(-0.3 * 12))
KSEL = KG * KE
SLOTS = TOK + P
META = 1 + NE
ROWN = D + META
GROUPS = ((0, 4), (4, 8))
NEG = -1.0e30


def pixel_layout():
    order = [(c, i, j) for c in range(NCH) for i in range(-1, PATCH + 1) for j in range(-1, PATCH + 1)
             if not (i in (-1, PATCH) and j in (-1, PATCH))]
    moves = [(0, 0), (0, -1), (0, 1), (-1, 0), (1, 0)]
    rows = np.full((NSH, NF), -1, np.int64)
    for f, (c, i, j) in enumerate(order):
        for v, (di, dj) in enumerate(moves):
            pi, pj = i - di, j - dj
            if 0 <= pi < PATCH and 0 <= pj < PATCH:
                rows[v, f] = (pi * PATCH + pj) * NSH * NCH + v * NCH + c
    return order, rows


def repeat(ap, axis, n):
    ap = ap.unsqueeze(axis)
    shape = list(ap.shape)
    shape[axis] = n
    return ap.broadcast_to(shape)


def vit_tower(nc, a, out):
    ctx = ExitStack()
    with ctx:
        def sb(name, shape, dtype=F32):
            return ctx.enter_context(nc.sbuf_tensor(name, shape, dtype))

        dispatch = nc.dram_tensor("dispatch", (NE * SLOTS, ROWN), F32, kind="Internal").ap()
        summed = nc.dram_tensor("summed", (TOK + P, D), F32, kind="Internal").ap()

        sems = {}

        def sem(name):
            if name not in sems:
                sems[name] = ctx.enter_context(nc.semaphore(name))
            return sems[name]

        ident = sb("ident", [P, P])
        ones = sb("ones", [P, P])
        blockmask = sb("blockmask", [P, TB])
        headmask = sb("headmask", [HC, HH])
        selfmask = sb("selfmask", [HC, NTOK])
        tri = sb("tri", [P, E * E])
        cnt = sb("cnt", [FP, FC])
        gamma5 = sb("gamma5", [FP, NSH, FC])
        beta5 = sb("beta5", [FP, NSH, FC])
        minus_half = sb("minus_half", [P, T])
        rows_sb = sb("rows_sb", [1, 2048])
        cols_sb = sb("cols_sb", [HC, 24])
        b1_sb = sb("b1_sb", [P, MC])
        gum = sb("gum", [P, 5])
        lamv = sb("lamv", [P, 4, 8])
        lam = sb("lam", [P, 8])
        headfac = sb("headfac", [P, 2, H])
        wab = sb("wab", [HC, 2 * 2 * 3 * D])
        weights = {L: wab[:, n * 6 * D:(n + 1) * 6 * D].rearrange("p (k n) -> p k n", k=2) for n, L in enumerate("AB")}
        weights["D"] = sb("wqkvD", [HC, 2, 3 * D])
        wout = {L: sb(f"wout{L}", [HC, 2, D]) for L in "ABDS"}
        w1 = sb("w1", [HC, 2, HID])
        w2 = sb("w2", [P, MC, D])
        w2small = sb("w2small", [P, MC * sum(KEEP)])
        w2s = [w2small[:, MC * sum(KEEP[:i]):MC * sum(KEEP[:i + 1])].rearrange("p (m n) -> p m n", m=MC) for i in range(3)]
        mo_w1 = [w1, wab[:, 0:2 * HID].rearrange("p (k m) -> p k m", k=2)]
        mo_w2 = [w2, w2small[:, 0:MC * D].rearrange("p (m d) -> p m d", m=MC)]
        mo_b1 = [sb(f"mo_b1{u}", [P, MC]) for u in range(2)]
        slot1 = sb("slot1", [P, NE])
        prefix = sb("prefix", [P, P])
        steps = sb("steps", [P, T - 1])
        slots_u = sb("slots_u", [P, T, KSEL], U32)
        starts = sb("starts", [P, NE + 1], I32)
        counts = sb("counts", [P, NE], I32)
        number_u = sb("number_u", [P, 1], U32)
        wr = sb("wr", [HC, 2, G + NE])
        b2all = sb("b2all", [NE, D])

        h = sb("h", [P, T, D])
        z = sb("z", [P, T, D])
        xn = sb("xn", [P, T, D])
        V = sb("V", [P, T, D])
        xT = sb("xT", [HC, 2, TOK])
        osb = sb("osb", [P, 2, D])
        oT = sb("oT", [HC, 2, 2, P])
        stats = sb("stats", [P, T, 6])
        mv = sb("mv", [P, T, 2])
        rstd = sb("rstd", [P, T])
        numbers = sb("numbers", [P, T + 1])
        tokst = sb("tokst", [P, T, 4])
        tmpt = sb("tmpt", [P, 2, D])
        colsum = sb("colsum", [P, D])
        cbias = sb("cbias", [P, D])
        smx = sb("smx", [HC, 2, IB])
        ssum = sb("ssum", [HC, 2, IB])
        srec = sb("srec", [HC, 2, IB])

        arena = sb("arena", [P, 24320])
        at = [0]

        def view(parts, n):
            v = arena[0:parts, at[0]:at[0] + n]
            at[0] += n
            return v

        xf = view(FP, FC * TOK).rearrange("p (c t) -> p c t", c=FC)
        xsq = view(FP, FC * TOK).rearrange("p (c t) -> p c t", c=FC)
        w5 = view(FP, NSH * FC * D).rearrange("p (c v n) -> p c v n", c=FC, v=NSH)
        weff = V[0:FP, :, :]
        at[0] = 0
        qbd = [view(HC, IB * HC).rearrange("p (b h i) -> p b h i", b=IB, h=HH) for _ in range(4)]
        prob = view(HC, 2 * B * NTOK).rearrange("p (f n x) -> p f n x", f=2, n=2)
        ptbd = [view(P, H * P).rearrange("p (h b i) -> p h b i", h=H, b=TB) for _ in range(2)]
        qk = view(HC, 4 * TOK).rearrange("p (o n x) -> p o n x", o=4, n=2)
        at[0] = 0
        qkD = view(P, T * 2 * D).rearrange("p (t n) -> p t n", t=T)
        prodS = [view(P, H * H * HD) for _ in range(2)]
        prodV = [view(P, H * H * HD) for _ in range(2)]
        scD = [view(P, 2 * H * H) for _ in range(3)]
        mxD = [view(P, 2 * H) for _ in range(3)]
        peff = [view(P, H * H) for _ in range(2)]
        oD = [view(P, D) for _ in range(2)]
        at[0] = 0
        hT = [view(P, MC * HALF).rearrange("p (m t) -> p m t", m=MC) for _ in range(4)]
        at[0] = 0
        at[0] = 3072 + 4 * 2304 + 3 * 288 + 3 * 24 + 2 * 144 + 2 * 192
        cmpa = view(P, 4 * NE * E)
        cmpb = view(P, 4 * NE * E)
        gwork = view(P, 2 * 4 * (G + NE) + 4 * (1 + G))
        lgG = view(P, 4 * G).rearrange("p (r e) -> p r e", e=G)
        lgE = view(P, 4 * NE).rearrange("p (r e) -> p r e", e=E)
        sel = view(P, T * NE).rearrange("p (t e) -> p t e", t=T)
        earlier = view(P, (T + 1) * NE).rearrange("p (t e) -> p t e", t=T + 1)
        key = view(P, 4 * NE).rearrange("p (t e) -> p t e", t=4)
        top8 = view(P, T * KSEL).rearrange("p (t k) -> p t k", t=T)
        tiles_f = view(P, 3 * NE).rearrange("p (a e) -> p a e", a=3)
        tilecmp = view(P, NE * (T - 1)).rearrange("p (e k) -> p e k", e=NE)
        cT = view(NE, T * P).rearrange("p (t x) -> p t x", t=T)
        y = view(P, T * D).rearrange("p (t d) -> p t d", t=T)
        xrow = view(P, T * ROWN).rearrange("p (t n) -> p t n", t=T)
        padrow = view(P, ROWN)
        assert at[0] <= 24320
        at[0] = 0
        mo_hT = view(P, MC * P).rearrange("p (m t) -> p m t", m=MC)
        mo_x = view(P, ROWN)
        mo_xT = view(HC, 2 * P).rearrange("p (k t) -> p k t", k=2)
        mo_meta = view(P, 2 * META)
        mo_res = view(P, D)
        gparts = {}
        gat = 0
        for which, r_, n_ in (("G", 4, G), ("E", 4 * G, E)):
            for part, size in (("sel", r_ * n_), ("d", r_ * n_), ("mx", r_)):
                v = gwork[:, gat:gat + size]
                gparts[which, part] = v.rearrange("p (r e) -> p r e", e=n_) if part != "mx" else v
                gat += size

        def gview(which, part):
            return gparts[which, part]

        bank = [ctx.enter_context(nc.psum_tensor(f"bank{i}", [P, 512], F32)) for i in range(8)]
        full = [sem(f"bank{i}_full") for i in range(8)]
        free = [sem(f"bank{i}_free") for i in range(8)]

        uses, used = {}, [0] * 8

        def use(b, *key):
            uses[key] = (b, used[b])
            used[b] += 1

        def claim(*key):
            b, k = uses[key]
            if k:
                nc.tensor.wait_ge(free[b], k)
            return bank[b]

        def filled(eng, *key):
            b, k = uses[key]
            eng.wait_ge(full[b], k + 1)
            return bank[b]

        def was_read(eng, *key):
            b, k = uses[key]
            eng.wait_ge(free[b], k + 1)

        def full_of(*key):
            return full[uses[key][0]]

        def free_of(*key):
            return free[uses[key][0]]

        def plan_transposes(L):
            for n in range(2):
                for k in range(2):
                    use(2 + k, L, "xT", n, k)

        def plan_attention(L):
            for n in range(2):
                for o in range(4):
                    use(4 + o % 2, L, "qk", n, o)
            for t in range(T):
                use(t % 2, L, "V", t)
            for n in range(2):
                for f in range(2):
                    use(6 + f, L, "score", n, f)
            for t in range(T + 3):
                if t < T:
                    use(2 + t % 2, L, "PT", t)
                if 0 <= t - 1 < T:
                    use((t - 1) % 2, L, "AV", t - 1)
                if 0 <= t - 2 < T:
                    use(4 + t % 2, L, "oT", t - 2)
                if 0 <= t - 3 < T:
                    use(6 + (t - 3) % 2, L, "proj", t - 3)

        for t in range(T // 2):
            use(t, "tok", t)
        use(5, "cbias")
        use(4, "colsum")
        for t in range(T // 2, T):
            use(t % 4, "tok", t)
        for L in "AB":
            plan_transposes(L)
            plan_attention(L)
        plan_transposes("M")
        for m in range(MC):
            use(2 + m, "fc1", 3, m)
        for i in (2, 1, 0):
            for m in range(MC):
                use(2 + m, "fc1", i, m)
        for t in range(T):
            use(t % 2, "fc2", t)
        plan_transposes("D")
        for t in range(T):
            use(4 + t % 2, "D", "qk", t)
            use(t % 2, "D", "V", t)
        for t in range(T + 1):
            if t < T:
                use(2 + t % 2, "D", "oT", t)
            if t >= 1:
                use(6 + t % 2, "D", "proj", t - 1)
            for g, (t0, t1) in enumerate(GROUPS):
                if t != t1:
                    continue
                for q in range(t0, t1):
                    use(4 + q % 2, "R", "xT", q)
                for q in range(t0, t1):
                    use(q % 2, "logit", q)
                use(4, "place", g)
                for q in range(t0, t1):
                    use(q % 2, "cT", q)
                    use(5, "y0", q)
        use(4, "counts")
        moe_base = list(used)

        lots = {}

        def load(eng, lot, dst, src):
            lots[lot] = lots.get(lot, 0) + 16
            eng.dma_start(dst, src).then_inc(sem(f"in_{lot}"), 16)

        LOT = {"const": 16 * 12, "A": 16 * 2, "B": 16 * 2, "D": 16 * 2, "mlp": 16 * 2, "small": 16 * 7,
               "route": 16 * 2}

        def loaded(eng, lot):
            eng.wait_ge(sem(f"in_{lot}"), LOT[lot])

        halves = "(k p) n -> p k n"
        MAXT = KSEL * T + NE
        ACC0 = 16

        def load_expert(eng, u, e):
            one = bass.ds(e, 1)
            eng.dma_start(mo_w1[u][:], a["moe_w1"][one].rearrange("o (k p) n -> p (o k) n", p=HC)).then_inc(sem(f"in_expert{u}"), 16)
            eng.dma_start(mo_w2[u][:], a["moe_w2"][one].rearrange("o (m p) n -> p (o m) n", p=P)).then_inc(sem(f"in_expert{u}"), 16)
            eng.dma_start(mo_b1[u][:], a["moe_b1"][one].rearrange("o p m -> p (o m)")).then_inc(sem(f"in_expert{u}"), 16)

        block = ctx.enter_context(nc.Block())

        @block.sync
        def _(sp):
            load(sp, "const", gamma5[:], a["gamma5"])
            for c in range(FC):
                sp.dma_start(w5[:, c], a["w5"][c]).then_inc(sem(f"in_pixels{c}"), 16)
                sp.dma_start(xf[:, c], a["xf"][c]).then_inc(sem(f"in_pixels{c}"), 16)
                if c == 0:
                    load(sp, "const", beta5[:], a["beta5"])
                    load(sp, "const", cnt[:], a["cnt"])
                    load(sp, "const", ident[:], a["ident"])
                    load(sp, "const", blockmask[:], a["blockmask"])
                    load(sp, "const", headmask[:], a["headmask"])
                    load(sp, "const", selfmask[:], a["selfmask"])
                    load(sp, "const", tri[:], a["tri"])
                    load(sp, "const", slot1[:], a["slot1"])
                    load(sp, "const", prefix[:], a["prefix"])
                    load(sp, "const", steps[:], a["steps"])
                    load(sp, "const", numbers[:], a["numbers"])
                    load(sp, "small", rows_sb[:], a["rows"])
                    load(sp, "small", cols_sb[:], a["cols"])
            load(sp, "A", weights["A"][:], a["wqkvA"].rearrange(halves, p=HC))
            load(sp, "A", wout["A"][:], a["woutA"].rearrange(halves, p=HC))
            load(sp, "small", gum[:, 0:3], a["gum"].broadcast_to([P, 3]))
            load(sp, "small", lamv[:], a["lamv"].broadcast_to([P, 4, 8]))
            load(sp, "small", b1_sb[:], a["b1"])
            load(sp, "small", b2all[:], a["moe_b2"])
            load(sp, "small", wr[:], a["wr"].rearrange(halves, p=HC))
            for L in "BD":
                load(sp, L, weights[L][:], a[f"wqkv{L}"].rearrange(halves, p=HC))
                load(sp, L, wout[L][:], a[f"wout{L}"].rearrange(halves, p=HC))
            load(sp, "mlp", w1[:], a["w1"].rearrange(halves, p=HC))
            load(sp, "mlp", w2[:], a["w2"].rearrange("(m p) n -> p m n", p=P))
            was_read(sp, "fc2", T - 1)
            for u in range(2):
                load_expert(sp, u, u)
            for t in range(T):
                was_read(sp, "y0", t)
                sp.dma_start(summed[t * P:(t + 1) * P, :], y[:, t, :]).then_inc(sem("sums_begun"), 16)
            sp.wait_ge(sem("table_ready"), 1)
            sp.dma_start(summed[TOK:TOK + P, :], padrow[:, 0:D]).then_inc(sem("sums_begun"), 16)
            with sp.Fori(0, NE) as e:
                n = sp.value_load(counts[0:1, bass.ds(e, 1)], min_val=0, max_val=TOK)
                sp.dma_start(dispatch[bass.ds(e * SLOTS + n, P), :], padrow).then_inc(sem("padded"), 16)
            sp.wait_ge(sem("padded"), 16 * NE)
            sp.wait_ge(sem("dispatched"), 16 * KSEL * T)
            with sp.Fori(0, NE) as e:
                first = sp.value_load(starts[0:1, bass.ds(e, 1)], min_val=0, max_val=MAXT - 1)
                end = sp.value_load(starts[0:1, bass.ds(e + 1, 1)], min_val=1, max_val=MAXT)
                with sp.Fori(first, end) as i:
                    at_row = sp.snap(nc.s_assert_within(e * SLOTS + (i - first) * P, 0, NE * SLOTS - P))
                    sp.wait_ge(sem("rows_free"), i + 1)
                    sp.dma_start(mo_x, dispatch[bass.ds(at_row, P), :]).then_inc(sem("rows_in"), 16)
            total = sp.value_load(starts[0:1, NE:NE + 1], min_val=1, max_val=MAXT)
            sp.wait_ge(sem("rows_free"), total + 1)
            sp.dma_start(mo_x, dispatch[0:P, :]).then_inc(sem("rows_in"), 16)
            sp.wait_ge(sem("accumulated"), total * 16 + ACC0)
            sp.dma_start(out[:, :], summed[0:TOK, :]).then_inc(sem("out_stored"), 16)
            sp.wait_ge(sem("out_stored"), 16)

        ROW = {"tokb": 0, "bqkvA": D, "boutA": 4 * D, "boutB": 5 * D, "b2": 6 * D, "route": 7 * D,
               "boutS": 7 * D + 64, "b2S": 8 * D + 64}
        COL = {"bqkA": 0, "n1l": 4, "n1s": 8, "n2l": 12, "n2s": 16, "scaleA": 20}

        def row(name, n=D):
            return rows_sb[0:1, ROW[name]:ROW[name] + n]

        @block.gpsimd
        def _(pool):
            step = [0]

            def link(ins):
                step[0] += 1
                ins.then_inc(sem("pool_step"), 1)
                pool.wait_ge(sem("pool_step"), step[0])

            nc.gpsimd.memset(ones[:], 1.0).then_inc(sem("ones_set"), 1)
            nc.gpsimd.memset(minus_half[:], -0.5).then_inc(sem("ones_set"), 1)
            pool.wait_ge(sem("ones_set"), 2)

            for n in range(2):
                s = slice(4 * n, 4 * n + 4)
                pool.wait_ge(sem("tokvar"), n + 1)
                nc.gpsimd.tensor_tensor(out=tokst[:, s, 3:4].rearrange("p t o -> p (t o)"), in0=tokst[:, s, 2:3].rearrange("p t o -> p (t o)"), in1=minus_half[:, s],
                                        op=ALU.pow).then_inc(sem("tokrstd"), 1)
            if True:
                loaded(pool, "small")
                loaded(pool, "B")
                loaded(pool, "mlp")
                link(nc.gpsimd.tensor_tensor(out=gum[:, 3:4], in0=gum[:, 0:1], in1=gum[:, 1:2], op=ALU.add))
                link(nc.gpsimd.tensor_tensor(out=gum[:, 4:5], in0=gum[:, 3:4], in1=gum[:, 2:3], op=ALU.add))

                def times(dst, src, g, p0, p1):
                    link(nc.gpsimd.tensor_scalar(out=dst, in0=src, scalar1=gum[p0:p1, g:g + 1], scalar2=None, op0=ALU.mult))

                for p0, p1, k, c0, c1, g in ((0, KEEP[2], 0, 0, KEEP[2], 4), (KEEP[2], HC, 0, 0, KEEP[2], 3),
                                             (0, HC, 0, KEEP[2], KEEP[1], 3), (0, HC, 0, KEEP[1], D, 0),
                                             (0, HC, 1, 0, D, 0)):
                    times(wout["S"][p0:p1, k, c0:c1], wout["B"][p0:p1, k, c0:c1], g, p0, p1)
                for dst, src in (("boutS", "boutB"), ("b2S", "b2")):
                    for c0, c1, g in ((0, KEEP[2], 4), (KEEP[2], KEEP[1], 3), (KEEP[1], D, 0)):
                        times(rows_sb[0:1, ROW[dst] + c0:ROW[dst] + c1], rows_sb[0:1, ROW[src] + c0:ROW[src] + c1], g, 0, 1)
                for i in range(3):
                    nc.gpsimd.tensor_scalar(out=w2s[i][:], in0=w2[:, :, 0:KEEP[i]], scalar1=gum[:, i:i + 1], scalar2=None, op0=ALU.mult).then_inc(sem("small_weights"), 1)

            ln = [0]

            def ln_rstd(t0, t1):
                s = slice(t0, t1)
                ln[0] += 1
                pool.wait_ge(sem("ln_stats"), ln[0])
                link(nc.gpsimd.tensor_scalar(out=rstd[:, s], in0=mv[:, s, 1:2].rearrange("p t o -> p (t o)"), scalar1=EPS_LN, scalar2=None, op0=ALU.add))
                nc.gpsimd.tensor_tensor(out=rstd[:, s], in0=rstd[:, s], in1=minus_half[:, s], op=ALU.pow).then_inc(sem("ln_rstd"), 1)

            for _ in range(5):
                ln_rstd(0, 4)
                ln_rstd(4, 8)
            link(nc.gpsimd.memset(padrow, 0.0))
            nc.gpsimd.tensor_copy(padrow[:, D:D + 1], numbers[:, T:T + 1]).then_inc(sem("pad_ready"), 1)
            nc.gpsimd.tensor_copy(xrow[:, :, D:D + 1], numbers[:, 0:T].unsqueeze(2)).then_inc(sem("pad_ready"), 1)
            for t in range(T):
                pool.wait_ge(sem("D_probs"), t + 1)
                was_read(pool, "D", "V", t)
                if t >= 2:
                    pool.wait_ge(sem("D_rows"), t - 1)
                p = peff[t % 2].rearrange("p (a b) -> p a b", a=H)
                v = V[:, t, :].rearrange("p (b x) -> p x b", x=HD)
                nc.gpsimd.tensor_tensor(out=prodV[t % 2].rearrange("p (a x b) -> p a x b", a=H, x=HD), in0=repeat(p, 2, HD), in1=repeat(v, 1, H), op=ALU.mult).then_inc(sem("D_weighed"), 1)
            pool.wait_ge(sem("pad_ready"), 2)
            for g, (t0, t1) in enumerate(GROUPS):
                ln_rstd(t0, t1)
                pool.wait_ge(sem("slots_ready"), g + 1)
                for t in range(t0, t1):
                    for k in range(KSEL):
                        pool.indirect_dma_start(out=dispatch, out_offset=bass.IndirectOffsetOnAxis(ap=slots_u[:, t, k:k + 1], axis=0),
                                                in_=xrow[:, t, :], in_offset=None).then_inc(sem("dispatched"), 16)
            pool.wait_ge(sem("table_ready"), 1)
            total = pool.value_load(starts[0:1, NE:NE + 1], min_val=1, max_val=MAXT)
            link(nc.gpsimd.tensor_copy(number_u[:], numbers[:, T:T + 1]))
            pool.wait_ge(sem("sums_begun"), 16 * (T + 1))
            pool.indirect_dma_start(out=summed, out_offset=bass.IndirectOffsetOnAxis(ap=number_u[:, 0:1], axis=0),
                                    in_=padrow[:, 0:D], in_offset=None, compute_op=ALU.add).then_inc(sem("accumulated"), 16)
            with pool.Fori(0, total) as i:
                pool.wait_ge(free[0], i + (moe_base[0] + 1))
                pool.sem_inc(sem("adding"), 1)
                pool.indirect_dma_start(out=summed, out_offset=bass.IndirectOffsetOnAxis(ap=number_u[:, 0:1], axis=0),
                                        in_=mo_res, in_offset=None, compute_op=ALU.add).then_inc(sem("accumulated"), 16)

        @block.scalar
        def _(act):
            for c in range(FC):
                act.wait_ge(sem(f"in_pixels{c}"), 32)
                nc.scalar.activation(xsq[:, c], xf[:, c], ACT.Square).then_inc(sem("squares"), 1)

            def transposed(L, affine):
                for n in range(2):
                    for k in range(2):
                        ps = filled(act, L, "xT", n, k)
                        dst = xT[:, k, n * HALF:(n + 1) * HALF]
                        if affine:
                            c = affine[n] + k
                            ins = nc.scalar.activation(dst, ps[0:HC, :], ACT.Identity, scale=cols_sb[:, c:c + 1], bias=cols_sb[:, c + 2:c + 3])
                        else:
                            ins = nc.scalar.activation(dst, ps[0:HC, :], ACT.Copy)
                        ins.then_inc(free_of(L, "xT", n, k), 1)

            def route(g, t0, t1):
                for t in range(t0, t1):
                    ps = filled(act, "R", "xT", t)
                    nc.scalar.activation(xT[:, :, t * P:(t + 1) * P], ps[0:HC, 0:2 * P].rearrange("p (k x) -> p k x", k=2), ACT.Copy).then_inc(free_of("R", "xT", t), 1)
                act.wait_ge(sem("gate_shifted"), 2 * g + 1)
                nc.scalar.activation(gview("G", "d"), gview("G", "d"), ACT.Exp).then_inc(sem("gate_exp"), 1)
                act.wait_ge(sem("gate_shifted"), 2 * g + 2)
                nc.scalar.activation(gview("E", "d"), gview("E", "d"), ACT.Exp).then_inc(sem("gate_exp"), 1)

            def attention(L):
                for n in range(2):
                    for o in range(4):
                        ps = filled(act, L, "qk", n, o)
                        if L == "A":
                            ins = nc.scalar.activation(qk[:, o, n, :], ps[0:HC, :], ACT.Identity, bias=cols_sb[:, COL["bqkA"] + o:COL["bqkA"] + o + 1])
                        else:
                            ins = nc.scalar.activation(qk[:, o, n, :], ps[0:HC, :], ACT.Copy)
                        ins.then_inc(free_of(L, "qk", n, o), 1)
                for t in range(T):
                    ps = filled(act, L, "V", t)
                    nc.scalar.activation(V[:, t, :], ps[:, 0:D], ACT.Copy).then_inc(free_of(L, "V", t), 1)
                u = 0
                for n in range(2):
                    for f in range(2):
                        u += 1
                        if L == "A":
                            act.wait_ge(sem("A_shifted"), u)
                        else:
                            was_read(act, L, "score", n, f)
                        p = prob[:, f, n, :]
                        nc.scalar.activation(p, p, ACT.Exp, scale={"A": 1.0, "B": HD ** -0.5}[L]).then_inc(sem(f"{L}_exp"), 1)
                for t in range(T + 2):
                    if 0 <= t - 1 < T:
                        ps = filled(act, L, "AV", t - 1)
                        if t - 1 >= 2:
                            act.wait_ge(full_of(L, "oT", t - 3), uses[L, "oT", t - 3][1] + 1)
                        nc.scalar.activation(osb[:, (t - 1) % 2, :], ps[:, 0:D], ACT.Copy).then_inc(free_of(L, "AV", t - 1), 1)
                    if 0 <= t - 2 < T:
                        ps = filled(act, L, "oT", t - 2)
                        if t - 2 >= 2:
                            act.wait_ge(full_of(L, "proj", t - 4), uses[L, "proj", t - 4][1] + 1)
                        nc.scalar.activation(oT[:, t % 2, :, :].rearrange("p k x -> p (k x)"), ps[0:HC, 0:2 * P], ACT.Copy).then_inc(free_of(L, "oT", t - 2), 1)

            loaded(act, "small")
            transposed("A", None)
            attention("A")
            transposed("B", (COL["n1l"], COL["n1s"]))
            attention("B")
            transposed("M", (COL["n2l"], COL["n2s"]))
            for i in (3, 2, 1, 0):
                for m in range(MC):
                    ps = filled(act, "fc1", i, m)
                    nc.scalar.activation(hT[i][:, m, :], ps[:, :], ACT.Gelu, bias=b1_sb[:, m:m + 1]).then_inc(free_of("fc1", i, m), 1)
            act.wait_ge(sem("lam_sums"), 1)
            nc.scalar.activation(lam[:, 2:4], lam[:, 0:2], ACT.Exp).then_inc(sem("lam_exp"), 1)
            transposed("D", None)
            for t in range(T):
                ps = filled(act, "D", "qk", t)
                nc.scalar.activation(qkD[:, t, :], ps[:, 0:2 * D], ACT.Copy).then_inc(free_of("D", "qk", t), 1)
                ps = filled(act, "D", "V", t)
                nc.scalar.activation(V[:, t, :], ps[:, 0:D], ACT.Copy).then_inc(free_of("D", "V", t), 1)
            for t in range(T + 3):
                if t < T:
                    act.wait_ge(sem("D_shifted"), t + 1)
                    nc.scalar.activation(scD[t % 3], scD[t % 3], ACT.Exp, scale=(HD // 2) ** -0.5).then_inc(sem("D_exp"), 1)
                if t >= 3:
                    q = t - 3
                    ps = filled(act, "D", "oT", q)
                    if q >= 2:
                        act.wait_ge(full_of("D", "proj", q - 2), uses["D", "proj", q - 2][1] + 1)
                    nc.scalar.activation(oT[:, q % 2, :, :].rearrange("p k x -> p (k x)"), ps[0:HC, 0:2 * P], ACT.Copy).then_inc(free_of("D", "oT", q), 1)
                for g, (t0, t1) in enumerate(GROUPS):
                    if t == min(t1 + 3, T + 2):
                        route(g, t0, t1)
            act.wait_ge(sem("table_ready"), 1)

            def expert(u, e, reload):
                loads = act.snap((e - u) * 24 + 48)
                act.wait_ge(sem("table_ready"), 1)
                act.wait_ge(sem(f"in_expert{u}"), loads)
                first = act.value_load(starts[0:1, bass.ds(e, 1)], min_val=0, max_val=MAXT - 1)
                end = act.value_load(starts[0:1, bass.ds(e + 1, 1)], min_val=1, max_val=MAXT)
                with act.Fori(first, end) as i:
                    act.wait_ge(full[0], i + moe_base[0])
                    for m in range(MC):
                        act.wait_ge(full[2 + m], i + (moe_base[2 + m] + 1))
                        nc.scalar.activation(mo_hT[:, m, :], bank[2 + m][:, 0:P], ACT.Gelu, bias=mo_b1[u][:, m:m + 1]).then_inc(free[2 + m], 1)
                if reload:
                    act.wait_ge(full[0], end + moe_base[0])
                    load_expert(act, u, e + 2)

            with act.Fori(0, NE // 2 - 1) as pair:
                for u in range(2):
                    expert(u, pair * 2 + u, True)
            for u in range(2):
                expert(u, NE - 2 + u, False)

        @block.vector
        def _(dve):
            step = [0]

            def link(ins):
                step[0] += 1
                ins.then_inc(sem("dve_step"), 1)
                dve.wait_ge(sem("dve_step"), step[0])

            tt, ts, stt = nc.vector.tensor_tensor, nc.vector.tensor_scalar, nc.vector.scalar_tensor_tensor
            loaded(dve, "const")
            for c in range(FC):
                dve.wait_ge(sem(f"in_pixels{c}"), 32)
                link(ts(out=weff[:, c, :], in0=w5[:, c, 0, :], scalar1=gamma5[:, 0, c:c + 1], scalar2=None, op0=ALU.mult))
                for v in range(1, NSH):
                    ins = stt(out=weff[:, c, :], in0=w5[:, c, v, :], scalar=gamma5[:, v, c:c + 1], in1=weff[:, c, :], op0=ALU.mult, op1=ALU.add)
                    if v < NSH - 1:
                        link(ins)
                ins.then_inc(sem("weff"), 1)
            ps = filled(dve, "cbias")
            nc.vector.tensor_copy(cbias[:], ps[:, 0:D]).then_inc(free_of("cbias"), 1)
            ps = filled(dve, "colsum")
            nc.vector.tensor_copy(colsum[:], ps[:, 0:D]).then_inc(free_of("colsum"), 1)
            was_read(dve, "cbias")
            was_read(dve, "colsum")
            for n in range(2):
                s = slice(4 * n, 4 * n + 4)
                for t in range(4 * n, 4 * n + 4):
                    ps = filled(dve, "tok", t)
                    link(nc.vector.tensor_copy(tokst[:, t, 0:2], ps[:, D:D + 2]))
                    link(stt(out=tokst[:, t, 2:3], in0=tokst[:, t, 0:1], scalar=tokst[:, t, 0:1], in1=tokst[:, t, 1:2], op0=ALU.mult, op1=ALU.subtract))
                ts(out=tokst[:, s, 2:3].rearrange("p t o -> p (t o)"), in0=tokst[:, s, 2:3].rearrange("p t o -> p (t o)"), scalar1=-1.0, scalar2=EPS_LN,
                   op0=ALU.mult, op1=ALU.add).then_inc(sem("tokvar"), 1)
                dve.wait_ge(sem("tokrstd"), n + 1)
                link(ts(out=tokst[:, s, 3:4].rearrange("p t o -> p (t o)"), in0=tokst[:, s, 3:4].rearrange("p t o -> p (t o)"), scalar1=-1.0, scalar2=None, op0=ALU.mult))
                for t in range(4 * n, 4 * n + 4):
                    ps = bank[uses["tok", t][0]]
                    stt(out=tmpt[:, t % 2, :], in0=colsum[:], scalar=tokst[:, t, 0:1], in1=ps[:, 0:D], op0=ALU.mult, op1=ALU.subtract).then_inc(free_of("tok", t), 1)
                    was_read(dve, "tok", t)
                    link(stt(out=h[:, t, :], in0=tmpt[:, t % 2, :], scalar=tokst[:, t, 3:4], in1=cbias[:], op0=ALU.mult, op1=ALU.add))

            ln = [0]

            def layernorm(src, dst, name, ready=None):
                for n in range(2):
                    for t in range(4 * n, 4 * n + 4):
                        if ready:
                            ready(t)
                        link(nc.vector.bn_stats(out=stats[:, t, :], in_=src[:, t, :]))
                    for t in range(4 * n, 4 * n + 4):
                        ins = nc.vector.bn_aggr(out=mv[:, t, :], in_=stats[:, t, :])
                        if t < 4 * n + 3:
                            link(ins)
                        else:
                            ins.then_inc(sem("ln_stats"), 1)
                for n in range(2):
                    ln[0] += 1
                    dve.wait_ge(sem("ln_rstd"), ln[0])
                    for t in range(4 * n, 4 * n + 4):
                        ts(out=dst[:, t, :], in0=src[:, t, :], scalar1=mv[:, t, 0:1], scalar2=rstd[:, t:t + 1],
                           op0=ALU.subtract, op1=ALU.mult).then_inc(sem(f"normed_{name}"), 1)

            def attention(L, residual, dst):
                units = [(n, f) for n in range(2) for f in range(2)]

                def spread(n, f):
                    was_read(dve, L, "qk", n, f)
                    for hh in range(HH):
                        ins = ts(out=qbd[2 * n + f][:, :, hh, :], in0=qk[:, f, n, :].rearrange("p (b i) -> p b i", i=NTOK),
                                 scalar1=headmask[:, hh:hh + 1], scalar2=None, op0=ALU.mult)
                    ins.then_inc(sem(f"{L}_spread"), 1)

                def softmax_front(n, f, u):
                    ps = filled(dve, L, "score", n, f)
                    sc = ps[0:HC, :].rearrange("p (b j) -> p b j", j=NTOK)
                    p = prob[:, f, n, :].rearrange("p (b j) -> p b j", j=NTOK)
                    if L == "A":
                        stt(out=p, in0=sc, scalar=cols_sb[:, COL["scaleA"] + f:COL["scaleA"] + f + 1], in1=repeat(selfmask[:], 1, IB), op0=ALU.mult, op1=ALU.add).then_inc(free_of(L, "score", n, f), 1)
                        was_read(dve, L, "score", n, f)
                        sc = p
                    link(nc.vector.reduce_max(smx[:, u % 2, :], sc, AX_X))
                    tt(out=p, in0=sc, in1=repeat(smx[:, u % 2, :], 2, NTOK), op=ALU.subtract).then_inc(sem("A_shifted") if L == "A" else free_of(L, "score", n, f), 1)

                def softmax_back(n, f, u):
                    p = prob[:, f, n, :].rearrange("p (b j) -> p b j", j=NTOK)
                    dve.wait_ge(sem(f"{L}_exp"), u + 1)
                    link(nc.vector.reduce_sum(ssum[:, u % 2, :], p, AX_X))
                    link(nc.vector.reciprocal(srec[:, u % 2, :], ssum[:, u % 2, :]))
                    tt(out=p, in0=p, in1=repeat(srec[:, u % 2, :], 2, NTOK), op=ALU.mult).then_inc(sem(f"{L}_probs"), 1)

                for k in range(4 + 4):
                    if k < 4:
                        spread(*units[k])
                    if 0 <= k - 2 < 4:
                        softmax_front(*units[k - 2], k - 2)
                    if 0 <= k - 4 < 4:
                        softmax_back(*units[k - 4], k - 4)
                for t in range(T + 3):
                    if t < T:
                        ps = filled(dve, L, "PT", t)
                        if t >= 2:
                            dve.wait_ge(full_of(L, "AV", t - 2), uses[L, "AV", t - 2][1] + 1)
                        src = ps[:, 0:D].rearrange("p (h i) -> p h i", i=NTOK)
                        tt(out=ptbd[t % 2], in0=repeat(src, 2, TB),
                           in1=repeat(repeat(blockmask[:], 1, H), 3, NTOK), op=ALU.mult).then_inc(free_of(L, "PT", t), 1)
                    if t >= 3:
                        ps = filled(dve, L, "proj", t - 3)
                        tt(out=dst[:, t - 3, :], in0=ps[:, 0:D], in1=residual[:, t - 3, :], op=ALU.add).then_inc(free_of(L, "proj", t - 3), 1)

            layernorm(h, xn, "A")
            loaded(dve, "small")
            attention("A", h, h)
            layernorm(h, z, "z", lambda t: was_read(dve, "A", "proj", t))
            layernorm(z, xn, "B", lambda t: dve.wait_ge(sem("normed_z"), t + 1))
            attention("B", z, z)
            layernorm(z, xn, "M", lambda t: was_read(dve, "B", "proj", t))
            for t in range(T):
                ps = filled(dve, "fc2", t)
                tt(out=z[:, t, :], in0=ps[:, 0:D], in1=z[:, t, :], op=ALU.add).then_inc(free_of("fc2", t), 1)
                was_read(dve, "fc2", t)
                link(tt(out=h[:, t, :], in0=z[:, t, :], in1=h[:, t, :], op=ALU.add))
            loaded(dve, "small")
            for s in range(2):
                link(tt(out=lamv[:, 2 * s, :], in0=lamv[:, 2 * s, :], in1=lamv[:, 2 * s + 1, :], op=ALU.mult))
                ins = nc.vector.reduce_sum(lam[:, s:s + 1], lamv[:, 2 * s, :], AX_X)
                if s == 0:
                    link(ins)
                else:
                    ins.then_inc(sem("lam_sums"), 1)
            dve.wait_ge(sem("lam_exp"), 1)
            link(tt(out=lam[:, 4:5], in0=lam[:, 3:4], in1=lam[:, 2:3], op=ALU.subtract))
            link(ts(out=lam[:, 5:6], in0=lam[:, 4:5], scalar1=LAMBDA_INIT, scalar2=None, op0=ALU.subtract))
            link(ts(out=lam[:, 7:8], in0=lam[:, 5:6], scalar1=1.0 - LAMBDA_INIT, scalar2=None, op0=ALU.mult))
            link(nc.vector.memset(headfac[:], 1.0))
            link(ts(out=headfac[:, 1, :], in0=headfac[:, 1, :], scalar1=lam[:, 7:8], scalar2=None, op0=ALU.mult))
            link(ts(out=headfac[:, 0, :], in0=headfac[:, 0, :], scalar1=1.0 - LAMBDA_INIT, scalar2=None, op0=ALU.mult))
            layernorm(h, xn, "D")
            def top_gates(which, lg, R, n, k, order):
                a4 = cmpa[:, 0:R * n * n].rearrange("p (r a b) -> p r a b", a=n, b=n)
                b4 = cmpb[:, 0:R * n * n].rearrange("p (r a b) -> p r a b", a=n, b=n)
                other, own = repeat(lg, 2, n), repeat(lg, 3, n)
                link(tt(out=a4, in0=other, in1=own, op=ALU.is_gt))
                link(tt(out=b4, in0=other, in1=own, op=ALU.is_equal))
                low = tri[:].rearrange("p (a b) -> p a b", b=E)[:, 0:n, 0:n]
                link(tt(out=b4, in0=b4, in1=repeat(low, 1, R), op=ALU.mult))
                link(tt(out=a4, in0=a4, in1=b4, op=ALU.add))
                chosen, d, mx = gview(which, "sel"), gview(which, "d"), gview(which, "mx")
                link(nc.vector.reduce_sum(chosen, a4, AX_X))
                link(ts(out=chosen, in0=chosen, scalar1=float(k), scalar2=None, op0=ALU.is_lt))
                link(nc.vector.reduce_max(mx, lg, AX_X))
                tt(out=d, in0=lg, in1=repeat(mx, 2, n), op=ALU.subtract).then_inc(sem("gate_shifted"), 1)
                dve.wait_ge(sem("gate_exp"), order)
                link(tt(out=d, in0=d, in1=chosen, op=ALU.mult))
                link(nc.vector.reduce_sum(mx, d, AX_X))
                link(nc.vector.reciprocal(mx, mx))
                link(tt(out=d, in0=d, in1=repeat(mx, 2, n), op=ALU.mult))
                link(stt(out=d, in0=d, scalar=EPS_GATE, in1=d, op0=ALU.is_ge, op1=ALU.mult))

            def route(g, t0, t1):
                R = t1 - t0
                if g == 0:
                    link(nc.vector.memset(earlier[:, 0, :], 0.0))
                for t in range(t0, t1):
                    was_read(dve, "D", "proj", t)
                    link(nc.vector.bn_stats(out=stats[:, t, :], in_=h[:, t, :]))
                for t in range(t0, t1):
                    ins = nc.vector.bn_aggr(out=mv[:, t, :], in_=stats[:, t, :])
                    if t < t1 - 1:
                        link(ins)
                ins.then_inc(sem("ln_stats"), 1)
                ln[0] += 1
                dve.wait_ge(sem("ln_rstd"), ln[0])
                for t in range(t0, t1):
                    ts(out=xrow[:, t, 0:D], in0=h[:, t, :], scalar1=mv[:, t, 0:1], scalar2=rstd[:, t:t + 1],
                       op0=ALU.subtract, op1=ALU.mult).then_inc(sem("normed_R"), 1)
                for t in range(t0, t1):
                    ps = filled(dve, "logit", t)
                    nc.vector.tensor_copy(lgG[:, t - t0, :], ps[:, 0:G])
                    nc.vector.tensor_copy(lgE[:, (t - t0) * G:(t - t0 + 1) * G, :], ps[:, G:G + NE].rearrange("p (g e) -> p g e", g=G)).then_inc(free_of("logit", t), 1)
                was_read(dve, "logit", t1 - 2)
                was_read(dve, "logit", t1 - 1)
                top_gates("G", lgG, R, G, KG, 2 * g + 1)
                top_gates("E", lgE, R * G, E, KE, 2 * g + 2)
                for name, dst in (("sel", sel[:, t0:t1, :]), ("d", xrow[:, t0:t1, D + 1:ROWN])):
                    for q in range(R):
                        ins = tt(out=dst[:, q, :].rearrange("p (g e) -> p g e", g=G), in0=gview("E", name)[:, q * G:(q + 1) * G, :],
                                 in1=repeat(gview("G", name)[:, q, :], 2, E), op=ALU.mult)
                    link(ins)
                for t in range(t0, t1):
                    ins = tt(out=earlier[:, t + 1, :], in0=earlier[:, t, :], in1=sel[:, t, :], op=ALU.add)
                    if t < t1 - 1:
                        link(ins)
                ins.then_inc(sem("chosen"), 1)
                ps = filled(dve, "place", g)
                place = ps[:, 0:R * NE].rearrange("p (t e) -> p t e", t=R)
                tt(out=key[:, 0:R, :], in0=place, in1=repeat(slot1[:], 1, R), op=ALU.add).then_inc(free_of("place", g), 1)
                was_read(dve, "place", g)
                link(tt(out=key[:, 0:R, :], in0=key[:, 0:R, :], in1=sel[:, t0:t1, :], op=ALU.mult))
                for t in range(t0, t1):
                    ins = nc.vector.max(out=top8[:, t, :], in_=key[:, t - t0, :])
                link(ins)
                ts(out=slots_u[:, t0:t1, :], in0=top8[:, t0:t1, :], scalar1=1.0, scalar2=None, op0=ALU.subtract).then_inc(sem("slots_ready"), 1)
                for t in range(t0, t1):
                    ps = filled(dve, "cT", t)
                    nc.vector.tensor_copy(cT[:, t, :], ps[0:NE, 0:P]).then_inc(free_of("cT", t), 1)
                    ps = filled(dve, "y0", t)
                    tt(out=y[:, t, :], in0=ps[:, 0:D], in1=h[:, t, :], op=ALU.add).then_inc(free_of("y0", t), 1)

            for t in range(T + 5):
                if t < T:
                    was_read(dve, "D", "qk", t)
                    q = qkD[:, t, 0:D].rearrange("p (h x) -> p h x", h=H)
                    k = qkD[:, t, D:2 * D].rearrange("p (h x) -> p h x", h=H)
                    pr = prodS[t % 2].rearrange("p (a b x) -> p a b x", a=H, b=H)
                    link(tt(out=pr, in0=repeat(q, 2, H), in1=repeat(k, 1, H), op=ALU.mult))
                    sc, mx = scD[t % 3], mxD[t % 3]
                    link(nc.vector.reduce_sum(sc.rearrange("p (s y) -> p y s", s=2), prodS[t % 2].rearrange("p (y s x) -> p y s x", s=2, x=HD // 2), AX_X))
                    sc3 = sc.rearrange("p (s x) -> p s x", x=H)
                    link(nc.vector.reduce_max(mx, sc3, AX_X))
                    tt(out=sc3, in0=sc3, in1=repeat(mx, 2, H), op=ALU.subtract).then_inc(sem("D_shifted"), 1)
                if 0 <= t - 1 < T:
                    q = t - 1
                    sc, mx = scD[q % 3], mxD[q % 3]
                    sc3 = sc.rearrange("p (s x) -> p s x", x=H)
                    dve.wait_ge(sem("D_exp"), q + 1)
                    link(nc.vector.reduce_sum(mx, sc3, AX_X))
                    link(nc.vector.reciprocal(mx, mx))
                    link(tt(out=mx, in0=mx, in1=headfac[:].rearrange("p s h -> p (s h)"), op=ALU.mult))
                    link(tt(out=sc3, in0=sc3, in1=repeat(mx, 2, H), op=ALU.mult))
                    if q >= 2:
                        dve.wait_ge(sem("D_weighed"), q - 1)
                    tt(out=peff[q % 2], in0=sc[:, 0:H * H], in1=sc[:, H * H:2 * H * H], op=ALU.add).then_inc(sem("D_probs"), 1)
                if 0 <= t - 3 < T:
                    q = t - 3
                    dve.wait_ge(sem("D_weighed"), q + 1)
                    if q >= 2:
                        dve.wait_ge(full_of("D", "oT", q - 2), uses["D", "oT", q - 2][1] + 1)
                    nc.vector.reduce_sum(oD[q % 2], prodV[q % 2].rearrange("p (y x) -> p y x", x=H), AX_X).then_inc(sem("D_rows"), 1)
                if t >= 5:
                    q = t - 5
                    ps = filled(dve, "D", "proj", q)
                    tt(out=h[:, q, :], in0=ps[:, 0:D], in1=h[:, q, :], op=ALU.add).then_inc(free_of("D", "proj", q), 1)
                for g, (t0, t1) in enumerate(GROUPS):
                    if t == t1 + 4:
                        route(g, t0, t1)
            ps = filled(dve, "counts")
            nc.vector.tensor_copy(tiles_f[:, 0, :], ps[:, 0:NE]).then_inc(free_of("counts"), 1)
            was_read(dve, "counts")
            link(nc.vector.tensor_copy(counts[:], tiles_f[:, 0, :]))
            link(tt(out=tilecmp, in0=repeat(tiles_f[:, 0, :], 2, T - 1), in1=repeat(steps[:], 1, NE), op=ALU.is_gt))
            link(nc.vector.reduce_sum(tiles_f[:, 1, :], tilecmp, AX_X))
            link(ts(out=tiles_f[:, 1, :], in0=tiles_f[:, 1, :], scalar1=1.0, scalar2=None, op0=ALU.add))
            link(nc.vector.tensor_tensor_scan(out=tiles_f[:, 2, :], data0=ones[:, 0:NE], data1=tiles_f[:, 1, :], initial=0.0, op0=ALU.mult, op1=ALU.add))
            link(nc.vector.tensor_copy(starts[:, 1:NE + 1], tiles_f[:, 2, :]))
            dve.wait_ge(sem("pad_ready"), 2)
            nc.vector.memset(starts[:, 0:1], 0).then_inc(sem("table_ready"), 1)
            dve.wait_ge(sem("table_ready"), 1)
            nc.vector.memset(mo_meta, 0.0).then_inc(sem("rows_free"), 1)
            dve.wait_ge(sem("rows_free"), 1)

            def take_rows(i):
                dve.wait_ge(full[1], i + (moe_base[1] + 1))
                nc.vector.tensor_copy(mo_xT.rearrange("p k t -> p (k t)"), bank[1][0:HC, 0:2 * P]).then_inc(free[1], 1)
                if not isinstance(i, int):
                    dve.wait_ge(free[0], i + (moe_base[0] - 1))
                nc.vector.tensor_copy(mo_meta[:, bass.ds(i % 2 * META, META)], mo_x[:, D:ROWN]).then_inc(sem("rows_free"), 1)

            take_rows(0)
            with dve.Fori(0, NE) as e:
                first = dve.value_load(starts[0:1, bass.ds(e, 1)], min_val=0, max_val=MAXT - 1)
                end = dve.value_load(starts[0:1, bass.ds(e + 1, 1)], min_val=1, max_val=MAXT)
                with dve.Fori(first, end) as i:
                    take_rows(i + 1)
                    dve.wait_ge(sem("rows_free"), i + 2)
                    dve.wait_ge(sem("accumulated"), i * 16 + ACC0)
                    meta = i % 2 * META
                    nc.vector.tensor_copy(number_u[:], mo_meta[:, bass.ds(meta, 1)])
                    dve.wait_ge(full[0], i + (moe_base[0] + 1))
                    ts(out=mo_res, in0=bank[0][:, 0:D], scalar1=mo_meta[:, bass.ds(meta + e + 1, 1)], scalar2=None, op0=ALU.mult).then_inc(free[0], 1)

        @block.tensor
        def _(pe):
            mm = nc.tensor.matmul
            pe.wait_ge(sem("ones_set"), 2)
            loaded(pe, "const")

            def tok_products(tiles):
                for c in range(FC):
                    for t in tiles:
                        if c == 0:
                            claim("tok", t)
                        if t == 0:
                            pe.wait_ge(sem("weff"), c + 1)
                        x = xf[:, c, t * P:(t + 1) * P]
                        ps = bank[uses["tok", t][0]]
                        mm(ps[:, 0:D], x, weff[:, c, :], start=(c == 0), stop=(c == FC - 1))

            def tok_sums(tiles):
                for col, src in ((D, xf), (D + 1, xsq)):
                    for c in range(FC):
                        pe.wait_ge(sem("squares"), c + 1)
                        for t in tiles:
                            ps = bank[uses["tok", t][0]]
                            ins = mm(ps[:, col:col + 1], src[:, c, t * P:(t + 1) * P], cnt[:, c:c + 1], start=(c == 0), stop=(c == FC - 1))
                            if col == D + 1 and c == FC - 1:
                                ins.then_inc(full_of("tok", t), 1)

            first = range(T // 2)
            tok_products(first)
            tok_sums(first)
            loaded(pe, "small")
            ps = claim("cbias")
            for c in range(FC):
                for v in range(NSH):
                    mm(ps[:, 0:D], beta5[:, v, c:c + 1].broadcast_to([FP, P]), w5[:, c, v, :], start=(c == 0 and v == 0), stop=False)
            mm(ps[:, 0:D], ones[0:1, :], row("tokb"), start=False, stop=True).then_inc(full_of("cbias"), 1)
            ps = claim("colsum")
            for c in range(FC):
                ins = mm(ps[:, 0:D], ones[0:FP, :], weff[:, c, :], start=(c == 0), stop=(c == FC - 1))
            ins.then_inc(full_of("colsum"), 1)
            tok_products(range(T // 2, T))
            tok_sums(range(T // 2, T))

            def transposes(L):
                for n in range(2):
                    for k in range(2):
                        ps = claim(L, "xT", n, k)
                        for j in range(4):
                            t = 4 * n + j
                            if k == 0:
                                pe.wait_ge(sem(f"normed_{L}"), t + 1)
                            ins = nc.tensor.transpose(ps[0:HC, j * P:(j + 1) * P], xn[:, t, k * HC:(k + 1) * HC], ident[:])
                        ins.then_inc(full_of(L, "xT", n, k), 1)

            def attention(L):
                W = weights[L]
                loaded(pe, L)
                for n in range(2):
                    for k in range(2):
                        was_read(pe, L, "xT", n, k)
                    for o in range(4):
                        ps = claim(L, "qk", n, o)
                        for k in range(2):
                            ins = mm(ps[0:HC, :], W[:, k, o * HC:(o + 1) * HC], xT[:, k, n * HALF:(n + 1) * HALF], start=(k == 0), stop=(k == 1))
                        ins.then_inc(full_of(L, "qk", n, o), 1)
                for t in range(T):
                    ps = claim(L, "V", t)
                    for k in range(2):
                        ins = mm(ps[:, 0:D], xT[:, k, t * P:(t + 1) * P], W[:, k, 2 * D:3 * D], start=(k == 0), stop=(k == 1 and L != "A"))
                    if L == "A":
                        ins = mm(ps[:, 0:D], ones[0:1, :], rows_sb[0:1, ROW["bqkvA"] + 2 * D:ROW["bqkvA"] + 3 * D], start=False, stop=True)
                    ins.then_inc(full_of(L, "V", t), 1)
                u = 0
                for n in range(2):
                    for f in range(2):
                        u += 1
                        pe.wait_ge(sem(f"{L}_spread"), u)
                        was_read(pe, L, "qk", n, 2 + f)
                        ps = claim(L, "score", n, f)
                        for b in range(IB):
                            ins = mm(ps[0:HC, b * NTOK:(b + 1) * NTOK], qbd[2 * n + f][:, b, :, :].rearrange("p h i -> p (h i)"),
                                     qk[:, 2 + f, n, b * NTOK:(b + 1) * NTOK], start=True, stop=True)
                        ins.then_inc(full_of(L, "score", n, f), 1)
                for t in range(T + 3):
                    if t < T:
                        n = t // 4
                        pe.wait_ge(sem(f"{L}_probs"), 2 * n + 2)
                        ps = claim(L, "PT", t)
                        for f in range(2):
                            ins = nc.tensor.transpose(ps[:, f * HC:(f + 1) * HC], prob[:, f, n, (t % 4) * P:(t % 4 + 1) * P], ident[0:HC, 0:HC])
                        ins.then_inc(full_of(L, "PT", t), 1)
                    if 0 <= t - 1 < T:
                        q = t - 1
                        was_read(pe, L, "PT", q)
                        was_read(pe, L, "V", q)
                        ps = claim(L, "AV", q)
                        for hh in range(H):
                            ins = mm(ps[:, hh * HD:(hh + 1) * HD], ptbd[q % 2][:, hh, :, :].rearrange("p b i -> p (b i)"), V[:, q, hh * HD:(hh + 1) * HD], start=True, stop=True)
                        ins.then_inc(full_of(L, "AV", q), 1)
                    if 0 <= t - 2 < T:
                        q = t - 2
                        was_read(pe, L, "AV", q)
                        ps = claim(L, "oT", q)
                        for k in range(2):
                            ins = nc.tensor.transpose(ps[0:HC, k * P:(k + 1) * P], osb[:, q % 2, k * HC:(k + 1) * HC], ident[:])
                        ins.then_inc(full_of(L, "oT", q), 1)
                    if 0 <= t - 3 < T:
                        q = t - 3
                        was_read(pe, L, "oT", q)
                        ps = claim(L, "proj", q)
                        wo = wout["S"] if L == "B" and q >= T // 2 else wout[L]
                        if L == "B" and q == T // 2:
                            pe.wait_ge(sem("small_weights"), 3)
                        for k in range(2):
                            ins = mm(ps[:, 0:D], oT[:, q % 2, k, :], wo[:, k, :], start=(k == 0), stop=False)
                        if True:
                            ins = mm(ps[:, 0:D], ones[0:1, :], row("boutA" if L == "A" else "boutB" if q < T // 2 else "boutS"), start=False, stop=True)
                        ins.then_inc(full_of(L, "proj", q), 1)

            transposes("A")
            attention("A")
            transposes("B")
            attention("B")
            transposes("M")
            loaded(pe, "mlp")
            for k in range(2):
                was_read(pe, "M", "xT", 0, k)
            for m in range(MC):
                ps = claim("fc1", 3, m)
                for k in range(2):
                    ins = mm(ps[:, :], w1[:, k, m * P:(m + 1) * P], xT[:, k, 0:HALF], start=(k == 0), stop=(k == 1))
                ins.then_inc(full_of("fc1", 3, m), 1)
            for k in range(2):
                was_read(pe, "M", "xT", 1, k)
            for i, p0, p1, k in ((2, 0, KEEP[2], 0), (1, KEEP[2], KEEP[1], 0), (0, 0, HC, 1)):
                for m in range(MC):
                    ps = claim("fc1", i, m)
                    mm(ps[:, :], w1[p0:p1, k, m * P:(m + 1) * P], xT[p0:p1, k, HALF:TOK], start=(i == 2), stop=True, skip_group_check=(i != 2)).then_inc(full_of("fc1", i, m), 1)
            for t in range(T):
                ps = claim("fc2", t)
                col = slice((t % 4) * P, (t % 4 + 1) * P)
                if t < T // 2:
                    for m in range(MC):
                        was_read(pe, "fc1", 3, m)
                        mm(ps[:, 0:D], hT[3][:, m, col], w2[:, m, :], start=(m == 0), stop=False)
                    mm(ps[:, 0:D], ones[0:1, :], row("b2"), start=False, stop=True).then_inc(full_of("fc2", t), 1)
                else:
                    mm(ps[:, 0:D], ones[0:1, :], row("b2S"), start=True, stop=False)
                    for i in (2, 1, 0):
                        for m in range(MC):
                            was_read(pe, "fc1", i, m)
                            ins = mm(ps[:, 0:KEEP[i]], hT[i][:, m, col], w2s[i][:, m, :], start=False, stop=(i == 0 and m == MC - 1))
                    ins.then_inc(full_of("fc2", t), 1)
            def route(g, t0, t1):
                for t in range(t0, t1):
                    pe.wait_ge(sem("normed_R"), t + 1)
                    ps = claim("R", "xT", t)
                    for k in range(2):
                        ins = nc.tensor.transpose(ps[0:HC, k * P:(k + 1) * P], xrow[:, t, k * HC:(k + 1) * HC], ident[:])
                    ins.then_inc(full_of("R", "xT", t), 1)
                for t in range(t0, t1):
                    was_read(pe, "R", "xT", t)
                    ps = claim("logit", t)
                    for k in range(2):
                        mm(ps[:, 0:G + NE], xT[:, k, t * P:(t + 1) * P], wr[:, k, :], start=(k == 0), stop=False)
                    mm(ps[:, 0:G + NE], ones[0:1, :], row("route", G + NE), start=False, stop=True).then_inc(full_of("logit", t), 1)
                pe.wait_ge(sem("chosen"), g + 1)
                ps = claim("place", g)
                mm(ps[:, 0:(t1 - t0) * NE], ones[:], earlier[:, t0:t1, :], start=True, stop=False)
                mm(ps[:, 0:(t1 - t0) * NE], prefix[:], sel[:, t0:t1, :], start=False, stop=True).then_inc(full_of("place", g), 1)
                for t in range(t0, t1):
                    ps = claim("cT", t)
                    nc.tensor.transpose(ps[0:NE, 0:P], xrow[:, t, D + 1:ROWN], ident[:]).then_inc(full_of("cT", t), 1)
                    was_read(pe, "cT", t)
                    ps = claim("y0", t)
                    mm(ps[:, 0:D], cT[:, t, :], b2all[:], start=True, stop=True).then_inc(full_of("y0", t), 1)

            transposes("D")
            loaded(pe, "D")
            W = weights["D"]
            for t in range(T):
                for k in range(2):
                    was_read(pe, "D", "xT", t // 4, k)
                for name, c0, c1 in (("qk", 0, 2 * D), ("V", 2 * D, 3 * D)):
                    ps = claim("D", name, t)
                    for k in range(2):
                        ins = mm(ps[:, 0:c1 - c0], xT[:, k, t * P:(t + 1) * P], W[:, k, c0:c1], start=(k == 0), stop=(k == 1))
                    ins.then_inc(full_of("D", name, t), 1)
            for t in range(T + 1):
                if t < T:
                    pe.wait_ge(sem("D_rows"), t + 1)
                    ps = claim("D", "oT", t)
                    for k in range(2):
                        ins = nc.tensor.transpose(ps[0:HC, k * P:(k + 1) * P], oD[t % 2][:, k * HC:(k + 1) * HC], ident[:])
                    ins.then_inc(full_of("D", "oT", t), 1)
                if t >= 1:
                    was_read(pe, "D", "oT", t - 1)
                    ps = claim("D", "proj", t - 1)
                    for k in range(2):
                        ins = mm(ps[:, 0:D], oT[:, (t - 1) % 2, k, :], wout["D"][:, k, :], start=(k == 0), stop=(k == 1))
                    ins.then_inc(full_of("D", "proj", t - 1), 1)
                for g, (t0, t1) in enumerate(GROUPS):
                    if t == t1:
                        route(g, t0, t1)
            ps = claim("counts")
            mm(ps[:, 0:NE], ones[:], earlier[:, T, :], start=True, stop=True).then_inc(full_of("counts"), 1)

            def transpose_rows(i):
                pe.wait_ge(sem("rows_in"), i * 16 + 16)
                for k in range(2):
                    ins = nc.tensor.transpose(bank[1][0:HC, k * P:(k + 1) * P], mo_x[:, k * HC:(k + 1) * HC], ident[:])
                ins.then_inc(full[1], 1)

            pe.wait_ge(free[1], moe_base[1])
            pe.wait_ge(sem("table_ready"), 1)
            transpose_rows(0)

            def expert(u, e):
                loads = pe.snap((e - u) * 24 + 48)
                pe.wait_ge(sem("table_ready"), 1)
                pe.wait_ge(sem(f"in_expert{u}"), loads)
                first = pe.value_load(starts[0:1, bass.ds(e, 1)], min_val=0, max_val=MAXT - 1)
                end = pe.value_load(starts[0:1, bass.ds(e + 1, 1)], min_val=1, max_val=MAXT)
                with pe.Fori(first, end) as i:
                    pe.wait_ge(free[1], i + (moe_base[1] + 1))
                    for m in range(MC):
                        pe.wait_ge(free[2 + m], i + moe_base[2 + m])
                        for k in range(2):
                            ins = mm(bank[2 + m][:, 0:P], mo_w1[u][:, k, m * P:(m + 1) * P], mo_xT[:, k, :], start=(k == 0), stop=(k == 1))
                        ins.then_inc(full[2 + m], 1)
                    transpose_rows(i + 1)
                    pe.wait_ge(free[0], i + moe_base[0])
                    for m in range(MC):
                        pe.wait_ge(free[2 + m], i + (moe_base[2 + m] + 1))
                        ins = mm(bank[0][:, 0:D], mo_hT[:, m, :], mo_w2[u][:, m, :], start=(m == 0), stop=(m == MC - 1))
                    ins.then_inc(full[0], 1)

            with pe.Fori(0, NE // 2) as pair:
                for u in range(2):
                    expert(u, pair * 2 + u)
        for k, v in lots.items():
            assert v == LOT[k], (k, v)


def kernel(**inputs):
    import concourse.bacc as bacc
    from concourse.bass_utils import run_bass_kernel_spmd

    f32 = np.float32
    i = {k: np.asarray(v) for k, v in inputs.items()}

    order, rows = pixel_layout()
    padded = np.pad(i["x"], ((0, 0), (0, 0), (1, 1), (1, 1)))
    xf = np.empty((NF, B, SIDE, SIDE), f32)
    for f, (c, r, w) in enumerate(order):
        xf[f] = padded[:, c, r + 1:r + 1 + IMG:PATCH, w + 1:w + 1 + IMG:PATCH][:, :SIDE, :SIDE]
    xf = xf.reshape(FC, FP, TOK)

    def by_shift(a):
        a = np.concatenate([a, np.zeros((1,) + a.shape[1:], a.dtype)])
        return a[rows]

    w5 = by_shift(i["L0_tok_w"]).reshape(NSH, FC, FP, D).transpose(1, 2, 0, 3)
    arr = {
        "xf": xf, "w5": w5,
        "gamma5": by_shift(i["L0_tok_ln_gamma"]).reshape(NSH, FC, FP).transpose(2, 0, 1),
        "beta5": by_shift(i["L0_tok_ln_beta"]).reshape(NSH, FC, FP).transpose(2, 0, 1),
        "cnt": ((rows >= 0).sum(0) / NPATCH).astype(f32).reshape(FC, FP).T,
        "ident": np.eye(P, dtype=f32),
        "blockmask": (np.arange(P)[:, None] // NTOK == np.arange(TB)[None, :]).astype(f32),
        "wqkvA": i["L0_attn_w_qkv"], "woutA": i["L0_attn_w_proj"],
        "wqkvB": i["L0_ffn_w_qkv"], "woutB": i["L0_ffn_w_proj"],
        "wqkvD": i["L1_attn_W_attn"].T, "woutD": i["L1_attn_W_out"].T,
        "gum": i["L0_ffn_gumbel_weights"].reshape(1, 3),
        "lamv": np.stack([i["L1_attn_lambda_q1"], i["L1_attn_lambda_k1"], i["L1_attn_lambda_q2"], i["L1_attn_lambda_k2"]])[None],
        "b1": i["L0_ffn_b_fc1"].reshape(MC, P).T, "w1": i["L0_ffn_w_fc1"], "w2": i["L0_ffn_w_fc2"],
        "wr": np.concatenate([i["L1_ffn_Wg"], i["L1_ffn_We"].transpose(1, 0, 2).reshape(D, NE)], 1),
        "moe_w1": i["L1_ffn_W1"].reshape(NE, D, HID), "moe_b1": i["L1_ffn_b1"].reshape(NE, MC, P).transpose(0, 2, 1),
        "moe_w2": i["L1_ffn_W2"].reshape(NE, HID, D), "moe_b2": i["L1_ffn_b2"].reshape(NE, D),
    }
    c = np.arange(HC)
    arr["headmask"] = (c[:, None] // HD == np.arange(HH)[None, :]).astype(f32)
    j = np.arange(NTOK)
    arr["selfmask"] = np.where((c % NTOK)[:, None] == j[None, :], np.where(j > 0, NEG, 0.0)[None, :], 0.0).astype(f32)
    arr["numbers"] = (np.arange(T + 1)[None, :] * P + np.arange(P)[:, None]).astype(f32)
    arr["slot1"] = np.tile((np.arange(NE) * SLOTS + 1.0).astype(f32)[None], (P, 1))
    arr["prefix"] = (np.arange(P)[:, None] < np.arange(P)[None, :]).astype(f32)
    arr["steps"] = np.tile((np.arange(1, T) * P).astype(f32)[None], (P, 1))
    arr["tri"] = np.tile((np.arange(E)[None, :] < np.arange(E)[:, None]).astype(f32).reshape(1, E * E), (P, 1))
    rowv = np.zeros((1, 2048), f32)
    pieces = [i["L0_tok_b"], i["L0_attn_b_qkv"], i["L0_attn_b_proj"], i["L0_ffn_b_proj"], i["L0_ffn_b_fc2"],
              i["L1_ffn_bg"], i["L1_ffn_be"].reshape(NE)]
    n = 0
    for p in pieces:
        rowv[0, n:n + p.size] = p
        n += p.size
    arr["rows"] = rowv
    colv = np.zeros((HC, 24), f32)
    colv[:, 0:4] = i["L0_attn_b_qkv"][:4 * HC].reshape(4, HC).T
    for at, name in ((4, "n1l"), (8, "n1s"), (12, "n2l"), (16, "n2s")):
        colv[:, at:at + 2] = i[f"L0_ffn_{name}_g"].reshape(2, HC).T
        colv[:, at + 2:at + 4] = i[f"L0_ffn_{name}_b"].reshape(2, HC).T
    colv[:, 20:22] = np.repeat(i["L0_attn_scale"], NTOK).reshape(2, HC).T
    arr["cols"] = colv

    nc = bacc.Bacc("TRN2", target_bir_lowering=False, num_devices=1)
    arrays = {f"in_{k}_dram": np.ascontiguousarray(v) for k, v in arr.items()}
    aps = {k: nc.dram_tensor(f"in_{k}_dram", arrays[f"in_{k}_dram"].shape, F32, kind="ExternalInput").ap() for k in arr}
    out = nc.dram_tensor("out_0_dram", (TOK, D), F32, kind="ExternalOutput").ap()
    vit_tower(nc, aps, out)
    r = run_bass_kernel_spmd(nc, [arrays], core_ids=[0])
    return r.results[0]["out_0_dram"].reshape(B, NTOK, D)
```

```python
from contextlib import ExitStack

import numpy as np

import concourse.bass as bass
from concourse import mybir
from concourse.alu_op_type import AluOpType as ALU

ACT = mybir.ActivationFunctionType
F32 = mybir.dt.float32
U32 = mybir.dt.uint32
I32 = mybir.dt.int32
AX_X = mybir.AxisListType.X

P = 128
B, NCH, IMG, PATCH = 64, 3, 64, 16
SIDE = IMG // PATCH
NTOK = SIDE * SIDE
TOK = B * NTOK
T = TOK // P
TB = P // NTOK
D = 192
HC = D // 2
H, HH, HD = 12, 6, 16
QUAD = 32
QB = QUAD // NTOK
QH = QUAD // HD
HALF = TOK // 2
IB = B // 2
HID = 768
MC = HID // P
NSH = 5
NF = NCH * ((PATCH + 2) ** 2 - 4)
FC, FP = 8, NF // 8
NPATCH = PATCH * PATCH * NSH * NCH
KEEP = (D, D // 2, D // 3)
G, E, KG, KE = 4, 8, 2, 4
NE = G * E
EPS_LN, EPS_GATE = 1e-5, 1e-6
LAMBDA_INIT = 0.8 - 0.6 * float(np.exp(-0.3 * 12))
KSEL = KG * KE
SLOTS = TOK + P
W2N = MC * D + MC
AHEAD = 4
META = 1 + NE
ROWN = D + META
GROUPS = ((0, 4), (4, 8))
NEG = -1.0e30


def tower_order():
    def attn(L, lo, hi):
        return [("av", L, s) for s in range(lo, hi)]

    def last(lo, hi):
        return [("D", "D", s) for s in range(lo, hi)]

    return (
        [("tok", "T", 0), ("ln", "A", 0), ("xT", "A", 0), ("tok", "T", 1), ("qk", "A", 0), ("ln", "A", 1), ("V", "A", 0),
         ("front", "A", 0), ("xT", "A", 1), ("qk", "A", 1), ("V", "A", 1), ("gumbel", "B", 0), ("back", "A", 0)]
        + attn("A", 0, 2) + [("front", "A", 1)] + attn("A", 2, 3) + [("back", "A", 1)] + attn("A", 3, 7)
        + [("ln", "z", 0)] + attn("A", 7, 8) + [("ln", "B", 0)] + attn("A", 8, 9) + [("xT", "B", 0), ("qk", "B", 0)]
        + attn("A", 9, T + 3) + [("V", "B", 0), ("front", "B", 0), ("ln", "z", 1), ("ln", "B", 1), ("back", "B", 0), ("xT", "B", 1), ("qk", "B", 1)]
        + attn("B", 0, 2) + [("V", "B", 1), ("front", "B", 1)] + attn("B", 2, 3) + [("back", "B", 1)] + attn("B", 3, 7)
        + [("ln", "M", 0)] + attn("B", 7, 8) + [("lambda", "D", 0)] + attn("B", 8, 9) + [("xT", "M", 0), ("fc1", "M", 0)]
        + attn("B", 9, T + 3) + [("ln", "M", 1), ("fc2", "M", 0), ("ffn", "M", 0), ("xT", "M", 1), ("ln", "D", 0), ("fc1", "M", 1), ("xT", "D", 0), ("qkv", "D", 0)]
        + [("fc2", "M", 1)] + last(0, 2) + [("ffn", "M", 1), ("ln", "D", 1), ("xT", "D", 1), ("qkv", "D", 1)]
        + last(2, 7) + [("norm", "R", 0)] + last(7, 8) + [("gates", "R", 0)] + last(8, 9) + [("slots", "R", 0), ("scatter", "R", 0)]
        + last(9, T + 3) + [("norm", "R", 1), ("scatter", "R", 1), ("scatter", "R", 2), ("scatter", "R", 3), ("gates", "R", 1), ("slots", "R", 1)]
        + [("scatter", "R", t) for t in range(4, T)] + [("counts", "R", 0), ("begin", "R", 0), ("begin", "R", 1)])


def pixel_layout():
    order = [(c, i, j) for c in range(NCH) for i in range(-1, PATCH + 1) for j in range(-1, PATCH + 1)
             if not (i in (-1, PATCH) and j in (-1, PATCH))]
    moves = [(0, 0), (0, -1), (0, 1), (-1, 0), (1, 0)]
    rows = np.full((NSH, NF), -1, np.int64)
    for f, (c, i, j) in enumerate(order):
        for v, (di, dj) in enumerate(moves):
            pi, pj = i - di, j - dj
            if 0 <= pi < PATCH and 0 <= pj < PATCH:
                rows[v, f] = (pi * PATCH + pj) * NSH * NCH + v * NCH + c
    return order, rows


def repeat(ap, axis, n):
    ap = ap.unsqueeze(axis)
    shape = list(ap.shape)
    shape[axis] = n
    return ap.broadcast_to(shape)


def vit_tower(nc, a, out):
    ctx = ExitStack()
    with ctx:
        def sb(name, shape, dtype=F32):
            return ctx.enter_context(nc.sbuf_tensor(name, shape, dtype))

        dispatch = nc.dram_tensor("dispatch", (NE * SLOTS, ROWN), F32, kind="Internal").ap()
        summed = nc.dram_tensor("summed", (TOK + P, D), F32, kind="Internal").ap()

        sems = {}

        def sem(name):
            if name not in sems:
                sems[name] = ctx.enter_context(nc.semaphore(name))
            return sems[name]

        ident = sb("ident", [P, P])
        ones = sb("ones", [P, P])
        blockmask = sb("blockmask", [P, QB])
        headmask = sb("headmask", [HC, QH])
        selfmask = sb("selfmask", [HC, NTOK])
        tri = sb("tri", [P, E * E])
        cnt = sb("cnt", [FP, FC])
        gamma5 = sb("gamma5", [FP, NSH, FC])
        beta5 = sb("beta5", [FP, NSH, FC])
        minus_half = sb("minus_half", [P, T])
        rows_sb = sb("rows_sb", [1, 2048])
        cols_sb = sb("cols_sb", [HC, 24])
        b1_sb = sb("b1_sb", [P, MC])
        gum = sb("gum", [P, 5])
        lamv = sb("lamv", [P, 4, 8])
        lam = sb("lam", [P, 8])
        headfac = sb("headfac", [P, 2, H])
        wab = sb("wab", [HC, 2 * 2 * 3 * D])
        weights = {L: wab[:, n * 6 * D:(n + 1) * 6 * D].rearrange("p (k n) -> p k n", k=2) for n, L in enumerate("AB")}
        weights["D"] = sb("wqkvD", [HC, 2, 3 * D])
        wout = {L: sb(f"wout{L}", [HC, 2, D]) for L in "ABDS"}
        w1 = sb("w1", [HC, 2, HID])
        w2_space = sb("w2_space", [P, W2N])
        w2 = w2_space[:, 0:MC * D].rearrange("p (m d) -> p m d", m=MC)
        w2small = sb("w2small", [P, MC * sum(KEEP)])
        w2s = [w2small[:, MC * sum(KEEP[:i]):MC * sum(KEEP[:i + 1])].rearrange("p (m n) -> p m n", m=MC) for i in range(3)]
        slot1 = sb("slot1", [P, NE])
        prefix = sb("prefix", [P, P])
        steps = sb("steps", [P, T - 1])
        slots_u = sb("slots_u", [P, T, KSEL], U32)
        starts = sb("starts", [P, NE + 1], I32)
        counts = sb("counts", [P, NE], I32)
        number_u = sb("number_u", [P, 1], U32)
        wr = sb("wr", [HC, 2, G + NE])
        b2all = sb("b2all", [NE, D])

        h = sb("h", [P, T, D])
        z = sb("z", [P, T, D])
        xn = sb("xn", [P, T, D])
        v_space = sb("v_space", [P, T * D + FC])
        V = v_space[:, 0:T * D].rearrange("p (t d) -> p t d", t=T)
        xT = sb("xT", [HC, 2, TOK])
        osb = sb("osb", [P, 2, D])
        oT = sb("oT", [HC, 2, 2, P])
        stats = sb("stats", [P, T, 6])
        mv = sb("mv", [P, T, 2])
        rstd = sb("rstd", [P, T])
        numbers = sb("numbers", [P, T + 1])
        tokst = sb("tokst", [P, T, 4])
        tmpt = sb("tmpt", [P, 2, D])
        colsum = sb("colsum", [P, D])
        cbias = sb("cbias", [P, D])
        smx = sb("smx", [HC, 2, IB])
        ssum = sb("ssum", [HC, 2, IB])
        srec = sb("srec", [HC, 2, IB])

        arena = sb("arena", [P, 24320])
        at = [0]

        def view(parts, n):
            v = arena[0:parts, at[0]:at[0] + n]
            at[0] += n
            return v

        xf = view(FP, FC * TOK).rearrange("p (c t) -> p c t", c=FC)
        xsq = view(FP, FC * TOK).rearrange("p (c t) -> p c t", c=FC)
        w5 = view(FP, NSH * FC * D).rearrange("p (c v n) -> p c v n", c=FC, v=NSH)
        weff = v_space[0:FP, :].rearrange("p (c n) -> p c n", c=FC)
        foldsum = z[0:FP, 0, :]
        betasum = z[0:FP, 1:1 + NSH, :]
        betaprod = xn[0:FP, 0:NSH, :]
        at[0] = 0
        hT_large = view(P, MC * HALF).rearrange("p (m t) -> p m t", m=MC)
        qbd = [view(HC, IB * QUAD).rearrange("p (b h i) -> p b h i", b=IB, h=QH) for _ in range(4)]
        prob = view(HC, 2 * B * NTOK).rearrange("p (f n x) -> p f n x", f=2, n=2)
        ptbd = [view(P, H * QUAD).rearrange("p (h b i) -> p h b i", h=H, b=QB) for _ in range(2)]
        qk = view(HC, 4 * TOK).rearrange("p (o n x) -> p o n x", o=4, n=2)
        behind_attention = at[0]
        at[0] = 0
        qkD = view(P, T * 2 * D).rearrange("p (t n) -> p t n", t=T)
        prodS = [view(P, H * H * HD) for _ in range(2)]
        prodV = [view(P, H * H * HD) for _ in range(2)]
        scD = [view(P, 2 * H * H) for _ in range(3)]
        mxD = [view(P, 2 * H) for _ in range(3)]
        peff = [view(P, H * H) for _ in range(2)]
        oD = [view(P, D) for _ in range(2)]
        behind_heads = at[0]
        at[0] = max(behind_heads, behind_attention)
        hT = [view(P, MC * HALF).rearrange("p (m t) -> p m t", m=MC) for _ in range(3)] + [hT_large]
        at[0] = behind_heads
        cmpa = view(P, 4 * NE * E)
        cmpb = view(P, 4 * NE * E)
        gwork = view(P, 2 * 4 * (G + NE) + 4 * (1 + G))
        lgG = view(P, 4 * G).rearrange("p (r e) -> p r e", e=G)
        lgE = view(P, 4 * NE).rearrange("p (r e) -> p r e", e=E)
        sel = view(P, T * NE).rearrange("p (t e) -> p t e", t=T)
        earlier = view(P, (T + 1) * NE).rearrange("p (t e) -> p t e", t=T + 1)
        key = view(P, 4 * NE).rearrange("p (t e) -> p t e", t=4)
        top8 = view(P, T * KSEL).rearrange("p (t k) -> p t k", t=T)
        tiles_f = view(P, 3 * NE).rearrange("p (a e) -> p a e", a=3)
        tilecmp = view(P, NE * (T - 1)).rearrange("p (e k) -> p e k", e=NE)
        cT = view(NE, T * P).rearrange("p (t x) -> p t x", t=T)
        y = view(P, T * D).rearrange("p (t d) -> p t d", t=T)
        xrow = view(P, T * ROWN).rearrange("p (t n) -> p t n", t=T)
        padrow = view(P, ROWN)
        assert at[0] <= 24320
        at[0] = 0
        mo_hT = view(P, MC * P).rearrange("p (m t) -> p m t", m=MC)
        mo_x = view(P, ROWN)
        mo_xT = view(HC, 2 * P).rearrange("p (k t) -> p k t", k=2)
        mo_meta = view(P, 2 * META)
        mo_res = view(P, D)
        mo_w1 = [w1[:].rearrange("p k m -> p (k m)"), wab[:, 0:2 * HID]] + [view(HC, 2 * HID) for _ in range(2)]
        mo_w2 = [w2_space[:], w2small[:, 0:W2N]] + [view(P, W2N) for _ in range(2)]
        assert at[0] <= behind_heads
        gparts = {}
        gat = 0
        for which, r_, n_ in (("G", 4, G), ("E", 4 * G, E)):
            for part, size in (("sel", r_ * n_), ("d", r_ * n_), ("mx", r_)):
                v = gwork[:, gat:gat + size]
                gparts[which, part] = v.rearrange("p (r e) -> p r e", e=n_) if part != "mx" else v
                gat += size

        def gview(which, part):
            return gparts[which, part]

        bank = [ctx.enter_context(nc.psum_tensor(f"bank{i}", [P, 512], F32)) for i in range(8)]
        full = [sem(f"bank{i}_full") for i in range(8)]
        free = [sem(f"bank{i}_free") for i in range(8)]

        uses, used = {}, [0] * 8

        def use(b, *key):
            uses[key] = (b, used[b])
            used[b] += 1

        def claim(*key):
            b, k = uses[key]
            if k:
                nc.tensor.wait_ge(free[b], k)
            return bank[b]

        def filled(eng, *key):
            b, k = uses[key]
            eng.wait_ge(full[b], k + 1)
            return bank[b]

        def was_read(eng, *key):
            b, k = uses[key]
            eng.wait_ge(free[b], k + 1)

        def full_of(*key):
            return full[uses[key][0]]

        def free_of(*key):
            return free[uses[key][0]]

        ORDER = tower_order()

        def plan(step, L, n):
            tiles = range(4 * n, 4 * n + 4)
            if step == "tok" and n == 0:
                for t in range(T):
                    use(t, "tok", t)
            elif step == "xT":
                for k in range(2):
                    use(2 + k, L, "xT", n, k)
            elif step == "qk":
                for o in range(4):
                    use(4 + o % 2, L, "qk", n, o)
            elif step == "V":
                for t in tiles:
                    use(t % 2, L, "V", t)
            elif step == "front":
                for f in range(2):
                    use(6 + f, L, "score", n, f)
            elif step == "av":
                t = n
                if t < T:
                    use(2 + t % 2, L, "PT", t)
                if 0 <= t - 1 < T:
                    use((t - 1) % 2, L, "AV", t - 1)
                if 0 <= t - 2 < T:
                    use(4 + t % 2, L, "oT", t - 2)
                if 0 <= t - 3 < T:
                    use(6 + (t - 3) % 2, L, "proj", t - 3)
            elif step == "fc1":
                for i in (3,) if n == 0 else (2, 1, 0):
                    for m in range(MC):
                        use(2 + m, "fc1", i, m)
            elif step == "fc2":
                for t in tiles:
                    use(t % 2 if n == 0 else (2, 3, 6, 7)[t % 4], "fc2", t)
            elif step == "qkv":
                for t in tiles:
                    use(4 + t % 2, L, "qk", t)
                    use(t % 2, L, "V", t)
            elif step == "D":
                if 0 <= n - 2 < T:
                    use(2 + n % 2, L, "oT", n - 2)
                    use(6 + n % 2, L, "proj", n - 2)
            elif step == "norm":
                for q in range(*GROUPS[n]):
                    use(4 + q % 2, "R", "xT", q)
                for q in range(*GROUPS[n]):
                    use(q % 2, "logit", q)
            elif step == "slots":
                use(4, "place", n)
            elif step == "counts":
                use(4, "counts")
            elif step == "begin":
                for q in range(*GROUPS[n]):
                    use(q % 2, "cT", q)
                    use(5 + q % 2, "y0", q)

        for entry in ORDER:
            plan(*entry)
        moe_base = list(used)

        lots = {}

        def load(eng, lot, dst, src):
            lots[lot] = lots.get(lot, 0) + 16
            eng.dma_start(dst, src).then_inc(sem(f"in_{lot}"), 16)

        LOT = {"const": 16 * 12, "A": 16 * 2, "B": 16 * 2, "D": 16 * 2, "mlp": 16 * 2, "small": 16 * 7,
               "route": 16 * 2}

        def loaded(eng, lot):
            eng.wait_ge(sem(f"in_{lot}"), LOT[lot])

        halves = "(k p) n -> p k n"
        MAXT = KSEL * T + NE
        ACC0 = 16

        def load_expert(eng, u, e):
            one = bass.ds(e, 1)
            eng.dma_start(mo_w1[u], a["moe_w1"][one].rearrange("o p n -> p (o n)")).then_inc(sem(f"in_expert{u}"), 16)
            eng.dma_start(mo_w2[u], a["moe_w2"][one].rearrange("o p n -> p (o n)")).then_inc(sem(f"in_expert{u}"), 16)

        def expert_bounds(eng, e0, n):
            return [eng.value_load(starts[0:1, bass.ds(e0 + u, 1)], min_val=min(u, 1), max_val=MAXT) for u in range(n + 1)]

        def pad_experts(eng, e0, e1):
            with eng.Fori(e0, e1) as e:
                n = eng.value_load(counts[0:1, bass.ds(e, 1)], min_val=0, max_val=TOK)
                eng.dma_start(dispatch[bass.ds(e * SLOTS + n, P), :], padrow).then_inc(sem("padded"), 16)

        block = ctx.enter_context(nc.Block())

        @block.sync
        def _(sp):
            load(sp, "const", gamma5[:], a["gamma5"])
            for c in range(FC):
                sp.dma_start(w5[:, c], a["w5"][c]).then_inc(sem(f"in_pixels{c}"), 16)
                sp.dma_start(xf[:, c], a["xf"][c]).then_inc(sem(f"in_pixels{c}"), 16)
                if c == 0:
                    load(sp, "const", beta5[:], a["beta5"])
                    load(sp, "const", cnt[:], a["cnt"])
                    load(sp, "const", ident[:], a["ident"])
                    load(sp, "const", blockmask[:], a["blockmask"])
                    load(sp, "const", headmask[:], a["headmask"])
                    load(sp, "const", selfmask[:], a["selfmask"])
                    load(sp, "const", tri[:], a["tri"])
                    load(sp, "const", slot1[:], a["slot1"])
                    load(sp, "const", prefix[:], a["prefix"])
                    load(sp, "const", steps[:], a["steps"])
                    load(sp, "const", numbers[:], a["numbers"])
                    load(sp, "small", rows_sb[:], a["rows"])
                    load(sp, "small", cols_sb[:], a["cols"])
            load(sp, "A", weights["A"][:], a["wqkvA"].rearrange(halves, p=HC))
            load(sp, "A", wout["A"][:], a["woutA"].rearrange(halves, p=HC))
            load(sp, "small", gum[:, 0:3], a["gum"].broadcast_to([P, 3]))
            load(sp, "small", lamv[:], a["lamv"].broadcast_to([P, 4, 8]))
            load(sp, "small", b1_sb[:], a["b1"])
            load(sp, "small", b2all[:], a["moe_b2"])
            load(sp, "small", wr[:], a["wr"].rearrange(halves, p=HC))
            for L in "BD":
                load(sp, L, weights[L][:], a[f"wqkv{L}"].rearrange(halves, p=HC))
                load(sp, L, wout[L][:], a[f"wout{L}"].rearrange(halves, p=HC))
            load(sp, "mlp", w1[:], a["w1"].rearrange(halves, p=HC))
            load(sp, "mlp", w2[:], a["w2"].rearrange("(m p) n -> p m n", p=P))
            was_read(sp, "fc2", T - 1)
            for u in range(2):
                load_expert(sp, u, u)
            was_read(sp, "D", "proj", T - 1)
            load_expert(sp, 2, 2)
            sp.wait_ge(sem("table_ready"), 1)
            sp.dma_start(summed[TOK:TOK + P, :], padrow[:, 0:D]).then_inc(sem("sums_begun"), 16)
            pad_experts(sp, 0, NE // 2)
            for t in range(T):
                was_read(sp, "y0", t)
                sp.dma_start(summed[t * P:(t + 1) * P, :], y[:, t, :]).then_inc(sem("sums_begun"), 16)
            sp.wait_ge(sem("padded"), 16 * NE)
            sp.wait_ge(sem("dispatched"), 16 * KSEL * T)
            with sp.Fori(0, NE) as e:
                first = sp.value_load(starts[0:1, bass.ds(e, 1)], min_val=0, max_val=MAXT - 1)
                end = sp.value_load(starts[0:1, bass.ds(e + 1, 1)], min_val=1, max_val=MAXT)
                with sp.Fori(first, end) as i:
                    at_row = sp.snap(nc.s_assert_within(e * SLOTS + (i - first) * P, 0, NE * SLOTS - P))
                    sp.wait_ge(sem("rows_free"), i + 1)
                    sp.dma_start(mo_x, dispatch[bass.ds(at_row, P), :]).then_inc(sem("rows_in"), 16)
            total = sp.value_load(starts[0:1, NE:NE + 1], min_val=1, max_val=MAXT)
            sp.wait_ge(sem("rows_free"), total + 1)
            sp.dma_start(mo_x, dispatch[0:P, :]).then_inc(sem("rows_in"), 16)
            sp.wait_ge(sem("accumulated"), total * 16 + ACC0)
            sp.dma_start(out[:, :], summed[0:TOK, :]).then_inc(sem("out_stored"), 16)
            sp.wait_ge(sem("out_stored"), 16)

        ROW = {"tokb": 0, "bqkvA": D, "boutA": 4 * D, "boutB": 5 * D, "b2": 6 * D, "route": 7 * D,
               "boutS": 7 * D + 64, "b2S": 8 * D + 64}
        COL = {"bqkA": 0, "n1l": 4, "n1s": 8, "n2l": 12, "n2s": 16, "scaleA": 20}

        def row(name, n=D):
            return rows_sb[0:1, ROW[name]:ROW[name] + n]

        @block.gpsimd
        def _(pool):
            step = [0]

            def link(ins):
                step[0] += 1
                ins.then_inc(sem("pool_step"), 1)
                pool.wait_ge(sem("pool_step"), step[0])

            nc.gpsimd.memset(ones[:], 1.0).then_inc(sem("ones_set"), 1)
            nc.gpsimd.memset(minus_half[:], -0.5).then_inc(sem("ones_set"), 1)
            pool.wait_ge(sem("ones_set"), 2)

            tt = nc.gpsimd.tensor_tensor

            def fold_sums():
                loaded(pool, "const")
                for c in range(FC):
                    pool.wait_ge(sem(f"in_pixels{c}"), 32)
                    link(tt(out=betaprod if c else betasum, in0=w5[:, c], in1=repeat(beta5[:, :, c], 2, D), op=ALU.mult))
                    if c:
                        link(tt(out=betasum, in0=betasum, in1=betaprod, op=ALU.add))
                    pool.wait_ge(sem("weff"), c + 1)
                    ins = tt(out=foldsum, in0=foldsum, in1=weff[:, c, 0:D], op=ALU.add) if c else nc.gpsimd.tensor_copy(foldsum, weff[:, c, 0:D])
                    if c < FC - 1:
                        link(ins)
                ins.then_inc(sem("fold_summed"), 1)

            def tok_rstd(n):
                s = slice(4 * n, 4 * n + 4)
                pool.wait_ge(sem("tokvar"), n + 1)
                nc.gpsimd.tensor_tensor(out=tokst[:, s, 3:4].rearrange("p t o -> p (t o)"), in0=tokst[:, s, 2:3].rearrange("p t o -> p (t o)"), in1=minus_half[:, s],
                                        op=ALU.pow).then_inc(sem("tokrstd"), 1)

            def gumbel():
                loaded(pool, "small")
                loaded(pool, "B")
                loaded(pool, "mlp")
                link(nc.gpsimd.tensor_tensor(out=gum[:, 3:4], in0=gum[:, 0:1], in1=gum[:, 1:2], op=ALU.add))
                link(nc.gpsimd.tensor_tensor(out=gum[:, 4:5], in0=gum[:, 3:4], in1=gum[:, 2:3], op=ALU.add))

                def times(dst, src, g, p0, p1):
                    link(nc.gpsimd.tensor_scalar(out=dst, in0=src, scalar1=gum[p0:p1, g:g + 1], scalar2=None, op0=ALU.mult))

                for p0, p1, k, c0, c1, g in ((0, KEEP[2], 0, 0, KEEP[2], 4), (KEEP[2], HC, 0, 0, KEEP[2], 3),
                                             (0, HC, 0, KEEP[2], KEEP[1], 3), (0, HC, 0, KEEP[1], D, 0),
                                             (0, HC, 1, 0, D, 0)):
                    times(wout["S"][p0:p1, k, c0:c1], wout["B"][p0:p1, k, c0:c1], g, p0, p1)
                for dst, src in (("boutS", "boutB"), ("b2S", "b2")):
                    for c0, c1, g in ((0, KEEP[2], 4), (KEEP[2], KEEP[1], 3), (KEEP[1], D, 0)):
                        times(rows_sb[0:1, ROW[dst] + c0:ROW[dst] + c1], rows_sb[0:1, ROW[src] + c0:ROW[src] + c1], g, 0, 1)
                for i in range(3):
                    nc.gpsimd.tensor_scalar(out=w2s[i][:], in0=w2[:, :, 0:KEEP[i]], scalar1=gum[:, i:i + 1], scalar2=None, op0=ALU.mult).then_inc(sem("small_weights"), 1)

            ln = [0]

            def ln_rstd(t0, t1):
                s = slice(t0, t1)
                ln[0] += 1
                pool.wait_ge(sem("ln_stats"), ln[0])
                link(nc.gpsimd.tensor_scalar(out=rstd[:, s], in0=mv[:, s, 1:2].rearrange("p t o -> p (t o)"), scalar1=EPS_LN, scalar2=None, op0=ALU.add))
                nc.gpsimd.tensor_tensor(out=rstd[:, s], in0=rstd[:, s], in1=minus_half[:, s], op=ALU.pow).then_inc(sem("ln_rstd"), 1)

            def weigh(t):
                pool.wait_ge(sem("D_probs"), t + 1)
                was_read(pool, "D", "V", t)
                if t >= 2:
                    pool.wait_ge(sem("D_rows"), t - 1)
                p = peff[t % 2].rearrange("p (a b) -> p a b", a=H)
                v = V[:, t, :].rearrange("p (b x) -> p x b", x=HD)
                nc.gpsimd.tensor_tensor(out=prodV[t % 2].rearrange("p (a x b) -> p a x b", a=H, x=HD), in0=repeat(p, 2, HD), in1=repeat(v, 1, H), op=ALU.mult).then_inc(sem("D_weighed"), 1)

            def scatter(t):
                if t == 0:
                    was_read(pool, "fc2", T - 1)
                    link(nc.gpsimd.memset(padrow, 0.0))
                    nc.gpsimd.tensor_copy(padrow[:, D:D + 1], numbers[:, T:T + 1]).then_inc(sem("pad_ready"), 1)
                    nc.gpsimd.tensor_copy(xrow[:, :, D:D + 1], numbers[:, 0:T].unsqueeze(2)).then_inc(sem("pad_ready"), 1)
                    pool.wait_ge(sem("pad_ready"), 2)
                pool.wait_ge(sem("slots_ready"), [t < t1 for t0, t1 in GROUPS].index(True) + 1)
                for k in range(KSEL):
                    pool.indirect_dma_start(out=dispatch, out_offset=bass.IndirectOffsetOnAxis(ap=slots_u[:, t, k:k + 1], axis=0),
                                            in_=xrow[:, t, :], in_offset=None).then_inc(sem("dispatched"), 16)

            fold_sums()
            for step_name, L, n in ORDER:
                if step_name == "tok":
                    tok_rstd(n)
                elif step_name == "ln":
                    ln_rstd(4 * n, 4 * n + 4)
                elif step_name == "gumbel":
                    gumbel()
                elif step_name == "D" and 0 <= n - 1 < T:
                    weigh(n - 1)
                elif step_name == "norm":
                    ln_rstd(*GROUPS[n])
                elif step_name == "scatter":
                    scatter(n)
            pool.wait_ge(sem("table_ready"), 1)
            total = pool.value_load(starts[0:1, NE:NE + 1], min_val=1, max_val=MAXT)
            link(nc.gpsimd.tensor_copy(number_u[:], numbers[:, T:T + 1]))
            pool.wait_ge(sem("sums_begun"), 16 * (T + 1))
            pool.indirect_dma_start(out=summed, out_offset=bass.IndirectOffsetOnAxis(ap=number_u[:, 0:1], axis=0),
                                    in_=padrow[:, 0:D], in_offset=None, compute_op=ALU.add).then_inc(sem("accumulated"), 16)
            with pool.Fori(0, total) as i:
                pool.wait_ge(free[0], i + (moe_base[0] + 1))
                pool.sem_inc(sem("adding"), 1)
                pool.indirect_dma_start(out=summed, out_offset=bass.IndirectOffsetOnAxis(ap=number_u[:, 0:1], axis=0),
                                        in_=mo_res, in_offset=None, compute_op=ALU.add).then_inc(sem("accumulated"), 16)

        @block.scalar
        def _(act):
            for c in range(FC):
                act.wait_ge(sem(f"in_pixels{c}"), 32)
                nc.scalar.activation(xsq[:, c], xf[:, c], ACT.Square).then_inc(sem("squares"), 1)

            AFFINE = {"A": None, "B": (COL["n1l"], COL["n1s"]), "M": (COL["n2l"], COL["n2s"]), "D": None}

            def transposed(L, n):
                for k in range(2):
                    ps = filled(act, L, "xT", n, k)
                    dst = xT[:, k, n * HALF:(n + 1) * HALF]
                    if AFFINE[L]:
                        c = AFFINE[L][n] + k
                        ins = nc.scalar.activation(dst, ps[0:HC, :], ACT.Identity, scale=cols_sb[:, c:c + 1], bias=cols_sb[:, c + 2:c + 3])
                    else:
                        ins = nc.scalar.activation(dst, ps[0:HC, :], ACT.Copy)
                    ins.then_inc(free_of(L, "xT", n, k), 1)

            def transposed_rows(t0, t1):
                for t in range(t0, t1):
                    ps = filled(act, "R", "xT", t)
                    nc.scalar.activation(xT[:, :, t * P:(t + 1) * P], ps[0:HC, 0:2 * P].rearrange("p (k x) -> p k x", k=2), ACT.Copy).then_inc(free_of("R", "xT", t), 1)

            def gate_exps(g):
                act.wait_ge(sem("gate_shifted"), 2 * g + 1)
                nc.scalar.activation(gview("G", "d"), gview("G", "d"), ACT.Exp).then_inc(sem("gate_exp"), 1)
                act.wait_ge(sem("gate_shifted"), 2 * g + 2)
                nc.scalar.activation(gview("E", "d"), gview("E", "d"), ACT.Exp).then_inc(sem("gate_exp"), 1)

            def store_qk(L, n):
                for o in range(4):
                    ps = filled(act, L, "qk", n, o)
                    if L == "A":
                        ins = nc.scalar.activation(qk[:, o, n, :], ps[0:HC, :], ACT.Identity, bias=cols_sb[:, COL["bqkA"] + o:COL["bqkA"] + o + 1])
                    else:
                        ins = nc.scalar.activation(qk[:, o, n, :], ps[0:HC, :], ACT.Copy)
                    ins.then_inc(free_of(L, "qk", n, o), 1)

            def store_v(L, n):
                for t in range(4 * n, 4 * n + 4):
                    ps = filled(act, L, "V", t)
                    nc.scalar.activation(V[:, t, :], ps[:, 0:D], ACT.Copy).then_inc(free_of(L, "V", t), 1)

            def exps(L, n):
                for f in range(2):
                    if L == "A":
                        act.wait_ge(sem("A_shifted"), 2 * n + f + 1)
                    else:
                        was_read(act, L, "score", n, f)
                    p = prob[:, f, n, :]
                    nc.scalar.activation(p, p, ACT.Exp, scale={"A": 1.0, "B": HD ** -0.5}[L]).then_inc(sem(f"{L}_exp"), 1)

            def attend(L, t):
                if 0 <= t - 1 < T:
                    ps = filled(act, L, "AV", t - 1)
                    if t - 1 >= 2:
                        act.wait_ge(full_of(L, "oT", t - 3), uses[L, "oT", t - 3][1] + 1)
                    nc.scalar.activation(osb[:, (t - 1) % 2, :], ps[:, 0:D], ACT.Copy).then_inc(free_of(L, "AV", t - 1), 1)
                if 0 <= t - 2 < T:
                    ps = filled(act, L, "oT", t - 2)
                    if t - 2 >= 2:
                        act.wait_ge(full_of(L, "proj", t - 4), uses[L, "proj", t - 4][1] + 1)
                    nc.scalar.activation(oT[:, t % 2, :, :].rearrange("p k x -> p (k x)"), ps[0:HC, 0:2 * P], ACT.Copy).then_inc(free_of(L, "oT", t - 2), 1)

            def hidden(n):
                for i in (3,) if n == 0 else (2, 1, 0):
                    for m in range(MC):
                        ps = filled(act, "fc1", i, m)
                        nc.scalar.activation(hT[i][:, m, :], ps[:, :], ACT.Gelu, bias=b1_sb[:, m:m + 1]).then_inc(free_of("fc1", i, m), 1)

            def store_qkv(n):
                for t in range(4 * n, 4 * n + 4):
                    ps = filled(act, "D", "qk", t)
                    nc.scalar.activation(qkD[:, t, :], ps[:, 0:2 * D], ACT.Copy).then_inc(free_of("D", "qk", t), 1)
                    ps = filled(act, "D", "V", t)
                    nc.scalar.activation(V[:, t, :], ps[:, 0:D], ACT.Copy).then_inc(free_of("D", "V", t), 1)

            def attend_heads(t):
                if t < T:
                    act.wait_ge(sem("D_shifted"), t + 1)
                    nc.scalar.activation(scD[t % 3], scD[t % 3], ACT.Exp, scale=(HD // 2) ** -0.5).then_inc(sem("D_exp"), 1)
                if 0 <= t - 2 < T:
                    q = t - 2
                    ps = filled(act, "D", "oT", q)
                    if q >= 2:
                        act.wait_ge(full_of("D", "proj", q - 2), uses["D", "proj", q - 2][1] + 1)
                    nc.scalar.activation(oT[:, q % 2, :, :].rearrange("p k x -> p (k x)"), ps[0:HC, 0:2 * P], ACT.Copy).then_inc(free_of("D", "oT", q), 1)

            loaded(act, "small")
            for step_name, L, n in ORDER:
                if step_name == "xT":
                    transposed(L, n)
                elif step_name == "qk":
                    store_qk(L, n)
                elif step_name == "V":
                    store_v(L, n)
                elif step_name == "front":
                    exps(L, n)
                elif step_name == "av":
                    attend(L, n)
                elif step_name == "fc1":
                    hidden(n)
                elif step_name == "lambda":
                    act.wait_ge(sem("lam_sums"), 1)
                    nc.scalar.activation(lam[:, 2:4], lam[:, 0:2], ACT.Exp).then_inc(sem("lam_exp"), 1)
                elif step_name == "qkv":
                    store_qkv(n)
                elif step_name == "D":
                    attend_heads(n)
                elif step_name == "norm":
                    transposed_rows(*GROUPS[n])
                elif step_name == "gates":
                    gate_exps(n)
            act.wait_ge(sem("table_ready"), 1)
            pad_experts(act, NE // 2, NE)

            def expert(u, e, first, end, reload):
                loads = act.snap((e - u) * (32 // AHEAD) + 32)
                b1 = mo_w2[u][:, MC * D:W2N]
                with act.Fori(first, end) as i:
                    act.wait_ge(sem(f"in_expert{u}"), loads)
                    act.wait_ge(full[0], i + moe_base[0])
                    for m in range(MC):
                        act.wait_ge(full[2 + m], i + (moe_base[2 + m] + 1))
                        nc.scalar.activation(mo_hT[:, m, :], bank[2 + m][:, 0:P], ACT.Gelu, bias=b1[:, m:m + 1]).then_inc(free[2 + m], 1)
                if reload:
                    act.wait_ge(full[0], first + moe_base[0])
                    load_expert(act, (u + AHEAD - 1) % AHEAD, e + AHEAD - 1)

            act.wait_ge(sem("table_ready"), 1)
            with act.Fori(0, NE // AHEAD - 1) as lot:
                bounds = expert_bounds(act, lot * AHEAD, AHEAD)
                for u in range(AHEAD):
                    expert(u, lot * AHEAD + u, bounds[u], bounds[u + 1], True)
            bounds = expert_bounds(act, NE - AHEAD, AHEAD)
            for u in range(AHEAD):
                expert(u, NE - AHEAD + u, bounds[u], bounds[u + 1], u == 0)

        @block.vector
        def _(dve):
            step = [0]

            def link(ins):
                step[0] += 1
                ins.then_inc(sem("dve_step"), 1)
                dve.wait_ge(sem("dve_step"), step[0])

            tt, ts, stt = nc.vector.tensor_tensor, nc.vector.tensor_scalar, nc.vector.scalar_tensor_tensor
            loaded(dve, "const")
            nc.vector.tensor_copy(weff[:, :, D:D + 1], cnt[:].unsqueeze(2)).then_inc(sem("means_column"), 1)
            for c in range(FC):
                dve.wait_ge(sem(f"in_pixels{c}"), 32)
                link(ts(out=weff[:, c, 0:D], in0=w5[:, c, 0, :], scalar1=gamma5[:, 0, c:c + 1], scalar2=None, op0=ALU.mult))
                for v in range(1, NSH):
                    ins = stt(out=weff[:, c, 0:D], in0=w5[:, c, v, :], scalar=gamma5[:, v, c:c + 1], in1=weff[:, c, 0:D], op0=ALU.mult, op1=ALU.add)
                    if v < NSH - 1:
                        link(ins)
                ins.then_inc(sem("weff"), 1)

            def tokenize(n):
                if n == 0:
                    filled(dve, "tok", 0)
                    filled(dve, "tok", 1)
                    nc.vector.tensor_copy(cbias[:], bank[0][:, 256:256 + D])
                    link(nc.vector.tensor_copy(colsum[:], bank[1][:, 256:256 + D]))
                s = slice(4 * n, 4 * n + 4)
                for t in range(4 * n, 4 * n + 4):
                    ps = filled(dve, "tok", t)
                    ins = nc.vector.tensor_copy(tokst[:, t, 0:2], ps[:, D:D + 2])
                link(ins)
                link(tt(out=tokst[:, s, 2:3], in0=tokst[:, s, 0:1], in1=tokst[:, s, 0:1], op=ALU.mult))
                link(tt(out=tokst[:, s, 2:3], in0=tokst[:, s, 1:2], in1=tokst[:, s, 2:3], op=ALU.subtract))
                ts(out=tokst[:, s, 2:3], in0=tokst[:, s, 2:3], scalar1=EPS_LN, scalar2=None, op0=ALU.add).then_inc(sem("tokvar"), 1)
                dve.wait_ge(sem("tokrstd"), n + 1)
                link(ts(out=tokst[:, s, 3:4], in0=tokst[:, s, 3:4], scalar1=-1.0, scalar2=None, op0=ALU.mult))
                for t in range(4 * n, 4 * n + 5):
                    if t < 4 * n + 4:
                        ps = bank[uses["tok", t][0]]
                        stt(out=tmpt[:, t % 2, :], in0=colsum[:], scalar=tokst[:, t, 0:1], in1=ps[:, 0:D], op0=ALU.mult, op1=ALU.subtract).then_inc(free_of("tok", t), 1)
                    if t > 4 * n:
                        q = t - 1
                        was_read(dve, "tok", q)
                        link(stt(out=h[:, q, :], in0=tmpt[:, q % 2, :], scalar=tokst[:, q, 3:4], in1=cbias[:], op0=ALU.mult, op1=ALU.add))

            ln = [0]

            def ln_stats(src, t0, t1):
                for t in range(t0, t1):
                    ins = nc.vector.bn_stats(out=stats[:, t, :], in_=src[:, t, :])
                link(ins)
                for t in range(t0, t1):
                    ins = nc.vector.bn_aggr(out=mv[:, t, :], in_=stats[:, t, :])
                ins.then_inc(sem("ln_stats"), 1)
                ln[0] += 1
                dve.wait_ge(sem("ln_rstd"), ln[0])

            STREAMS = {"A": (h, xn), "z": (h, z), "B": (z, xn), "M": (z, xn), "D": (h, xn)}

            def layernorm(L, n):
                src, dst = STREAMS[L]
                if L == "z":
                    was_read(dve, "A", "proj", 4 * n + 2)
                    was_read(dve, "A", "proj", 4 * n + 3)
                elif L == "B":
                    dve.wait_ge(sem("normed_z"), 4 * n + 4)
                elif L == "M":
                    was_read(dve, "B", "proj", 4 * n + 2)
                    was_read(dve, "B", "proj", 4 * n + 3)
                ln_stats(src, 4 * n, 4 * n + 4)
                for t in range(4 * n, 4 * n + 4):
                    ts(out=dst[:, t, :], in0=src[:, t, :], scalar1=mv[:, t, 0:1], scalar2=rstd[:, t:t + 1],
                       op0=ALU.subtract, op1=ALU.mult).then_inc(sem(f"normed_{L}"), 1)

            def spread(L, n, f):
                was_read(dve, L, "qk", n, f)
                for hh in range(QH):
                    ins = ts(out=qbd[2 * n + f][:, :, hh, :], in0=qk[:, f, n, :].rearrange("p (b i) -> p b i", i=NTOK),
                             scalar1=headmask[:, hh:hh + 1], scalar2=None, op0=ALU.mult)
                ins.then_inc(sem(f"{L}_spread"), 1)

            def softmax_front(L, n, f):
                ps = filled(dve, L, "score", n, f)
                sc = ps[0:HC, :].rearrange("p (b j) -> p b j", j=NTOK)
                p = prob[:, f, n, :].rearrange("p (b j) -> p b j", j=NTOK)
                if L == "A":
                    stt(out=p, in0=sc, scalar=cols_sb[:, COL["scaleA"] + f:COL["scaleA"] + f + 1], in1=repeat(selfmask[:], 1, IB), op0=ALU.mult, op1=ALU.add).then_inc(free_of(L, "score", n, f), 1)
                    was_read(dve, L, "score", n, f)
                    sc = p
                link(nc.vector.reduce_max(smx[:, f, :], sc, AX_X))
                tt(out=p, in0=sc, in1=repeat(smx[:, f, :], 2, NTOK), op=ALU.subtract).then_inc(sem("A_shifted") if L == "A" else free_of(L, "score", n, f), 1)

            def softmax_back(L, n, f):
                p = prob[:, f, n, :].rearrange("p (b j) -> p b j", j=NTOK)
                dve.wait_ge(sem(f"{L}_exp"), 2 * n + f + 1)
                link(nc.vector.reduce_sum(ssum[:, f, :], p, AX_X))
                link(nc.vector.reciprocal(srec[:, f, :], ssum[:, f, :]))
                tt(out=p, in0=p, in1=repeat(srec[:, f, :], 2, NTOK), op=ALU.mult).then_inc(sem(f"{L}_probs"), 1)

            def attend(L, t):
                res = {"A": h, "B": z}[L]
                if t < T:
                    ps = filled(dve, L, "PT", t)
                    if t >= 2:
                        dve.wait_ge(full_of(L, "AV", t - 2), uses[L, "AV", t - 2][1] + 1)
                    src = ps[:, 0:D].rearrange("p (h i) -> p h i", i=NTOK)
                    tt(out=ptbd[t % 2], in0=repeat(src, 2, QB),
                       in1=repeat(repeat(blockmask[:], 1, H), 3, NTOK), op=ALU.mult).then_inc(free_of(L, "PT", t), 1)
                if t >= 3:
                    ps = filled(dve, L, "proj", t - 3)
                    tt(out=res[:, t - 3, :], in0=ps[:, 0:D], in1=res[:, t - 3, :], op=ALU.add).then_inc(free_of(L, "proj", t - 3), 1)

            def add_ffn(n):
                for t in range(4 * n, 4 * n + 5):
                    if t < 4 * n + 4:
                        ps = filled(dve, "fc2", t)
                        tt(out=z[:, t, :], in0=ps[:, 0:D], in1=z[:, t, :], op=ALU.add).then_inc(free_of("fc2", t), 1)
                    if t > 4 * n:
                        q = t - 1
                        was_read(dve, "fc2", q)
                        ins = tt(out=h[:, q, :], in0=z[:, q, :], in1=h[:, q, :], op=ALU.add)
                link(ins)

            def find_lambda():
                for s in range(2):
                    link(tt(out=lamv[:, 2 * s, :], in0=lamv[:, 2 * s, :], in1=lamv[:, 2 * s + 1, :], op=ALU.mult))
                    ins = nc.vector.reduce_sum(lam[:, s:s + 1], lamv[:, 2 * s, :], AX_X)
                    if s == 0:
                        link(ins)
                    else:
                        ins.then_inc(sem("lam_sums"), 1)
                dve.wait_ge(sem("lam_exp"), 1)
                link(tt(out=lam[:, 4:5], in0=lam[:, 3:4], in1=lam[:, 2:3], op=ALU.subtract))
                link(ts(out=lam[:, 5:6], in0=lam[:, 4:5], scalar1=LAMBDA_INIT, scalar2=None, op0=ALU.subtract))
                link(ts(out=lam[:, 7:8], in0=lam[:, 5:6], scalar1=1.0 - LAMBDA_INIT, scalar2=None, op0=ALU.mult))
                link(nc.vector.memset(headfac[:], 1.0))
                link(ts(out=headfac[:, 1, :], in0=headfac[:, 1, :], scalar1=lam[:, 7:8], scalar2=None, op0=ALU.mult))
                link(ts(out=headfac[:, 0, :], in0=headfac[:, 0, :], scalar1=1.0 - LAMBDA_INIT, scalar2=None, op0=ALU.mult))

            def top_gates(which, lg, R, n, k, order):
                a4 = cmpa[:, 0:R * n * n].rearrange("p (r a b) -> p r a b", a=n, b=n)
                b4 = cmpb[:, 0:R * n * n].rearrange("p (r a b) -> p r a b", a=n, b=n)
                other, own = repeat(lg, 2, n), repeat(lg, 3, n)
                link(tt(out=a4, in0=other, in1=own, op=ALU.is_gt))
                link(tt(out=b4, in0=other, in1=own, op=ALU.is_equal))
                low = tri[:].rearrange("p (a b) -> p a b", b=E)[:, 0:n, 0:n]
                link(tt(out=b4, in0=b4, in1=repeat(low, 1, R), op=ALU.mult))
                link(tt(out=a4, in0=a4, in1=b4, op=ALU.add))
                chosen, d, mx = gview(which, "sel"), gview(which, "d"), gview(which, "mx")
                link(nc.vector.reduce_sum(chosen, a4, AX_X))
                link(ts(out=chosen, in0=chosen, scalar1=float(k), scalar2=None, op0=ALU.is_lt))
                link(nc.vector.reduce_max(mx, lg, AX_X))
                tt(out=d, in0=lg, in1=repeat(mx, 2, n), op=ALU.subtract).then_inc(sem("gate_shifted"), 1)
                dve.wait_ge(sem("gate_exp"), order)
                link(tt(out=d, in0=d, in1=chosen, op=ALU.mult))
                link(nc.vector.reduce_sum(mx, d, AX_X))
                link(nc.vector.reciprocal(mx, mx))
                link(tt(out=d, in0=d, in1=repeat(mx, 2, n), op=ALU.mult))
                link(stt(out=d, in0=d, scalar=EPS_GATE, in1=d, op0=ALU.is_ge, op1=ALU.mult))

            def normalize_rows(t0, t1):
                for t in range(t0, t1):
                    was_read(dve, "D", "proj", t)
                ln_stats(h, t0, t1)
                for t in range(t0, t1):
                    ts(out=xrow[:, t, 0:D], in0=h[:, t, :], scalar1=mv[:, t, 0:1], scalar2=rstd[:, t:t + 1],
                       op0=ALU.subtract, op1=ALU.mult).then_inc(sem("normed_R"), 1)

            def gates(g, t0, t1):
                R = t1 - t0
                if g == 0:
                    link(nc.vector.memset(earlier[:, 0, :], 0.0))
                for t in range(t0, t1):
                    ps = filled(dve, "logit", t)
                    nc.vector.tensor_copy(lgG[:, t - t0, :], ps[:, 0:G])
                    nc.vector.tensor_copy(lgE[:, (t - t0) * G:(t - t0 + 1) * G, :], ps[:, G:G + NE].rearrange("p (g e) -> p g e", g=G)).then_inc(free_of("logit", t), 1)
                was_read(dve, "logit", t1 - 2)
                was_read(dve, "logit", t1 - 1)
                top_gates("G", lgG, R, G, KG, 2 * g + 1)
                top_gates("E", lgE, R * G, E, KE, 2 * g + 2)
                for name, dst in (("sel", sel[:, t0:t1, :]), ("d", xrow[:, t0:t1, D + 1:ROWN])):
                    for q in range(R):
                        ins = tt(out=dst[:, q, :].rearrange("p (g e) -> p g e", g=G), in0=gview("E", name)[:, q * G:(q + 1) * G, :],
                                 in1=repeat(gview("G", name)[:, q, :], 2, E), op=ALU.mult)
                    link(ins)
                for t in range(t0, t1):
                    ins = tt(out=earlier[:, t + 1, :], in0=earlier[:, t, :], in1=sel[:, t, :], op=ALU.add)
                    if t < t1 - 1:
                        link(ins)
                ins.then_inc(sem("chosen"), 1)

            def slots(g, t0, t1):
                R = t1 - t0
                ps = filled(dve, "place", g)
                place = ps[:, 0:R * NE].rearrange("p (t e) -> p t e", t=R)
                tt(out=key[:, 0:R, :], in0=place, in1=repeat(slot1[:], 1, R), op=ALU.add).then_inc(free_of("place", g), 1)
                was_read(dve, "place", g)
                link(tt(out=key[:, 0:R, :], in0=key[:, 0:R, :], in1=sel[:, t0:t1, :], op=ALU.mult))
                for t in range(t0, t1):
                    ins = nc.vector.max(out=top8[:, t, :], in_=key[:, t - t0, :])
                link(ins)
                ts(out=slots_u[:, t0:t1, :], in0=top8[:, t0:t1, :], scalar1=1.0, scalar2=None, op0=ALU.subtract).then_inc(sem("slots_ready"), 1)

            def sums_begin(t0, t1):
                for t in range(t0, t1):
                    ps = filled(dve, "cT", t)
                    nc.vector.tensor_copy(cT[:, t, :], ps[0:NE, 0:P]).then_inc(free_of("cT", t), 1)
                    ps = filled(dve, "y0", t)
                    tt(out=y[:, t, :], in0=ps[:, 0:D], in1=h[:, t, :], op=ALU.add).then_inc(free_of("y0", t), 1)

            def count_tiles():
                ps = filled(dve, "counts")
                nc.vector.tensor_copy(tiles_f[:, 0, :], ps[:, 0:NE]).then_inc(free_of("counts"), 1)
                was_read(dve, "counts")
                link(nc.vector.tensor_copy(counts[:], tiles_f[:, 0, :]))
                link(tt(out=tilecmp, in0=repeat(tiles_f[:, 0, :], 2, T - 1), in1=repeat(steps[:], 1, NE), op=ALU.is_gt))
                link(nc.vector.reduce_sum(tiles_f[:, 1, :], tilecmp, AX_X))
                link(ts(out=tiles_f[:, 1, :], in0=tiles_f[:, 1, :], scalar1=1.0, scalar2=None, op0=ALU.add))
                link(nc.vector.tensor_tensor_scan(out=tiles_f[:, 2, :], data0=ones[:, 0:NE], data1=tiles_f[:, 1, :], initial=0.0, op0=ALU.mult, op1=ALU.add))
                link(nc.vector.tensor_copy(starts[:, 1:NE + 1], tiles_f[:, 2, :]))
                dve.wait_ge(sem("pad_ready"), 2)
                nc.vector.memset(starts[:, 0:1], 0).then_inc(sem("table_ready"), 1)

            def attend_heads(t):
                if t < T:
                    was_read(dve, "D", "qk", t)
                    q = qkD[:, t, 0:D].rearrange("p (h x) -> p h x", h=H)
                    k = qkD[:, t, D:2 * D].rearrange("p (h x) -> p h x", h=H)
                    pr = prodS[t % 2].rearrange("p (a b x) -> p a b x", a=H, b=H)
                    link(tt(out=pr, in0=repeat(q, 2, H), in1=repeat(k, 1, H), op=ALU.mult))
                    sc, mx = scD[t % 3], mxD[t % 3]
                    link(nc.vector.reduce_sum(sc.rearrange("p (s y) -> p y s", s=2), prodS[t % 2].rearrange("p (y s x) -> p y s x", s=2, x=HD // 2), AX_X))
                    sc3 = sc.rearrange("p (s x) -> p s x", x=H)
                    link(nc.vector.reduce_max(mx, sc3, AX_X))
                    tt(out=sc3, in0=sc3, in1=repeat(mx, 2, H), op=ALU.subtract).then_inc(sem("D_shifted"), 1)
                if 0 <= t - 1 < T:
                    q = t - 1
                    sc, mx = scD[q % 3], mxD[q % 3]
                    sc3 = sc.rearrange("p (s x) -> p s x", x=H)
                    dve.wait_ge(sem("D_exp"), q + 1)
                    link(nc.vector.reduce_sum(mx, sc3, AX_X))
                    link(nc.vector.reciprocal(mx, mx))
                    link(tt(out=mx, in0=mx, in1=headfac[:].rearrange("p s h -> p (s h)"), op=ALU.mult))
                    link(tt(out=sc3, in0=sc3, in1=repeat(mx, 2, H), op=ALU.mult))
                    if q >= 2:
                        dve.wait_ge(sem("D_weighed"), q - 1)
                    tt(out=peff[q % 2], in0=sc[:, 0:H * H], in1=sc[:, H * H:2 * H * H], op=ALU.add).then_inc(sem("D_probs"), 1)
                if 0 <= t - 2 < T:
                    q = t - 2
                    dve.wait_ge(sem("D_weighed"), q + 1)
                    if q >= 2:
                        dve.wait_ge(full_of("D", "oT", q - 2), uses["D", "oT", q - 2][1] + 1)
                    nc.vector.reduce_sum(oD[q % 2], prodV[q % 2].rearrange("p (y x) -> p y x", x=H), AX_X).then_inc(sem("D_rows"), 1)
                if t >= 3:
                    q = t - 3
                    ps = filled(dve, "D", "proj", q)
                    tt(out=h[:, q, :], in0=ps[:, 0:D], in1=h[:, q, :], op=ALU.add).then_inc(free_of("D", "proj", q), 1)

            for step_name, L, n in ORDER:
                if step_name == "tok":
                    tokenize(n)
                elif step_name == "ln":
                    layernorm(L, n)
                elif step_name == "qk":
                    loaded(dve, "small")
                    for f in range(2):
                        spread(L, n, f)
                elif step_name == "front":
                    for f in range(2):
                        softmax_front(L, n, f)
                elif step_name == "back":
                    for f in range(2):
                        softmax_back(L, n, f)
                elif step_name == "av":
                    attend(L, n)
                elif step_name == "ffn":
                    add_ffn(n)
                elif step_name == "lambda":
                    find_lambda()
                elif step_name == "D":
                    attend_heads(n)
                elif step_name == "norm":
                    normalize_rows(*GROUPS[n])
                elif step_name == "gates":
                    gates(n, *GROUPS[n])
                elif step_name == "slots":
                    slots(n, *GROUPS[n])
                elif step_name == "counts":
                    count_tiles()
                elif step_name == "begin":
                    sums_begin(*GROUPS[n])
            dve.wait_ge(sem("table_ready"), 1)
            nc.vector.memset(mo_meta, 0.0).then_inc(sem("rows_free"), 1)
            dve.wait_ge(sem("rows_free"), 1)

            def take_rows(i):
                dve.wait_ge(full[1], i + (moe_base[1] + 1))
                nc.vector.tensor_copy(mo_xT.rearrange("p k t -> p (k t)"), bank[1][0:HC, 0:2 * P]).then_inc(free[1], 1)
                if not isinstance(i, int):
                    dve.wait_ge(free[0], i + (moe_base[0] - 1))
                nc.vector.tensor_copy(mo_meta[:, bass.ds(i % 2 * META, META)], mo_x[:, D:ROWN]).then_inc(sem("rows_free"), 1)

            take_rows(0)
            with dve.Fori(0, NE) as e:
                first = dve.value_load(starts[0:1, bass.ds(e, 1)], min_val=0, max_val=MAXT - 1)
                end = dve.value_load(starts[0:1, bass.ds(e + 1, 1)], min_val=1, max_val=MAXT)
                with dve.Fori(first, end) as i:
                    take_rows(i + 1)
                    dve.wait_ge(sem("rows_free"), i + 2)
                    dve.wait_ge(sem("accumulated"), i * 16 + ACC0)
                    meta = i % 2 * META
                    nc.vector.tensor_copy(number_u[:], mo_meta[:, bass.ds(meta, 1)])
                    dve.wait_ge(full[0], i + (moe_base[0] + 1))
                    ts(out=mo_res, in0=bank[0][:, 0:D], scalar1=mo_meta[:, bass.ds(meta + e + 1, 1)], scalar2=None, op0=ALU.mult).then_inc(free[0], 1)

        @block.tensor
        def _(pe):
            mm = nc.tensor.matmul
            pe.wait_ge(sem("ones_set"), 2)
            loaded(pe, "const")

            def tokenize():
                pe.wait_ge(sem("means_column"), 1)
                for c in range(FC):
                    pe.wait_ge(sem("weff"), c + 1)
                    for t in range(T):
                        ps = claim("tok", t) if c == 0 else bank[t]
                        mm(ps[:, 0:D + 1], xf[:, c, t * P:(t + 1) * P], weff[:, c, :], start=(c == 0), stop=(c == FC - 1))
                    if c == FC - 1:
                        pe.wait_ge(sem("fold_summed"), 1)
                        loaded(pe, "small")
                        for v in range(NSH):
                            mm(bank[0][:, 256:256 + D], ones[0:FP, :], betasum[:, v, :], start=False, stop=False, skip_group_check=True)
                        mm(bank[0][:, 256:256 + D], ones[0:1, :], row("tokb"), start=False, stop=True, skip_group_check=True)
                        mm(bank[1][:, 256:256 + D], ones[0:FP, :], foldsum, start=False, stop=True, skip_group_check=True)
                    pe.wait_ge(sem("squares"), c + 1)
                    for t in range(T):
                        ins = mm(bank[t][:, D + 1:D + 2], xsq[:, c, t * P:(t + 1) * P], cnt[:, c:c + 1], start=False, stop=(c == FC - 1), skip_group_check=True)
                        if c == FC - 1:
                            ins.then_inc(full_of("tok", t), 1)

            def transposes(L, n):
                for k in range(2):
                    ps = claim(L, "xT", n, k)
                    for j in range(4):
                        t = 4 * n + j
                        if k == 0:
                            pe.wait_ge(sem(f"normed_{L}"), t + 1)
                        ins = nc.tensor.transpose(ps[0:HC, j * P:(j + 1) * P], xn[:, t, k * HC:(k + 1) * HC], ident[:])
                    ins.then_inc(full_of(L, "xT", n, k), 1)

            def queries_keys(L, n):
                W = weights[L]
                loaded(pe, L)
                for k in range(2):
                    was_read(pe, L, "xT", n, k)
                for o in range(4):
                    ps = claim(L, "qk", n, o)
                    for k in range(2):
                        ins = mm(ps[0:HC, :], W[:, k, o * HC:(o + 1) * HC], xT[:, k, n * HALF:(n + 1) * HALF], start=(k == 0), stop=(k == 1))
                    ins.then_inc(full_of(L, "qk", n, o), 1)

            def values(L, n):
                W = weights[L]
                for t in range(4 * n, 4 * n + 4):
                    ps = claim(L, "V", t)
                    for k in range(2):
                        ins = mm(ps[:, 0:D], xT[:, k, t * P:(t + 1) * P], W[:, k, 2 * D:3 * D], start=(k == 0), stop=(k == 1 and L != "A"))
                    if L == "A":
                        ins = mm(ps[:, 0:D], ones[0:1, :], rows_sb[0:1, ROW["bqkvA"] + 2 * D:ROW["bqkvA"] + 3 * D], start=False, stop=True)
                    ins.then_inc(full_of(L, "V", t), 1)

            def scores(L, n):
                for f in range(2):
                    pe.wait_ge(sem(f"{L}_spread"), 2 * n + f + 1)
                    was_read(pe, L, "qk", n, 2 + f)
                    ps = claim(L, "score", n, f)
                    for b in range(IB):
                        for r in range(0, HC, QUAD):
                            ins = mm(ps[r:r + QUAD, b * NTOK:(b + 1) * NTOK], qbd[2 * n + f][r:r + QUAD, b, :, :].rearrange("p h i -> p (h i)"),
                                     qk[r:r + QUAD, 2 + f, n, b * NTOK:(b + 1) * NTOK], start=True, stop=True)
                    ins.then_inc(full_of(L, "score", n, f), 1)

            def attend(L, t):
                if t < T:
                    n = t // 4
                    pe.wait_ge(sem(f"{L}_probs"), 2 * n + 2)
                    ps = claim(L, "PT", t)
                    for f in range(2):
                        ins = nc.tensor.transpose(ps[:, f * HC:(f + 1) * HC], prob[:, f, n, (t % 4) * P:(t % 4 + 1) * P], ident[0:HC, 0:HC])
                    ins.then_inc(full_of(L, "PT", t), 1)
                if 0 <= t - 1 < T:
                    q = t - 1
                    was_read(pe, L, "PT", q)
                    was_read(pe, L, "V", q)
                    ps = claim(L, "AV", q)
                    for hh in range(H):
                        for r in range(0, P, QUAD):
                            ins = mm(ps[r:r + QUAD, hh * HD:(hh + 1) * HD], ptbd[q % 2][r:r + QUAD, hh, :, :].rearrange("p b i -> p (b i)"),
                                     V[r:r + QUAD, q, hh * HD:(hh + 1) * HD], start=True, stop=True)
                    ins.then_inc(full_of(L, "AV", q), 1)
                if 0 <= t - 2 < T:
                    q = t - 2
                    was_read(pe, L, "AV", q)
                    ps = claim(L, "oT", q)
                    for k in range(2):
                        ins = nc.tensor.transpose(ps[0:HC, k * P:(k + 1) * P], osb[:, q % 2, k * HC:(k + 1) * HC], ident[:])
                    ins.then_inc(full_of(L, "oT", q), 1)
                if 0 <= t - 3 < T:
                    q = t - 3
                    was_read(pe, L, "oT", q)
                    ps = claim(L, "proj", q)
                    wo = wout["S"] if L == "B" and q >= T // 2 else wout[L]
                    if L == "B" and q == T // 2:
                        pe.wait_ge(sem("small_weights"), 3)
                    for k in range(2):
                        mm(ps[:, 0:D], oT[:, q % 2, k, :], wo[:, k, :], start=(k == 0), stop=False)
                    mm(ps[:, 0:D], ones[0:1, :], row("boutA" if L == "A" else "boutB" if q < T // 2 else "boutS"), start=False, stop=True).then_inc(full_of(L, "proj", q), 1)

            def hidden(n):
                for k in range(2):
                    was_read(pe, "M", "xT", n, k)
                if n == 0:
                    loaded(pe, "mlp")
                    for m in range(MC):
                        ps = claim("fc1", 3, m)
                        for k in range(2):
                            ins = mm(ps[:, :], w1[:, k, m * P:(m + 1) * P], xT[:, k, 0:HALF], start=(k == 0), stop=(k == 1))
                        ins.then_inc(full_of("fc1", 3, m), 1)
                else:
                    for i, p0, p1, k in ((2, 0, KEEP[2], 0), (1, KEEP[2], KEEP[1], 0), (0, 0, HC, 1)):
                        for m in range(MC):
                            ps = claim("fc1", i, m)
                            mm(ps[:, :], w1[p0:p1, k, m * P:(m + 1) * P], xT[p0:p1, k, HALF:TOK], start=(i == 2), stop=True, skip_group_check=(i != 2)).then_inc(full_of("fc1", i, m), 1)

            def ffn_out(n):
                for t in range(4 * n, 4 * n + 4):
                    ps = claim("fc2", t)
                    col = slice((t % 4) * P, (t % 4 + 1) * P)
                    if n == 0:
                        for m in range(MC):
                            was_read(pe, "fc1", 3, m)
                            mm(ps[:, 0:D], hT[3][:, m, col], w2[:, m, :], start=(m == 0), stop=False)
                        mm(ps[:, 0:D], ones[0:1, :], row("b2"), start=False, stop=True).then_inc(full_of("fc2", t), 1)
                    else:
                        mm(ps[:, 0:D], ones[0:1, :], row("b2S"), start=True, stop=False)
                        for i in (2, 1, 0):
                            for m in range(MC):
                                was_read(pe, "fc1", i, m)
                                ins = mm(ps[:, 0:KEEP[i]], hT[i][:, m, col], w2s[i][:, m, :], start=False, stop=(i == 0 and m == MC - 1))
                        ins.then_inc(full_of("fc2", t), 1)

            def queries_keys_values(n):
                loaded(pe, "D")
                W = weights["D"]
                for k in range(2):
                    was_read(pe, "D", "xT", n, k)
                for t in range(4 * n, 4 * n + 4):
                    for name, c0, c1 in (("qk", 0, 2 * D), ("V", 2 * D, 3 * D)):
                        ps = claim("D", name, t)
                        for k in range(2):
                            ins = mm(ps[:, 0:c1 - c0], xT[:, k, t * P:(t + 1) * P], W[:, k, c0:c1], start=(k == 0), stop=(k == 1))
                        ins.then_inc(full_of("D", name, t), 1)

            def attend_heads(t):
                if 0 <= t - 2 < T:
                    q = t - 2
                    pe.wait_ge(sem("D_rows"), q + 1)
                    ps = claim("D", "oT", q)
                    for k in range(2):
                        ins = nc.tensor.transpose(ps[0:HC, k * P:(k + 1) * P], oD[q % 2][:, k * HC:(k + 1) * HC], ident[:])
                    ins.then_inc(full_of("D", "oT", q), 1)
                    was_read(pe, "D", "oT", q)
                    ps = claim("D", "proj", q)
                    for k in range(2):
                        ins = mm(ps[:, 0:D], oT[:, q % 2, k, :], wout["D"][:, k, :], start=(k == 0), stop=(k == 1))
                    ins.then_inc(full_of("D", "proj", q), 1)

            def logits(t0, t1):
                for t in range(t0, t1):
                    pe.wait_ge(sem("normed_R"), t + 1)
                    ps = claim("R", "xT", t)
                    for k in range(2):
                        ins = nc.tensor.transpose(ps[0:HC, k * P:(k + 1) * P], xrow[:, t, k * HC:(k + 1) * HC], ident[:])
                    ins.then_inc(full_of("R", "xT", t), 1)
                for t in range(t0, t1):
                    was_read(pe, "R", "xT", t)
                    ps = claim("logit", t)
                    for k in range(2):
                        mm(ps[:, 0:G + NE], xT[:, k, t * P:(t + 1) * P], wr[:, k, :], start=(k == 0), stop=False)
                    mm(ps[:, 0:G + NE], ones[0:1, :], row("route", G + NE), start=False, stop=True).then_inc(full_of("logit", t), 1)

            def places(g, t0, t1):
                pe.wait_ge(sem("chosen"), g + 1)
                ps = claim("place", g)
                mm(ps[:, 0:(t1 - t0) * NE], ones[:], earlier[:, t0:t1, :], start=True, stop=False)
                mm(ps[:, 0:(t1 - t0) * NE], prefix[:], sel[:, t0:t1, :], start=False, stop=True).then_inc(full_of("place", g), 1)

            def sums_begin(t0, t1):
                for t in range(t0, t1):
                    ps = claim("cT", t)
                    nc.tensor.transpose(ps[0:NE, 0:P], xrow[:, t, D + 1:ROWN], ident[:]).then_inc(full_of("cT", t), 1)
                    was_read(pe, "cT", t)
                    ps = claim("y0", t)
                    mm(ps[:, 0:D], cT[:, t, :], b2all[:], start=True, stop=True).then_inc(full_of("y0", t), 1)

            for step_name, L, n in ORDER:
                if step_name == "tok" and n == 0:
                    tokenize()
                elif step_name == "xT":
                    transposes(L, n)
                elif step_name == "qk":
                    queries_keys(L, n)
                elif step_name == "V":
                    values(L, n)
                elif step_name == "front":
                    scores(L, n)
                elif step_name == "av":
                    attend(L, n)
                elif step_name == "fc1":
                    hidden(n)
                elif step_name == "fc2":
                    ffn_out(n)
                elif step_name == "qkv":
                    queries_keys_values(n)
                elif step_name == "D":
                    attend_heads(n)
                elif step_name == "norm":
                    logits(*GROUPS[n])
                elif step_name == "slots":
                    places(n, *GROUPS[n])
                elif step_name == "counts":
                    mm(claim("counts")[:, 0:NE], ones[:], earlier[:, T, :], start=True, stop=True).then_inc(full_of("counts"), 1)
                elif step_name == "begin":
                    sums_begin(*GROUPS[n])

            def transpose_rows(i):
                pe.wait_ge(sem("rows_in"), i * 16 + 16)
                for k in range(2):
                    ins = nc.tensor.transpose(bank[1][0:HC, k * P:(k + 1) * P], mo_x[:, k * HC:(k + 1) * HC], ident[:])
                ins.then_inc(full[1], 1)

            pe.wait_ge(free[1], moe_base[1])
            pe.wait_ge(sem("table_ready"), 1)
            transpose_rows(0)

            def expert(u, e, first, end):
                loads = pe.snap((e - u) * (32 // AHEAD) + 32)
                w1e = mo_w1[u].rearrange("p (k m) -> p k m", k=2)
                w2e = mo_w2[u][:, 0:MC * D].rearrange("p (m d) -> p m d", m=MC)
                with pe.Fori(first, end) as i:
                    pe.wait_ge(sem(f"in_expert{u}"), loads)
                    pe.wait_ge(free[1], i + (moe_base[1] + 1))
                    for m in range(MC):
                        pe.wait_ge(free[2 + m], i + moe_base[2 + m])
                        for k in range(2):
                            ins = mm(bank[2 + m][:, 0:P], w1e[:, k, m * P:(m + 1) * P], mo_xT[:, k, :], start=(k == 0), stop=(k == 1))
                        ins.then_inc(full[2 + m], 1)
                    transpose_rows(i + 1)
                    pe.wait_ge(free[0], i + moe_base[0])
                    for m in range(MC):
                        pe.wait_ge(free[2 + m], i + (moe_base[2 + m] + 1))
                        ins = mm(bank[0][:, 0:D], mo_hT[:, m, :], w2e[:, m, :], start=(m == 0), stop=(m == MC - 1))
                    ins.then_inc(full[0], 1)

            with pe.Fori(0, NE // AHEAD) as lot:
                bounds = expert_bounds(pe, lot * AHEAD, AHEAD)
                for u in range(AHEAD):
                    expert(u, lot * AHEAD + u, bounds[u], bounds[u + 1])
        for k, v in lots.items():
            assert v == LOT[k], (k, v)


def kernel(**inputs):
    import concourse.bacc as bacc
    from concourse.bass_utils import run_bass_kernel_spmd

    f32 = np.float32
    i = {k: np.asarray(v) for k, v in inputs.items()}

    order, rows = pixel_layout()
    padded = np.pad(i["x"], ((0, 0), (0, 0), (1, 1), (1, 1)))
    xf = np.empty((NF, B, SIDE, SIDE), f32)
    for f, (c, r, w) in enumerate(order):
        xf[f] = padded[:, c, r + 1:r + 1 + IMG:PATCH, w + 1:w + 1 + IMG:PATCH][:, :SIDE, :SIDE]
    xf = xf.reshape(FC, FP, TOK)

    def by_shift(a):
        a = np.concatenate([a, np.zeros((1,) + a.shape[1:], a.dtype)])
        return a[rows]

    w5 = by_shift(i["L0_tok_w"]).reshape(NSH, FC, FP, D).transpose(1, 2, 0, 3)
    arr = {
        "xf": xf, "w5": w5,
        "gamma5": by_shift(i["L0_tok_ln_gamma"]).reshape(NSH, FC, FP).transpose(2, 0, 1),
        "beta5": by_shift(i["L0_tok_ln_beta"]).reshape(NSH, FC, FP).transpose(2, 0, 1),
        "cnt": ((rows >= 0).sum(0) / NPATCH).astype(f32).reshape(FC, FP).T,
        "ident": np.eye(P, dtype=f32),
        "blockmask": (np.arange(P)[:, None] // NTOK % QB == np.arange(QB)[None, :]).astype(f32),
        "wqkvA": i["L0_attn_w_qkv"], "woutA": i["L0_attn_w_proj"],
        "wqkvB": i["L0_ffn_w_qkv"], "woutB": i["L0_ffn_w_proj"],
        "wqkvD": i["L1_attn_W_attn"].T, "woutD": i["L1_attn_W_out"].T,
        "gum": i["L0_ffn_gumbel_weights"].reshape(1, 3),
        "lamv": np.stack([i["L1_attn_lambda_q1"], i["L1_attn_lambda_k1"], i["L1_attn_lambda_q2"], i["L1_attn_lambda_k2"]])[None],
        "b1": i["L0_ffn_b_fc1"].reshape(MC, P).T, "w1": i["L0_ffn_w_fc1"], "w2": i["L0_ffn_w_fc2"],
        "wr": np.concatenate([i["L1_ffn_Wg"], i["L1_ffn_We"].transpose(1, 0, 2).reshape(D, NE)], 1),
        "moe_w1": i["L1_ffn_W1"].reshape(NE, 2, HC, HID).transpose(0, 2, 1, 3).reshape(NE, HC, 2 * HID),
        "moe_w2": np.concatenate([i["L1_ffn_W2"].reshape(NE, MC, P, D).transpose(0, 2, 1, 3).reshape(NE, P, MC * D),
                                  i["L1_ffn_b1"].reshape(NE, MC, P).transpose(0, 2, 1)], 2),
        "moe_b2": i["L1_ffn_b2"].reshape(NE, D),
    }
    c = np.arange(HC)
    arr["headmask"] = (c[:, None] // HD % QH == np.arange(QH)[None, :]).astype(f32)
    j = np.arange(NTOK)
    arr["selfmask"] = np.where((c % NTOK)[:, None] == j[None, :], np.where(j > 0, NEG, 0.0)[None, :], 0.0).astype(f32)
    arr["numbers"] = (np.arange(T + 1)[None, :] * P + np.arange(P)[:, None]).astype(f32)
    arr["slot1"] = np.tile((np.arange(NE) * SLOTS + 1.0).astype(f32)[None], (P, 1))
    arr["prefix"] = (np.arange(P)[:, None] < np.arange(P)[None, :]).astype(f32)
    arr["steps"] = np.tile((np.arange(1, T) * P).astype(f32)[None], (P, 1))
    arr["tri"] = np.tile((np.arange(E)[None, :] < np.arange(E)[:, None]).astype(f32).reshape(1, E * E), (P, 1))
    rowv = np.zeros((1, 2048), f32)
    pieces = [i["L0_tok_b"], i["L0_attn_b_qkv"], i["L0_attn_b_proj"], i["L0_ffn_b_proj"], i["L0_ffn_b_fc2"],
              i["L1_ffn_bg"], i["L1_ffn_be"].reshape(NE)]
    n = 0
    for p in pieces:
        rowv[0, n:n + p.size] = p
        n += p.size
    arr["rows"] = rowv
    colv = np.zeros((HC, 24), f32)
    colv[:, 0:4] = i["L0_attn_b_qkv"][:4 * HC].reshape(4, HC).T
    for at, name in ((4, "n1l"), (8, "n1s"), (12, "n2l"), (16, "n2s")):
        colv[:, at:at + 2] = i[f"L0_ffn_{name}_g"].reshape(2, HC).T
        colv[:, at + 2:at + 4] = i[f"L0_ffn_{name}_b"].reshape(2, HC).T
    colv[:, 20:22] = np.repeat(i["L0_attn_scale"], NTOK).reshape(2, HC).T
    arr["cols"] = colv

    nc = bacc.Bacc("TRN2", target_bir_lowering=False, num_devices=1)
    arrays = {f"in_{k}_dram": np.ascontiguousarray(v) for k, v in arr.items()}
    aps = {k: nc.dram_tensor(f"in_{k}_dram", arrays[f"in_{k}_dram"].shape, F32, kind="ExternalInput").ap() for k in arr}
    out = nc.dram_tensor("out_0_dram", (TOK, D), F32, kind="ExternalOutput").ap()
    vit_tower(nc, aps, out)
    r = run_bass_kernel_spmd(nc, [arrays], core_ids=[0])
    return r.results[0]["out_0_dram"].reshape(B, NTOK, D)
```
